# Optimizing a Trainium2 kernel written in Bass

```python
import numpy as np
import jax
import jax.numpy as jnp

def _softmax(x, axis=-1):
    return jax.nn.softmax(x, axis=axis)

def _gelu(x):
    return jax.nn.gelu(x, approximate=True)

def _silu(x):
    return jax.nn.silu(x)

def _sigmoid(x):
    return jax.nn.sigmoid(x)

def _layernorm(x, axis=-1, eps=1e-05):
    m = jnp.mean(x, axis=axis, keepdims=True)
    v = jnp.var(x, axis=axis, keepdims=True)
    return (x - m) / jnp.sqrt(v + eps)

def _scatter_add(tgt, idx, src, axis=0):
    return tgt.at[idx].add(src)

def _segment_sum(src, seg, n):
    return jax.ops.segment_sum(src, seg, n)
kernel_name = 'mk_early_fusion_d2_tok_img256_r4_a82d6e'

def setup_inputs(seed: int=0):
    np.random.seed(seed)
    _w = jnp.asarray

    def _rec_inputs():
        import jax
        import jax.numpy as jnp
        _rk = jax.random.key(seed)
        x = -0.000928989 + 1.00043 * jax.random.normal(jax.random.fold_in(_rk, 1), (32, 64, 64, 1), jnp.float32)
        txt = -0.0645857 + 1.41221 * jax.random.normal(jax.random.fold_in(_rk, 2), (32, 128, 64), jnp.float32)
        return (x, txt)
    x, txt = _rec_inputs()

    def _L0_tok_setup():
        import jax, jax.numpy as jnp
        import numpy as np
        L = 4
        M1 = 12
        M2 = 12
        BN_EPS = 1e-05

        def _fourier_layer(v, W1, W2):
            B, C, Sx, Sy = v.shape
            x_ft = jnp.fft.rfft2(v)
            out1 = jnp.einsum('bixy,ioxy->boxy', x_ft[:, :, :M1, :M2], W1)
            out2 = jnp.einsum('bixy,ioxy->boxy', x_ft[:, :, -M1:, :M2], W2)
            out_ft = jnp.zeros((B, C, Sx, Sy // 2 + 1), jnp.complex64)
            out_ft = out_ft.at[:, :, :M1, :M2].set(out1)
            out_ft = out_ft.at[:, :, Sx - M1:, :M2].set(out2)
            return jnp.fft.irfft2(out_ft, s=(Sx, Sy))
        key = jax.random.key(seed)
        ks = jax.random.split(key, 10)
        B, S, d_a, d_v, d_u = (16, 64, 3, 32, 1)
        return {'x': jax.random.normal(ks[0], (B, S, S, 1), jnp.float32), 'p_w': jax.random.normal(ks[1], (d_a, d_v), jnp.float32) * 0.3, 'p_b': jax.random.normal(ks[2], (d_v,), jnp.float32) * 0.1, 'fw1': jax.random.normal(ks[3], (L, d_v, d_v, M1, M2, 2), jnp.float32) * (1.0 / d_v), 'fw2': jax.random.normal(ks[4], (L, d_v, d_v, M1, M2, 2), jnp.float32) * (1.0 / d_v), 'w_w': jax.random.normal(ks[5], (L, d_v, d_v), jnp.float32) * (1.0 / np.sqrt(d_v)), 'w_b': jax.random.normal(ks[6], (L, d_v), jnp.float32) * 0.1, 'bn_g': jnp.ones((L, d_v), jnp.float32), 'bn_b': jnp.zeros((L, d_v), jnp.float32), 'q_w': jax.random.normal(ks[7], (d_v, d_u), jnp.float32) * 0.3, 'q_b': jax.random.normal(ks[8], (d_u,), jnp.float32) * 0.1}
    _L0_tok_all = _L0_tok_setup()
    _L0_tok_in = {k: v for k, v in _L0_tok_all.items() if k in ('p_w', 'p_b', 'fw1', 'fw2', 'w_w', 'w_b', 'bn_g', 'bn_b', 'q_w', 'q_b')}
    del _L0_tok_all

    def _L0_attn_setup():
        import jax, jax.numpy as jnp
        import numpy as np
        import math
        B, S, D = (4, 1024, 64)
        key = jax.random.key(seed)
        ks = jax.random.split(key, 9)
        s = 1.0 / math.sqrt(D)
        return {'src': jax.random.normal(ks[0], (B, S, D), dtype=jnp.float32), 'Wq': jax.random.normal(ks[1], (D, D), dtype=jnp.float32) * s, 'bq': jax.random.normal(ks[2], (D,), dtype=jnp.float32) * s, 'Wk': jax.random.normal(ks[3], (D, D), dtype=jnp.float32) * s, 'bk': jax.random.normal(ks[4], (D,), dtype=jnp.float32) * s, 'Wv': jax.random.normal(ks[5], (D, D), dtype=jnp.float32) * s, 'bv': jax.random.normal(ks[6], (D,), dtype=jnp.float32) * s, 'Wo': jax.random.normal(ks[7], (D, D), dtype=jnp.float32) * s, 'bo': jax.random.normal(ks[8], (D,), dtype=jnp.float32) * s}
    _L0_attn_all = _L0_attn_setup()
    _L0_attn_in = {k: v for k, v in _L0_attn_all.items() if k in ('Wq', 'bq', 'Wk', 'bk', 'Wv', 'bv', 'Wo', 'bo')}
    del _L0_attn_all

    def _L0_ffn_setup():
        import jax, jax.numpy as jnp
        import numpy as np
        DIM = 64
        H = 8
        D = 64
        G = 64
        INNER = H * D
        SCALE = D ** (-0.5)
        key = jax.random.key(seed)
        ks = jax.random.split(key, 12)
        B, N = (4, 4096)
        x = jax.random.normal(ks[0], (B, N, DIM), dtype=jnp.float32)
        s = lambda fan_in: 1.0 / np.sqrt(fan_in)
        W_fx = jax.random.normal(ks[1], (DIM, INNER), dtype=jnp.float32) * s(DIM)
        b_fx = jnp.zeros((INNER,), dtype=jnp.float32)
        W_x = jax.random.normal(ks[2], (DIM, INNER), dtype=jnp.float32) * s(DIM)
        b_x = jnp.zeros((INNER,), dtype=jnp.float32)
        A = jax.random.normal(ks[3], (G, D), dtype=jnp.float32)
        Q, _ = jnp.linalg.qr(A.T)
        W_slice = Q[:, :G].astype(jnp.float32)
        b_slice = jnp.zeros((G,), dtype=jnp.float32)
        W_q = jax.random.normal(ks[4], (D, D), dtype=jnp.float32) * s(D)
        W_k = jax.random.normal(ks[5], (D, D), dtype=jnp.float32) * s(D)
        W_v = jax.random.normal(ks[6], (D, D), dtype=jnp.float32) * s(D)
        W_out = jax.random.normal(ks[7], (INNER, DIM), dtype=jnp.float32) * s(INNER)
        b_out = jnp.zeros((DIM,), dtype=jnp.float32)
        temperature = jnp.ones((1, H, 1, 1), dtype=jnp.float32) * 0.5
        return {'x': x, 'W_fx': W_fx, 'b_fx': b_fx, 'W_x': W_x, 'b_x': b_x, 'W_slice': W_slice, 'b_slice': b_slice, 'W_q': W_q, 'W_k': W_k, 'W_v': W_v, 'W_out': W_out, 'b_out': b_out, 'temperature': temperature}
    _L0_ffn_all = _L0_ffn_setup()
    _L0_ffn_in = {k: v for k, v in _L0_ffn_all.items() if k in ('W_fx', 'b_fx', 'W_x', 'b_x', 'W_slice', 'b_slice', 'W_q', 'W_k', 'W_v', 'W_out', 'b_out', 'temperature')}
    del _L0_ffn_all

    def _L1_attn_setup():
        import jax, jax.numpy as jnp
        import numpy as np
        B, T, D = (4, 512, 64)
        W_LORA, A_LORA, G_LORA = (64, 64, 128)
        DECAY_SCALE = -0.6065306597126334
        EPS = D * 1e-05

        def _forward(x, x_mix, W_r, W_k, W_v, W_o, A_w, B_w, b_w, A_a, B_a, b_a, A_g, B_g, k_k, k_a, r_k, gn_w, gn_b):
            b, t, d = x.shape
            shifted = jnp.pad(x, ((0, 0), (1, 0), (0, 0)))[:, :-1]
            delta = shifted - x
            xr, xw, xk, xv, xa, xg = [x + delta * x_mix[i] for i in range(6)]
            r = xr @ W_r
            w = DECAY_SCALE * jax.nn.sigmoid(jnp.tanh(xw @ A_w) @ B_w + b_w)
            k = xk @ W_k
            v = xv @ W_v
            a = jax.nn.sigmoid(xa @ A_a @ B_a + b_a)
            g = jax.nn.sigmoid(xg @ A_g) @ B_g
            kk = k * k_k
            kk = kk / jnp.maximum(jnp.linalg.norm(kk, axis=-1, keepdims=True), 1e-12)
            k = k * (1.0 + (a - 1.0) * k_a)
            decay = jnp.exp(w)

            def step(S, inp):
                r_t, dec_t, k_t, v_t, kk_t, a_t = inp
                b_t = kk_t * a_t
                sa = jnp.einsum('bvk,bk->bv', S, -kk_t)
                S = S * dec_t[:, None, :] + sa[:, :, None] * b_t[:, None, :] + v_t[:, :, None] * k_t[:, None, :]
                o_t = jnp.einsum('bvk,bk->bv', S, r_t)
                return (S, o_t)
            tm = lambda z: jnp.swapaxes(z, 0, 1)
            S0 = jnp.zeros((b, d, d), x.dtype)
            _, o = jax.lax.scan(step, S0, (tm(r), tm(decay), tm(k), tm(v), tm(kk), tm(a)))
            o = jnp.swapaxes(o, 0, 1)
            mu = jnp.mean(o, axis=-1, keepdims=True)
            var = jnp.var(o, axis=-1, keepdims=True)
            o = (o - mu) * jax.lax.rsqrt(var + EPS) * gn_w + gn_b
            o = o + jnp.sum(r * k * r_k, axis=-1, keepdims=True) * v
            return o * g @ W_o
        key = jax.random.key(seed)
        ks = jax.random.split(key, 20)
        n = jax.random.normal
        p = {}
        p['x'] = n(ks[0], (B, T, D), jnp.float32)
        p['x_mix'] = n(ks[1], (6, D), jnp.float32) * 0.1
        s = 1.0 / np.sqrt(D).astype(np.float32)
        p['W_r'] = n(ks[2], (D, D), jnp.float32) * s
        p['W_k'] = n(ks[3], (D, D), jnp.float32) * s
        p['W_v'] = n(ks[4], (D, D), jnp.float32) * s
        p['W_o'] = n(ks[5], (D, D), jnp.float32) * s
        p['A_w'] = n(ks[6], (D, W_LORA), jnp.float32) * s
        p['B_w'] = n(ks[7], (W_LORA, D), jnp.float32) / np.sqrt(W_LORA).astype(np.float32)
        p['b_w'] = n(ks[8], (D,), jnp.float32) * 0.5
        p['A_a'] = n(ks[9], (D, A_LORA), jnp.float32) * s
        p['B_a'] = n(ks[10], (A_LORA, D), jnp.float32) / np.sqrt(A_LORA).astype(np.float32)
        p['b_a'] = n(ks[11], (D,), jnp.float32) * 0.1
        p['A_g'] = n(ks[12], (D, G_LORA), jnp.float32) * s
        p['B_g'] = n(ks[13], (G_LORA, D), jnp.float32) / np.sqrt(G_LORA).astype(np.float32)
        p['k_k'] = n(ks[14], (D,), jnp.float32) * 0.5 + 0.85
        p['k_a'] = n(ks[15], (D,), jnp.float32) * 0.1 + 1.0
        p['r_k'] = n(ks[16], (D,), jnp.float32) * 0.1
        p['gn_w'] = jnp.ones((D,), jnp.float32)
        p['gn_b'] = jnp.zeros((D,), jnp.float32)
        return p
    _L1_attn_all = _L1_attn_setup()
    _L1_attn_in = {k: v for k, v in _L1_attn_all.items() if k in ('x_mix', 'W_r', 'W_k', 'W_v', 'W_o', 'A_w', 'B_w', 'b_w', 'A_a', 'B_a', 'b_a', 'A_g', 'B_g', 'k_k', 'k_a', 'r_k', 'gn_w', 'gn_b')}
    del _L1_attn_all

    def _L1_ffn_setup():
        import jax, jax.numpy as jnp
        import numpy as np
        E = 8
        K = 2
        D = 64
        H = 128
        DOUT = 64
        EPS = 1e-05
        key = jax.random.key(seed)
        ks = jax.random.split(key, 9)
        s = 0.02
        return {'x': jax.random.normal(ks[0], (4, 2048, D), jnp.float32), 'gamma': 1.0 + 0.05 * jax.random.normal(ks[1], (D,), jnp.float32), 'beta': 0.05 * jax.random.normal(ks[2], (D,), jnp.float32), 'Wr': 0.01 * jax.random.normal(ks[3], (D, E), jnp.float32), 'br': jnp.zeros((E,), jnp.float32), 'W1': s * jax.random.normal(ks[4], (E, D, H), jnp.float32), 'b1': s * jax.random.normal(ks[5], (E, H), jnp.float32), 'W2': s * jax.random.normal(ks[6], (E, H, DOUT), jnp.float32), 'b2': s * jax.random.normal(ks[7], (E, DOUT), jnp.float32)}
    _L1_ffn_all = _L1_ffn_setup()
    _L1_ffn_in = {k: v for k, v in _L1_ffn_all.items() if k in ('gamma', 'beta', 'Wr', 'br', 'W1', 'b1', 'W2', 'b2')}
    del _L1_ffn_all
    return {'x': x, 'txt': txt, 'L0_tok_p_w': _L0_tok_in['p_w'], 'L0_tok_p_b': _L0_tok_in['p_b'], 'L0_tok_fw1': _L0_tok_in['fw1'], 'L0_tok_fw2': _L0_tok_in['fw2'], 'L0_tok_w_w': _L0_tok_in['w_w'], 'L0_tok_w_b': _L0_tok_in['w_b'], 'L0_tok_bn_g': _L0_tok_in['bn_g'], 'L0_tok_bn_b': _L0_tok_in['bn_b'], 'L0_tok_q_w': _L0_tok_in['q_w'], 'L0_tok_q_b': _L0_tok_in['q_b'], 'L0_attn_Wq': _L0_attn_in['Wq'], 'L0_attn_bq': _L0_attn_in['bq'], 'L0_attn_Wk': _L0_attn_in['Wk'], 'L0_attn_bk': _L0_attn_in['bk'], 'L0_attn_Wv': _L0_attn_in['Wv'], 'L0_attn_bv': _L0_attn_in['bv'], 'L0_attn_Wo': _L0_attn_in['Wo'], 'L0_attn_bo': _L0_attn_in['bo'], 'L0_ffn_W_fx': _L0_ffn_in['W_fx'], 'L0_ffn_b_fx': _L0_ffn_in['b_fx'], 'L0_ffn_W_x': _L0_ffn_in['W_x'], 'L0_ffn_b_x': _L0_ffn_in['b_x'], 'L0_ffn_W_slice': _L0_ffn_in['W_slice'], 'L0_ffn_b_slice': _L0_ffn_in['b_slice'], 'L0_ffn_W_q': _L0_ffn_in['W_q'], 'L0_ffn_W_k': _L0_ffn_in['W_k'], 'L0_ffn_W_v': _L0_ffn_in['W_v'], 'L0_ffn_W_out': _L0_ffn_in['W_out'], 'L0_ffn_b_out': _L0_ffn_in['b_out'], 'L0_ffn_temperature': _L0_ffn_in['temperature'], 'L1_attn_x_mix': _L1_attn_in['x_mix'], 'L1_attn_W_r': _L1_attn_in['W_r'], 'L1_attn_W_k': _L1_attn_in['W_k'], 'L1_attn_W_v': _L1_attn_in['W_v'], 'L1_attn_W_o': _L1_attn_in['W_o'], 'L1_attn_A_w': _L1_attn_in['A_w'], 'L1_attn_B_w': _L1_attn_in['B_w'], 'L1_attn_b_w': _L1_attn_in['b_w'], 'L1_attn_A_a': _L1_attn_in['A_a'], 'L1_attn_B_a': _L1_attn_in['B_a'], 'L1_attn_b_a': _L1_attn_in['b_a'], 'L1_attn_A_g': _L1_attn_in['A_g'], 'L1_attn_B_g': _L1_attn_in['B_g'], 'L1_attn_k_k': _L1_attn_in['k_k'], 'L1_attn_k_a': _L1_attn_in['k_a'], 'L1_attn_r_k': _L1_attn_in['r_k'], 'L1_attn_gn_w': _L1_attn_in['gn_w'], 'L1_attn_gn_b': _L1_attn_in['gn_b'], 'L1_ffn_gamma': _L1_ffn_in['gamma'], 'L1_ffn_beta': _L1_ffn_in['beta'], 'L1_ffn_Wr': _L1_ffn_in['Wr'], 'L1_ffn_br': _L1_ffn_in['br'], 'L1_ffn_W1': _L1_ffn_in['W1'], 'L1_ffn_b1': _L1_ffn_in['b1'], 'L1_ffn_W2': _L1_ffn_in['W2'], 'L1_ffn_b2': _L1_ffn_in['b2']}

def reference(x, txt, L0_tok_p_w, L0_tok_p_b, L0_tok_fw1, L0_tok_fw2, L0_tok_w_w, L0_tok_w_b, L0_tok_bn_g, L0_tok_bn_b, L0_tok_q_w, L0_tok_q_b, L0_attn_Wq, L0_attn_bq, L0_attn_Wk, L0_attn_bk, L0_attn_Wv, L0_attn_bv, L0_attn_Wo, L0_attn_bo, L0_ffn_W_fx, L0_ffn_b_fx, L0_ffn_W_x, L0_ffn_b_x, L0_ffn_W_slice, L0_ffn_b_slice, L0_ffn_W_q, L0_ffn_W_k, L0_ffn_W_v, L0_ffn_W_out, L0_ffn_b_out, L0_ffn_temperature, L1_attn_x_mix, L1_attn_W_r, L1_attn_W_k, L1_attn_W_v, L1_attn_W_o, L1_attn_A_w, L1_attn_B_w, L1_attn_b_w, L1_attn_A_a, L1_attn_B_a, L1_attn_b_a, L1_attn_A_g, L1_attn_B_g, L1_attn_k_k, L1_attn_k_a, L1_attn_r_k, L1_attn_gn_w, L1_attn_gn_b, L1_ffn_gamma, L1_ffn_beta, L1_ffn_Wr, L1_ffn_br, L1_ffn_W1, L1_ffn_b1, L1_ffn_W2, L1_ffn_b2):
    import jax
    import jax.numpy as jnp

    def _L0_tok_ref(x, p_w, p_b, fw1, fw2, w_w, w_b, bn_g, bn_b, q_w, q_b):
        import jax, jax.numpy as jnp
        import numpy as np
        L = 4
        M1 = 12
        M2 = 12
        BN_EPS = 1e-05

        def _fourier_layer(v, W1, W2):
            B, C, Sx, Sy = v.shape
            x_ft = jnp.fft.rfft2(v)
            out1 = jnp.einsum('bixy,ioxy->boxy', x_ft[:, :, :M1, :M2], W1)
            out2 = jnp.einsum('bixy,ioxy->boxy', x_ft[:, :, -M1:, :M2], W2)
            out_ft = jnp.zeros((B, C, Sx, Sy // 2 + 1), jnp.complex64)
            out_ft = out_ft.at[:, :, :M1, :M2].set(out1)
            out_ft = out_ft.at[:, :, Sx - M1:, :M2].set(out2)
            return jnp.fft.irfft2(out_ft, s=(Sx, Sy))
        B, Sx, Sy, _ = x.shape
        gx = jnp.broadcast_to(jnp.linspace(0.0, 1.0, Sx, dtype=jnp.float32)[None, :, None, None], (B, Sx, Sy, 1))
        gy = jnp.broadcast_to(jnp.linspace(0.0, 1.0, Sy, dtype=jnp.float32)[None, None, :, None], (B, Sx, Sy, 1))
        h = jnp.concatenate([x, gx, gy], axis=-1)
        v = h @ p_w + p_b
        v = jnp.transpose(v, (0, 3, 1, 2))
        for i in range(L):
            W1 = fw1[i, ..., 0] + 1j * fw1[i, ..., 1]
            W2 = fw2[i, ..., 0] + 1j * fw2[i, ..., 1]
            x1 = _fourier_layer(v, W1, W2)
            x2 = jnp.einsum('bcxy,cd->bdxy', v, w_w[i]) + w_b[i][None, :, None, None]
            v = x1 + x2
            mean = jnp.mean(v, axis=(0, 2, 3), keepdims=True)
            var = jnp.var(v, axis=(0, 2, 3), keepdims=True)
            v = (v - mean) * jax.lax.rsqrt(var + BN_EPS)
            v = v * bn_g[i][None, :, None, None] + bn_b[i][None, :, None, None]
            if i < L - 1:
                v = jax.nn.relu(v)
        out = jnp.einsum('bcxy,cu->bxyu', v, q_w) + q_b
        return jnp.squeeze(out)

    def _L0_attn_ref(src, Wq, bq, Wk, bk, Wv, bv, Wo, bo):
        import jax, jax.numpy as jnp
        import numpy as np
        import math
        B, S, D = (4, 1024, 64)
        q = src @ Wq.T + bq
        k = src @ Wk.T + bk
        v = src @ Wv.T + bv
        row_mask = (q[:, :, 0] != 0) & (k[:, :, 0] != 0)
        mask = row_mask[:, :, None]
        scale = 1.0 / math.sqrt(D)
        scores = jnp.einsum('bid,bjd->bij', q, k) * scale
        scores = jnp.where(mask, scores, jnp.float32(-1000000000.0))
        prob = jax.nn.softmax(scores, axis=-1)
        prob = jnp.where(mask, prob, 0.0)
        out = jnp.einsum('bij,bjd->bid', prob, v)
        return out @ Wo.T + bo

    def _L0_ffn_ref(x, W_fx, b_fx, W_x, b_x, W_slice, b_slice, W_q, W_k, W_v, W_out, b_out, temperature):
        import jax, jax.numpy as jnp
        import numpy as np
        DIM = 64
        H = 8
        D = 64
        G = 64
        INNER = H * D
        SCALE = D ** (-0.5)
        B, N, _ = x.shape
        fx_mid = (x @ W_fx + b_fx).reshape(B, N, H, D).transpose(0, 2, 1, 3)
        x_mid = (x @ W_x + b_x).reshape(B, N, H, D).transpose(0, 2, 1, 3)
        temp = jnp.clip(temperature, 0.1, 5.0)
        slice_weights = jax.nn.softmax((x_mid @ W_slice + b_slice) / temp, axis=-1)
        slice_norm = slice_weights.sum(axis=2)
        slice_token = jnp.einsum('bhnc,bhng->bhgc', fx_mid, slice_weights)
        slice_token = slice_token / (slice_norm[..., None] + 1e-05)
        q = slice_token @ W_q
        k = slice_token @ W_k
        v = slice_token @ W_v
        attn = jax.nn.softmax(jnp.einsum('bhgc,bhkc->bhgk', q, k) * SCALE, axis=-1)
        out_slice = jnp.einsum('bhgk,bhkc->bhgc', attn, v)
        out_x = jnp.einsum('bhgc,bhng->bhnc', out_slice, slice_weights)
        out_x = out_x.transpose(0, 2, 1, 3).reshape(B, N, INNER)
        return out_x @ W_out + b_out

    def _L1_attn_ref(x, x_mix, W_r, W_k, W_v, W_o, A_w, B_w, b_w, A_a, B_a, b_a, A_g, B_g, k_k, k_a, r_k, gn_w, gn_b):
        import jax, jax.numpy as jnp
        import numpy as np
        B, T, D = (4, 512, 64)
        W_LORA, A_LORA, G_LORA = (64, 64, 128)
        DECAY_SCALE = -0.6065306597126334
        EPS = D * 1e-05

        def _forward(x, x_mix, W_r, W_k, W_v, W_o, A_w, B_w, b_w, A_a, B_a, b_a, A_g, B_g, k_k, k_a, r_k, gn_w, gn_b):
            b, t, d = x.shape
            shifted = jnp.pad(x, ((0, 0), (1, 0), (0, 0)))[:, :-1]
            delta = shifted - x
            xr, xw, xk, xv, xa, xg = [x + delta * x_mix[i] for i in range(6)]
            r = xr @ W_r
            w = DECAY_SCALE * jax.nn.sigmoid(jnp.tanh(xw @ A_w) @ B_w + b_w)
            k = xk @ W_k
            v = xv @ W_v
            a = jax.nn.sigmoid(xa @ A_a @ B_a + b_a)
            g = jax.nn.sigmoid(xg @ A_g) @ B_g
            kk = k * k_k
            kk = kk / jnp.maximum(jnp.linalg.norm(kk, axis=-1, keepdims=True), 1e-12)
            k = k * (1.0 + (a - 1.0) * k_a)
            decay = jnp.exp(w)

            def step(S, inp):
                r_t, dec_t, k_t, v_t, kk_t, a_t = inp
                b_t = kk_t * a_t
                sa = jnp.einsum('bvk,bk->bv', S, -kk_t)
                S = S * dec_t[:, None, :] + sa[:, :, None] * b_t[:, None, :] + v_t[:, :, None] * k_t[:, None, :]
                o_t = jnp.einsum('bvk,bk->bv', S, r_t)
                return (S, o_t)
            tm = lambda z: jnp.swapaxes(z, 0, 1)
            S0 = jnp.zeros((b, d, d), x.dtype)
            _, o = jax.lax.scan(step, S0, (tm(r), tm(decay), tm(k), tm(v), tm(kk), tm(a)))
            o = jnp.swapaxes(o, 0, 1)
            mu = jnp.mean(o, axis=-1, keepdims=True)
            var = jnp.var(o, axis=-1, keepdims=True)
            o = (o - mu) * jax.lax.rsqrt(var + EPS) * gn_w + gn_b
            o = o + jnp.sum(r * k * r_k, axis=-1, keepdims=True) * v
            return o * g @ W_o
        return _forward(x, x_mix, W_r, W_k, W_v, W_o, A_w, B_w, b_w, A_a, B_a, b_a, A_g, B_g, k_k, k_a, r_k, gn_w, gn_b)

    def _L1_ffn_ref(x, gamma, beta, Wr, br, W1, b1, W2, b2):
        import jax, jax.numpy as jnp
        import numpy as np
        E = 8
        K = 2
        D = 64
        H = 128
        DOUT = 64
        EPS = 1e-05
        mu = jnp.mean(x, axis=-1, keepdims=True)
        var = jnp.mean(jnp.square(x - mu), axis=-1, keepdims=True)
        xn = (x - mu) * jax.lax.rsqrt(var + EPS) * gamma + beta
        logits = jnp.einsum('bsd,de->bse', xn, Wr) + br
        top_vals, top_idx = jax.lax.top_k(logits, K)
        w = jax.nn.softmax(top_vals, axis=-1)
        w_full = jnp.einsum('bsk,bske->bse', w, jax.nn.one_hot(top_idx, E, dtype=w.dtype))
        y = jnp.zeros(x.shape[:-1] + (DOUT,), x.dtype)
        for e in range(E):
            h = jax.nn.gelu(jnp.einsum('bsd,dh->bsh', xn, W1[e]) + b1[e], approximate=False)
            y_e = jnp.einsum('bsh,hd->bsd', h, W2[e]) + b2[e]
            y = y + y_e * w_full[..., e, None]
        return y
    h = _L0_tok_ref(x, L0_tok_p_w, L0_tok_p_b, L0_tok_fw1, L0_tok_fw2, L0_tok_w_w, L0_tok_w_b, L0_tok_bn_g, L0_tok_bn_b, L0_tok_q_w, L0_tok_q_b)
    h = jnp.concatenate([h, txt], axis=1)
    h = h + _L0_attn_ref(_layernorm(h, axis=-1), L0_attn_Wq, L0_attn_bq, L0_attn_Wk, L0_attn_bk, L0_attn_Wv, L0_attn_bv, L0_attn_Wo, L0_attn_bo)
    h = h + _L0_ffn_ref(_layernorm(h, axis=-1), L0_ffn_W_fx, L0_ffn_b_fx, L0_ffn_W_x, L0_ffn_b_x, L0_ffn_W_slice, L0_ffn_b_slice, L0_ffn_W_q, L0_ffn_W_k, L0_ffn_W_v, L0_ffn_W_out, L0_ffn_b_out, L0_ffn_temperature)
    h = h + _L1_attn_ref(_layernorm(h, axis=-1), L1_attn_x_mix, L1_attn_W_r, L1_attn_W_k, L1_attn_W_v, L1_attn_W_o, L1_attn_A_w, L1_attn_B_w, L1_attn_b_w, L1_attn_A_a, L1_attn_B_a, L1_attn_b_a, L1_attn_A_g, L1_attn_B_g, L1_attn_k_k, L1_attn_k_a, L1_attn_r_k, L1_attn_gn_w, L1_attn_gn_b)
    h = h + _L1_ffn_ref(_layernorm(h, axis=-1), L1_ffn_gamma, L1_ffn_beta, L1_ffn_Wr, L1_ffn_br, L1_ffn_W1, L1_ffn_b1, L1_ffn_W2, L1_ffn_b2)
    return h

_drawn_inputs = setup_inputs


def setup_inputs(seed=0):
    import zlib

    import numpy as np

    out = dict(_drawn_inputs(seed))
    spreads = {'L0_tok_bn_g': (1.0, 0.2),
     'L0_tok_bn_b': (0.0, 0.1),
     'L0_ffn_b_fx': (0.0, 0.1),
     'L0_ffn_b_x': (0.0, 0.8),
     'L0_ffn_b_slice': (0.0, 0.8),
     'L0_ffn_b_out': (0.0, 0.1),
     'L0_ffn_temperature': (0.5, 0.6),
     'L1_attn_gn_w': (1.0, 0.2),
     'L1_attn_gn_b': (0.0, 0.331),
     'L1_ffn_br': (0.0, 0.735)}
    factors = {'L0_tok_p_b': 64.0,
     'L0_tok_w_b': 64.0,
     'L0_attn_bk': 64.0,
     'L0_ffn_W_x': 3.483,
     'L0_ffn_W_slice': 4.094,
     'L0_ffn_W_q': 8.0,
     'L0_ffn_W_k': 8.0,
     'L1_attn_b_a': 3.686,
     'L1_ffn_gamma': 8.0,
     'L1_ffn_beta': 8.0,
     'L1_ffn_Wr': 6.272,
     'L1_ffn_W1': 7.116,
     'L1_ffn_b1': 25.414,
     'L1_ffn_W2': 6.95,
     'L1_ffn_b2': 29.798}
    for name, (base, spread) in spreads.items():
        noise = np.random.default_rng([zlib.crc32(name.encode()), seed]).standard_normal(out[name].shape)
        drawn = base * np.exp(spread * noise) if base else spread * noise
        out[name] = jnp.asarray(drawn.astype(out[name].dtype))
    for name, factor in factors.items():
        out[name] = (out[name] * factor).astype(out[name].dtype)
    return out
```

```python
from contextlib import ExitStack

import concourse.bass as bass
import numpy as np
from concourse import mybir

F32 = mybir.dt.float32
ALU = mybir.AluOpType
ACT = mybir.ActivationFunctionType
AX = mybir.AxisListType

P = 128
S = 64
XY = S * S
C = 32
L = 4
KY = 12
KX = 24
B = 32
QB = 4
NQ = B // QB
NSUB = XY // 512
BN_EPS = 1e-5


def fourier_constants():
    n = np.arange(S)
    ky = np.arange(KY)
    kx = np.concatenate([np.arange(KX // 2), np.arange(S - KX // 2, S)])
    ay = 2 * np.pi * np.outer(n, ky) / S
    ax = 2 * np.pi * np.outer(n, kx) / S
    fy = np.zeros((2, S, KY, 2, 2))
    for a in range(2):
        fy[a, :, :, a, 0] = np.cos(ay)
        fy[a, :, :, a, 1] = -np.sin(ay)
    fx = np.zeros((S, 2, 2, KX, 2))
    re = np.stack([np.cos(ax), np.sin(ax)], 1)
    im = np.stack([-np.sin(ax), np.cos(ax)], 1)
    fx[:, :, 0, :, 0] = re
    fx[:, :, 0, :, 1] = im
    fx[:, :, 1, :, 0] = -im
    fx[:, :, 1, :, 1] = re
    ix = np.zeros((2, KX, 2, 2, S, 2))
    for a in range(2):
        ix[a, :, 0, a, :, 0] = np.cos(ax).T
        ix[a, :, 1, a, :, 0] = -np.sin(ax).T
        ix[a, :, 0, a, :, 1] = np.sin(ax).T
        ix[a, :, 1, a, :, 1] = np.cos(ax).T
    wgt = np.where(ky == 0, 1.0, 2.0)[:, None] / XY
    iy = np.zeros((4, KY, 2, 4, S))
    for a in range(4):
        iy[a, :, 0, a] = wgt * np.cos(ay).T
        iy[a, :, 1, a] = -wgt * np.sin(ay).T
    f = np.float32
    return {
        "fy": fy.reshape(2 * S, KY * 4).astype(f),
        "fx": fx.reshape(2 * S, 4 * KX).astype(f),
        "ix": ix.reshape(4 * KX, 4 * S).astype(f),
        "iy": iy.reshape(8 * KY, 4 * S).astype(f),
    }


def fourier_operator(nc, barrier, ps, x, y_img, d, step0):
    ctx = ExitStack()
    sb = lambda n, s: ctx.enter_context(nc.sbuf_tensor("fno_" + n, s, F32))
    own = []

    def sem(n):
        own.append(ctx.enter_context(nc.semaphore(n)))
        return own[-1]


    V = sb("V", [P, NQ, XY])
    XS = sb("XS", [P, KY, KX // 2, 2, B])
    W = sb("W", [P, KY, KX // 2, C])
    stage = sb("stage", [P, 4608])
    fy = sb("fy", [P, 4 * KY])
    fx = sb("fx", [P, 4 * KX])
    ix = sb("ix", [4 * KX, 4 * S])
    iy = sb("iy", [8 * KY, 4 * S])
    ident = sb("ident", [P, P])
    avg4 = sb("avg4", [P, P])
    lift = sb("lift", [7, P])
    conv = sb("conv", [P, P])
    pv = sb("pv", [P, 3, L])
    stats = sb("stats", [P, NQ * NSUB, 6])
    agg = sb("agg", [P, 16])
    qcol = sb("qcol", [P, QB])
    qone = sb("qone", [P, QB])
    qb = sb("qb", [QB, 2])

    VB = [stage[:, 512 * k:512 * (k + 1)].rearrange("p (t n) -> p t n", n=P) for k in range(2)]
    Y1 = stage[:, 1024:1024 + 1536].rearrange("p (k n) -> p k n", n=P)
    T1 = stage[:, 2560:2560 + 1536].rearrange("p (k n) -> p k n", n=P)
    O = stage[:].rearrange("p (q k m) -> p q k m", q=NQ, k=KY)
    xs_flat = XS[:].rearrange("p k x s b -> p (k x s b)")
    T2 = [xs_flat[0:4 * KX, 768 * k:768 * (k + 1)].rearrange("p (k n) -> p k n", n=P) for k in range(2)]
    G = xs_flat[:, 3072:3072 + 1536].rearrange("p (x m) -> p x m", m=2 * KY)
    G2 = [xs_flat[0:8 * KY, 4608 + 2048 * k:4608 + 2048 * (k + 1)].rearrange("p (j n) -> p j n", n=P)
          for k in range(2)]
    XR = W[0:7].rearrange("p k x c -> p (k x c)")[:, 0:XY]

    s_const = sem("fno_const"); s_zero = sem("fno_zero"); s_lay = sem("fno_layer_weights")
    s_w = sem("fno_mode_weights"); s_x = sem("fno_images"); s_yout = sem("fno_out")
    s_lift = sem("fno_lifted"); s_liftv = sem("fno_lift_copied")
    s_v = sem("fno_v_ready")
    s_tr = [sem(f"fno_v_turned{k}") for k in range(2)]
    s_vb = [sem(f"fno_vb_ready{k}") for k in range(2)]
    s_f1 = sem("fno_f1"); s_y1 = sem("fno_y1_ready")
    s_t1p = sem("fno_y1_turned"); s_t1 = sem("fno_t1_ready")
    s_f2 = sem("fno_f2"); s_xa = sem("fno_xs_by_act"); s_xd = sem("fno_xs_by_dve")
    s_mix = sem("fno_mixed"); s_oa = sem("fno_o_by_act"); s_od = sem("fno_o_by_dve")
    s_t2p = sem("fno_o_turned"); s_t2 = sem("fno_t2_ready")
    s_gp = sem("fno_gp"); s_g = sem("fno_g_ready")
    s_g2p = sem("fno_g_turned"); s_g2 = sem("fno_g2_ready")
    s_sum = sem("fno_summed"); s_vw = sem("fno_v_written"); s_st = sem("fno_stats")
    s_bn = sem("fno_bn_dve"); s_bnp = sem("fno_bn_pe"); s_bna = sem("fno_bn_act"); s_scale = sem("fno_scale")
    s_q = sem("fno_q"); s_qv = sem("fno_q_copied"); s_qc = sem("fno_q_col")

    scale, shift = agg[:, 8:9], agg[:, 9:10]

    def sync_program(sp):
        n = 0
        for dst, src in ((fy, d["fy"]), (fx, d["fx"]), (ix, d["ix"]), (iy, d["iy"]), (ident, d["ident"]), (avg4, d["avg4"])):
            sp.dma_start(dst[:], src).then_inc(s_const, 16); n += 1
        sp.dma_start(XR[4:7], d["grid"]).then_inc(s_const, 16); n += 1
        sp.wait_ge(s_zero, 3)
        for b in range(QB):
            c = slice(C * b, C * (b + 1))
            sp.dma_start(lift[b:b + 1, c], d["p_w"][0:1, :]).then_inc(s_const, 16)
            sp.dma_start(lift[4:6, c], d["p_w"][1:3, :]).then_inc(s_const, 16)
            sp.dma_start(lift[6:7, c], d["p_b"].rearrange("(a c) -> a c", a=1)).then_inc(s_const, 16)
            for k, name in enumerate(("w_b", "bn_g", "bn_b")):
                sp.dma_start(pv[c, k, :], d[name]).then_inc(s_const, 16)
            sp.dma_start(qone[c, b:b + 1], d["q_w"]).then_inc(s_const, 16)
            n += 7
        sp.dma_start(qb[0:QB, 0:1], d["q_b4"]).then_inc(s_const, 16); n += 1
        assert n == NDMA, n
        for q in range(NQ):
            if q:
                sp.wait_ge(s_lift, NSUB * q)
            sp.dma_start(XR[0:QB], x[QB * q:QB * (q + 1), :]).then_inc(s_x, 16)
        sp.wait_ge(s_lift, NSUB * NQ)

        def layer_weights(l):
            sp.dma_start(W[:].rearrange("p k x c -> p (k x c)"), d["modes"][bass.ds(l, 1)].rearrange("l p n -> (l p) n")).then_inc(s_w, 16)
        def conv_weights(l):
            for b in range(QB):
                sp.dma_start(conv[C * b:C * (b + 1), C * b:C * (b + 1)],
                             d["w_w"][bass.ds(l, 1)].rearrange("l c e -> (l c) e")).then_inc(s_lay, 16)
        layer_weights(0)
        conv_weights(0)
        barrier(sp, step0 + 1)
        for l in range(L - 1):
            barrier(sp, step0 + 2 + 3 * l)
            layer_weights(l + 1)
            barrier(sp, step0 + 3 + 3 * l)
            conv_weights(l + 1)
            barrier(sp, step0 + 4 + 3 * l)
        barrier(sp, step0 + 2 + 3 * (L - 1))
        barrier(sp, step0 + 3 + 3 * (L - 1))
        sp.wait_ge(s_qv, NQ * NSUB)
        sp.dma_start(y_img.rearrange("(q b) n -> b q n", b=QB), V[0:QB]).then_inc(s_yout, 16)
        sp.wait_ge(s_yout, 16)

    NDMA = 6 + 1 + 7 * QB + 1

    def pe_forward(pe, f, lifted):
        def turn(t):
            q, s = divmod(t, NSUB)
            k = t % 2
            if lifted:
                pe.wait_ge(s_liftv, t + 1)
            else:
                pe.wait_ge(s_v, (f - 1) * NQ * NSUB + t + 1)
            pe.wait_ge(s_vb[k], f * 32 + t // 2)
            for j in range(4):
                mm = pe.transpose(ps[:, k, P * j:P * (j + 1)], V[:, q, 512 * s + P * j:512 * s + P * (j + 1)], ident[:])
            mm.then_inc(s_tr[k], 1)

        def along_y(t):
            q, s = divmod(t, NSUB)
            k = t % 2
            pe.wait_ge(s_vb[k], f * 32 + t // 2 + 1)
            if k == 0:
                pe.wait_ge(s_y1, f * 32 + t // 2)
            for j in range(4):
                c = 48 * (4 * k + j)
                mm = pe.matmul(ps[:, 2, c:c + 48], VB[k][:, j, :], fy[:], start=True, stop=True)
            mm.then_inc(s_f1, 1)

        def turn_y1(q):
            pe.wait_ge(s_y1, f * 32 + 4 * q + 4)
            for g in range(3):
                n = (f * NQ + q) * 3 + g
                if g < 2:
                    pe.wait_ge(s_t1, (f * NQ + q) * 3 + (g - 1 if g else 0))
                else:
                    pe.wait_ge(s_t1, n - 1)
                for j in range(4):
                    mm = pe.transpose(ps[:, 3 + g % 2, P * j:P * (j + 1)], Y1[:, 4 * g + j, :], ident[:])
                mm.then_inc(s_t1p, 1)

        def along_x(q):
            pe.wait_ge(s_t1, (f * NQ + q + 1) * 3)
            pe.wait_ge(s_xa, (f * NQ + q) * 8)
            pe.wait_ge(s_xd, (f * NQ + q) * 8)
            for j in range(KY):
                mm = pe.matmul(ps[:, 5 + j // 4, 96 * (j % 4):96 * (j % 4) + 96], T1[:, j, :], fx[:], start=True, stop=True)
            mm.then_inc(s_f2, 1)

        for t in range(NQ * NSUB + 3):
            if t < NQ * NSUB:
                turn(t)
            if 1 <= t <= NQ * NSUB:
                along_y(t - 1)
            if t % NSUB == 1 and t > NSUB:
                turn_y1(t // NSUB - 1)
            if t % NSUB == 2 and t > NSUB:
                along_x(t // NSUB - 1)

    def y1_view(q_sub):
        return Y1.rearrange("p k (t m) -> p t k m", m=4)[:, 8 * q_sub:8 * (q_sub + 1)]

    def xs_parts():
        return [(b, h, c) for b in range(QB) for h in range(2) for c in range(2)]

    def xs_copy(op, q, b, h, c):
        src = ps[C * b:C * (b + 1), 5:8, 0:384].rearrange("p g (k m) -> p g k m", k=4)[:, :, :, 48 * c + 24 * h:48 * c + 24 * h + 24]
        r = 64 * h + 32 * c
        dst = XS[r:r + 32].rearrange("p (g k) x s b -> p g k (x s) b", g=3)[:, :, :, :, QB * q + b]
        return op(dst, src)

    def act_copy(dst, src):
        return nc.scalar.activation(dst, src, ACT.Copy)

    def act_forward(act, f, lifted):
        def ready(t):
            q, s = divmod(t, NSUB)
            v = V[:, q, 512 * s:512 * (s + 1)]
            if lifted:
                act.wait_ge(s_lift, t + 1)
                nc.scalar.copy(v, ps[:, 6 + t % 2, :]).then_inc(s_liftv, 1)
            else:
                if t == 0:
                    act.wait_ge(s_scale, f)
                act.activation(v, v, ACT.Relu, bias=shift, scale=scale).then_inc(s_v, 1)
        def y1(u):
            act.wait_ge(s_f1, f * 64 + 2 * u + 2)
            if u % 4 == 0:
                act.wait_ge(s_t1p, (f * NQ + u // 4) * 3)
            src = ps[:, 2, 0:384].rearrange("p (t k m) -> p t k m", t=8, k=KY)
            nc.scalar.activation(y1_view(u % 4), src, ACT.Copy).then_inc(s_y1, 1)
        def xs(q):
            act.wait_ge(s_f2, f * NQ + q + 1)
            for b, h, c in xs_parts()[:8]:
                xs_copy(act_copy, q, b, h, c).then_inc(s_xa, 1)
        N = NQ * NSUB
        for t in range(N + 4):
            if t < N and not lifted:
                ready(t)
            if t >= 3 and t % 2 == 1 and (t - 3) // 2 < N // 2:
                y1((t - 3) // 2)
            if t % NSUB == 3 and t > NSUB:
                xs(t // NSUB - 1)

    def dve_forward(dve, f):
        def vb(t):
            k = t % 2
            dve.wait_ge(s_tr[k], f * 32 + t // 2 + 1)
            if t >= 2:
                dve.wait_ge(s_f1, f * 64 + t - 1)
            nc.vector.tensor_copy(VB[k].rearrange("p t n -> p (t n)"), ps[:, k, :]).then_inc(s_vb[k], 1)
        def t1(q):
            for g in range(3):
                dve.wait_ge(s_t1p, (f * NQ + q) * 3 + g + 1)
                if g == 0:
                    dve.wait_ge(s_f2, f * NQ + q)
                nc.vector.tensor_copy(T1[:, 4 * g:4 * g + 4, :].rearrange("p k n -> p (k n)"), ps[:, 3 + g % 2, :]).then_inc(s_t1, 1)
        def xs(q):
            dve.wait_ge(s_f2, f * NQ + q + 1)
            for b, h, c in xs_parts()[8:]:
                xs_copy(nc.vector.tensor_copy, q, b, h, c).then_inc(s_xd, 1)
        N = NQ * NSUB
        for t in range(N + 3):
            if t < N:
                vb(t)
            if t % NSUB == 1 and t > NSUB:
                t1(t // NSUB - 1)
            if t % NSUB == 2 and t > NSUB:
                xs(t // NSUB - 1)

    def pe_mix(pe, m):
        for k in range(2, KY, 2):
            pe.wait_ge(s_const, m * 24 + 4 * (k // 2))
        pe.wait_ge(s_w, 16 * m + 16)
        pe.transpose(ps[:, 0, 0:P], ident[:], ident[:])
        for k in range(KY):
            if k >= 2:
                pe.wait_ge(s_w, 16)
                pe.wait_ge(s_od if k % 2 else s_oa, m * 24 + 4 * (k // 2))
            for j in range(KX // 2):
                for h in range(2):
                    mm = pe.matmul(ps[0:C, 4 * (k % 2) + 2 * h + j // 6, 64 * (j % 6):64 * (j % 6) + 64],
                                   W[64 * h:64 * h + 64, k, j, :],
                                   XS[64 * h:64 * h + 64, k, j].rearrange("p s b -> p (s b)"), start=True, stop=True)
            mm.then_inc(s_mix, 1)

    def o_copy(op, k, b):
        src = ps[0:C, 4 * (k % 2):4 * (k % 2) + 4, 0:384].rearrange("p g (m q b) -> p g m q b", q=NQ, b=QB)[:, :, :, :, b]
        dst = O[C * b:C * (b + 1), :, k, :].rearrange("p q (g m) -> p g m q", g=4)
        return op(dst, src)

    def act_mix(act, m):
        for k in range(0, KY, 2):
            act.wait_ge(s_mix, m * KY + k + 1)
            for b in range(QB):
                o_copy(act_copy, k, b).then_inc(s_oa, 1)

    def dve_mix(dve, m):
        for k in range(1, KY, 2):
            dve.wait_ge(s_mix, m * KY + k + 1)
            for b in range(QB):
                o_copy(nc.vector.tensor_copy, k, b).then_inc(s_od, 1)

    def pe_inverse(pe, m):
        def turn_o(q):
            if q:
                pe.wait_ge(s_g2, (m * NQ + q) * 4)
            for g in range(2):
                for j in range(3):
                    k = 6 * g + 2 * j
                    mm = pe.transpose(ps[0:4 * KX, g, P * j:P * (j + 1)], O[:, q, k:k + 2, :].rearrange("p k m -> p (k m)"), ident[:])
                mm.then_inc(s_t2p, 1)
        def along_x(q):
            for g in range(3):
                pe.wait_ge(s_t2, (m * NQ + q) * 2 + (2 if g else 1))
                if q or g == 2:
                    pe.wait_ge(s_g, (m * NQ + q) * 3 + (1 if g == 2 else 0))
                for j in range(2):
                    mm = pe.matmul(ps[:, 2 + g % 2, 256 * j:256 * (j + 1)], T2[q % 2][:, 2 * g + j, :], ix[:], start=True, stop=True)
                mm.then_inc(s_gp, 1)
        def turn_g(q):
            pe.wait_ge(s_g, (m * NQ + q) * 3 + 3)
            for g in range(4):
                if g < 2:
                    pe.wait_ge(s_t2, (m * NQ + q) * 2 + 2)
                else:
                    pe.wait_ge(s_g2, (m * NQ + q) * 4 + g - 1)
                for j in range(4):
                    mm = pe.transpose(ps[0:8 * KY, g % 2, P * j:P * (j + 1)],
                                      G[:, 16 * g + 4 * j:16 * g + 4 * j + 4, :].rearrange("p x m -> p (x m)"), ident[:])
                mm.then_inc(s_g2p, 1)
        def sums(q, s):
            t = q * NSUB + s
            if s == 0:
                pe.wait_ge(s_g2, (m * NQ + q) * 4 + 4)
            if t >= 4:
                pe.wait_ge(s_vw, m * 64 + t - 3)
            bank = ps[:, 4 + t % 4, :]
            pe.matmul(bank, conv[:], V[:, q, 512 * s:512 * (s + 1)], start=True, stop=False, skip_group_check=True)
            for j in range(2):
                mm = pe.matmul(bank[:, 256 * j:256 * (j + 1)], G2[q % 2][:, 2 * s + j, :], iy[:], start=False, stop=True, skip_group_check=True)
            mm.then_inc(s_sum, 1)
        pe.wait_ge(s_lay, 16 * QB * (m + 1))
        turn_o(0); along_x(0); turn_g(0)
        for q in range(NQ):
            for s in range(NSUB):
                sums(q, s)
                if q + 1 < NQ:
                    if s == 0: turn_o(q + 1)
                    if s == 2: along_x(q + 1)
                    if s == 4: turn_g(q + 1)
        pe.wait_ge(s_bn, 5 * m + 1)
        pe.matmul(ps[:, 0, 0:1], avg4[:], agg[:, 0:1], start=True, stop=True).then_inc(s_bnp, 1)
        pe.wait_ge(s_bn, 5 * m + 3)
        pe.matmul(ps[:, 1, 0:1], avg4[:], agg[:, 3:4], start=True, stop=True).then_inc(s_bnp, 1)

    def dve_inverse(dve, m):
        def t2(q):
            for g in range(2):
                dve.wait_ge(s_t2p, (m * NQ + q) * 2 + g + 1)
                if g == 0 and q >= 2:
                    dve.wait_ge(s_gp, (m * NQ + q - 1) * 3)
                nc.vector.tensor_copy(T2[q % 2][:, 3 * g:3 * g + 3, :].rearrange("p k n -> p (k n)"), ps[0:4 * KX, g, 0:384]).then_inc(s_t2, 1)
        def g2(q):
            for g in range(4):
                dve.wait_ge(s_g2p, (m * NQ + q) * 4 + g + 1)
                if g == 0 and q >= 2:
                    dve.wait_ge(s_sum, m * 64 + NSUB * (q - 1))
                nc.vector.tensor_copy(G2[q % 2][:, 4 * g:4 * g + 4, :].rearrange("p k n -> p (k n)"), ps[0:8 * KY, g % 2, :]).then_inc(s_g2, 1)
        def st(q, s):
            t = q * NSUB + s
            dve.wait_ge(s_sum, m * 64 + t + 1)
            nc.vector.bn_stats(stats[:, t, :], ps[:, 4 + t % 4, :]).then_inc(s_st, 1)
        t2(0); g2(0)
        for q in range(NQ):
            for s in range(NSUB):
                st(q, s)
                if q + 1 < NQ:
                    if s == 0: t2(q + 1)
                    if s == 4: g2(q + 1)
        dve.wait_ge(s_st, 64)
        dve.wait_ge(s_st, m * 64 + 64)
        mean, var, dev, sq = agg[:, 0:1], agg[:, 1:2], agg[:, 2:3], agg[:, 3:4]
        nc.vector.bn_aggr(agg[:, 0:2], stats[:].rearrange("p n s -> p (n s)")).then_inc(s_bn, 1)
        dve.wait_ge(s_bnp, 2 * m + 1)
        nc.vector.tensor_tensor(dev, mean, ps[:, 0, 0:1], ALU.subtract).then_inc(s_bn, 1)
        dve.wait_ge(s_bn, 5 * m + 2)
        nc.vector.scalar_tensor_tensor(sq, dev, dev, var, ALU.mult, ALU.add).then_inc(s_bn, 1)
        dve.wait_ge(s_bnp, 2 * m + 2)
        nc.vector.tensor_scalar(agg[:, 4:5], ps[:, 1, 0:1], BN_EPS, None, ALU.add).then_inc(s_bn, 1)
        dve.wait_ge(s_bna, m + 1)
        nc.vector.reciprocal(agg[:, 6:7], agg[:, 5:6]).then_inc(s_bn, 1)
        dve.wait_ge(s_bn, 5 * m + 5)
        w_b, bn_g, bn_b = (pv[:, k, bass.ds(m, 1)] for k in range(3))
        nc.vector.tensor_tensor(scale, agg[:, 6:7], bn_g, ALU.mult).then_inc(s_scl, 1)
        nc.vector.tensor_tensor(agg[:, 7:8], ps[:, 0, 0:1], w_b, ALU.add).then_inc(s_scl, 1)
        dve.wait_ge(s_scl, 3 * m + 2)
        nc.vector.tensor_tensor(agg[:, 10:11], agg[:, 7:8], scale, ALU.mult).then_inc(s_scl, 1)
        dve.wait_ge(s_scl, 3 * m + 3)
        nc.vector.tensor_tensor(shift, bn_b, agg[:, 10:11], ALU.subtract).then_inc(s_scale, 1)

    s_scl = sem("fno_scl")

    def act_inverse(act, m):
        def g(q):
            for g in range(3):
                act.wait_ge(s_gp, (m * NQ + q) * 3 + g + 1)
                if g == 0 and q:
                    act.wait_ge(s_g2p, (m * NQ + q) * 4)
                src = ps[:, 2 + g % 2, :].rearrange("p (k x r) -> p k x r", k=4, r=2)
                dst = G.rearrange("p x (k r) -> p k x r", r=2)[:, 4 * g:4 * g + 4]
                nc.scalar.activation(dst, src, ACT.Copy).then_inc(s_g, 1)
        def vw(q, s):
            t = q * NSUB + s
            act.wait_ge(s_st, m * 64 + t + 1)
            act.activation(V[:, q, 512 * s:512 * (s + 1)], ps[:, 4 + t % 4, :], ACT.Identity, bias=wb_col[:]).then_inc(s_vw, 1)
        act.wait_ge(s_const, 16 * NDMA)
        nc.scalar.copy(wb_col[:], pv[:, 0, bass.ds(m, 1)]).then_inc(s_wb, 1)
        g(0)
        act.wait_ge(s_wb, m + 1)
        for q in range(NQ):
            for s in range(NSUB):
                vw(q, s)
                if q + 1 < NQ and s == 2:
                    g(q + 1)
        act.wait_ge(s_bn, 5 * m + 4)
        nc.scalar.activation(agg[:, 5:6], agg[:, 4:5], ACT.Sqrt).then_inc(s_bna, 1)

    wb_col = sb("wb_col", [P, 1])
    s_wb = sem("fno_wb")

    def tensor_program(pe):
        pe.wait_ge(s_const, 16 * NDMA)
        for t in range(NQ * NSUB):
            q, s = divmod(t, NSUB)
            if s == 0:
                pe.wait_ge(s_x, 16 * (q + 1))
            if t >= 2:
                pe.wait_ge(s_liftv, t - 1)
            pe.matmul(ps[:, 6 + t % 2, :], lift[:], XR[:, 512 * s:512 * (s + 1)], start=True, stop=True).then_inc(s_lift, 1)
        pe_forward(pe, 0, True)
        barrier(pe, step0 + 1)
        with pe.Fori(0, L - 1) as l:
            pe_mix(pe, l)
            barrier(pe, step0 + 2 + 3 * l)
            pe_inverse(pe, l)
            barrier(pe, step0 + 3 + 3 * l)
            pe_forward(pe, l + 1, False)
            barrier(pe, step0 + 4 + 3 * l)
        pe_mix(pe, L - 1)
        barrier(pe, step0 + 2 + 3 * (L - 1))
        pe_inverse(pe, L - 1)
        barrier(pe, step0 + 3 + 3 * (L - 1))
        pe.wait_ge(s_qc, 2)
        pe.matmul(ps[0:QB, 4, 0:1], qone[:], agg[:, 9:10], start=True, stop=True).then_inc(s_q, 1)
        for t in range(NQ * NSUB):
            q, s = divmod(t, NSUB)
            if t >= 4:
                pe.wait_ge(s_qv, t - 3)
            pe.matmul(ps[0:QB, t % 4, :], qcol[:], V[:, q, 512 * s:512 * (s + 1)], start=True, stop=True).then_inc(s_q, 1)

    def scalar_program(act):
        for t in range(NQ * NSUB):
            q, s = divmod(t, NSUB)
            act.wait_ge(s_lift, t + 1)
            nc.scalar.copy(V[:, q, 512 * s:512 * (s + 1)], ps[:, 6 + t % 2, :]).then_inc(s_liftv, 1)
        act_forward(act, 0, True)
        barrier(act, step0 + 1)
        with act.Fori(0, L - 1) as l:
            act_mix(act, l)
            barrier(act, step0 + 2 + 3 * l)
            act_inverse(act, l)
            barrier(act, step0 + 3 + 3 * l)
            act_forward(act, l + 1, False)
            barrier(act, step0 + 4 + 3 * l)
        act_mix(act, L - 1)
        barrier(act, step0 + 2 + 3 * (L - 1))
        act_inverse(act, L - 1)
        barrier(act, step0 + 3 + 3 * (L - 1))
        act.wait_ge(s_q, 1)
        act.activation(qb[:, 1:2], ps[0:QB, 4, 0:1], ACT.Identity, bias=qb[:, 0:1]).then_inc(s_qc, 1)
        act.wait_ge(s_qc, 3)
        for t in range(NQ * NSUB):
            q, s = divmod(t, NSUB)
            act.wait_ge(s_q, t + 2)
            act.activation(V[0:QB, q, 512 * s:512 * (s + 1)], ps[0:QB, t % 4, :], ACT.Identity, bias=qb[:, 1:2]).then_inc(s_qv, 1)

    def vector_program(dve):
        nc.vector.memset(lift[:], 0.0).then_inc(s_zero, 1)
        nc.vector.memset(conv[:], 0.0).then_inc(s_zero, 1)
        nc.vector.memset(qone[:], 0.0).then_inc(s_zero, 1)
        dve_forward(dve, 0)
        barrier(dve, step0 + 1)
        with dve.Fori(0, L - 1) as l:
            dve_mix(dve, l)
            barrier(dve, step0 + 2 + 3 * l)
            dve_inverse(dve, l)
            barrier(dve, step0 + 3 + 3 * l)
            dve_forward(dve, l + 1)
            barrier(dve, step0 + 4 + 3 * l)
        dve_mix(dve, L - 1)
        barrier(dve, step0 + 2 + 3 * (L - 1))
        dve_inverse(dve, L - 1)
        barrier(dve, step0 + 3 + 3 * (L - 1))
        dve.wait_ge(s_const, 16 * NDMA)
        nc.vector.tensor_scalar(qcol[:], qone[:], scale, None, ALU.mult).then_inc(s_qc, 2)

    return ctx, dict(sync=sync_program, tensor=tensor_program, scalar=scalar_program, vector=vector_program), step0 + 3 * L, own


D = 64
T = 192
NP = 16
NC = 3
ROW = NC * D
LN_EPS = 1e-5
WEIGHTS = 8192


class Names:
    pass


def signals(nc, ctx, tag, names):
    return [ctx.enter_context(nc.semaphore(f"{tag}_{n}")) for n in names]


def wait_apart(eng, m, *waits):
    waits = [(sem, eng.snap(value)) for sem, value in waits]
    eng.wait_ge(m.weights, 16)
    for sem, value in waits:
        eng.wait_ge(sem, value)


def pair(t, n, w=ROW):
    return t[:, bass.ds(n * w, w)]


def bcast(ap, w):
    return ap.unsqueeze(2).broadcast_to(list(ap.shape) + [w])


def rolled(m, s, nth, nprep, steps, before=lambda: None, values=None):
    def program(eng):
        before()
        eng.wait_ge(m.weights, 16 * m.n_weights)
        eng.wait_ge(s.prep, nprep)
        eng.wait_ge(m.ln.rstd, nth)
        with eng.Fori(0, NP // 2) as it:
            m.turn = it
            if values:
                for v in values(it):
                    eng.wait_ge(m.weights, v)
            for step in steps:
                for k in range(2):
                    step(eng, 2 * it + k, k)
    return program


def layer_norm(nc, m, j, eps=LN_EPS, src=None):
    s = m.ln
    src = m.H if src is None else src
    h3, xc3, sq3 = (t[:].rearrange("p (n d) -> p n d", d=D) for t in (src, m.XC, m.SQ))

    def vector(dve):
        nc.vector.tensor_reduce(m.msum[:], h3, AX.X, ALU.add).then_inc(s.dve, 1)
        dve.wait_ge(s.dve, 5 * j + 1)
        nc.vector.tensor_scalar(m.mean[:], m.msum[:], 1.0 / D, None, ALU.mult).then_inc(s.dve, 1)
        dve.wait_ge(s.dve, 5 * j + 2)
        nc.vector.tensor_tensor(xc3, h3, bcast(m.mean[:], D), ALU.subtract).then_inc(s.dve, 1)
        dve.wait_ge(s.square, j + 1)
        nc.vector.tensor_reduce(m.ssq[:], sq3, AX.X, ALU.add).then_inc(s.dve, 1)
        dve.wait_ge(s.dve, 5 * j + 4)
        nc.vector.tensor_scalar(m.var[:], m.ssq[:], 1.0 / D, eps, ALU.mult, ALU.add).then_inc(s.dve, 1)

    def scalar(act):
        act.wait_ge(s.dve, 5 * j + 3)
        nc.scalar.activation(m.SQ[:], m.XC[:], ACT.Square).then_inc(s.square, 1)

    def gpsimd(pool):
        pool.wait_ge(s.dve, 5 * j + 5)
        pool.wait_ge(s.mhalf, 1)
        nc.gpsimd.tensor_tensor(m.rstd[:], m.var[:], m.mhalf[:], ALU.pow).then_inc(s.rstd, 1)

    return dict(vector=vector, scalar=scalar, gpsimd=gpsimd)


def attention(nc, ctx, work, m, d, nth):
    wb = m.weight
    sb = lambda n, s: work.enter_context(nc.sbuf_tensor("att_" + n, s, F32))
    s = Names()
    (s.prep, s.xn, s.turned, s.xt, s.proj, s.qk, s.v, s.scores, s.centred, s.probs, s.turnedp, s.pt,
     s.heads, s.ready, s.turnedo, s.ot, s.out, s.free) = signals(nc, ctx, "att", (
        "prep", "xn", "turned", "xt", "proj", "qk", "v", "scores", "centred", "probs", "turnedp", "pt",
        "heads", "ready", "turnedo", "ot", "out", "free"))
    ps, ident, H = m.ps, m.ident, m.H
    wqk = wb("wqk", [D + 1, 2 * D])
    wv = wb("wv", [D + 1, D + 2])
    wo = wb("wo", [D + 1, D])
    L2 = range(2)
    xn = [sb(f"xn{k}", [P, NC, D + 1]) for k in L2]
    xt = [sb(f"xt{k}", [D + 1, NC, P]) for k in L2]
    qk = [sb(f"qk{k}", [D, 2, NC, P]) for k in L2]
    v = [sb(f"v{k}", [P, NC, D + 1]) for k in L2]
    mask = [sb(f"mask{k}", [P, 2, NC]) for k in L2]
    top = [sb(f"top{k}", [P, NC]) for k in L2]
    sc = [sb(f"sc{k}", [P, NC, T]) for k in L2]
    pr = [sb(f"pr{k}", [P, NC, NC, P]) for k in L2]
    pt = [sb(f"pt{k}", [P, NC, NC, P]) for k in L2]
    rs = [sb(f"rs{k}", [P, 2, NC]) for k in L2]
    o = [sb(f"o{k}", [P, NC, D + 1]) for k in L2]
    ot = [sb(f"ot{k}", [D + 1, NC, P]) for k in L2]
    bank = lambda k, b: ps[:, 4 * k + b, :]
    NPREP = 8

    def sync(sp):
        for dst, src in ((wqk, d["att_wqk"]), (wv, d["att_wv"]), (wo, d["att_wo"])):
            m.n_weights += 1
            sp.dma_start(dst[:], src).then_inc(m.weights, 16)

    def prep():
        for k in L2:
            nc.vector.memset(pr[k][:], 0.0).then_inc(s.prep, 1)
            nc.vector.memset(v[k][:, :, D:D + 1], 1.0).then_inc(s.prep, 1)
            nc.vector.memset(xn[k][:, :, D:D + 1], 1.0).then_inc(s.prep, 1)
            nc.vector.memset(o[k][:, :, D:D + 1], 1.0).then_inc(s.prep, 1)
        nc.vector.memset(m.junk[:], 0.0).then_inc(s.free, 2)

    def normalise(dve, n, k):
        dve.wait_ge(s.free, n + 1)
        nc.vector.tensor_tensor(xn[k][:, :, 0:D], pair(m.XC, n).rearrange("p (c d) -> p c d", d=D),
                                bcast(pair(m.rstd, n, NC), D), ALU.mult).then_inc(s.xn, 1)

    def turn_x(pe, n, k):
        pe.wait_ge(s.xn, n + 1)
        for c in range(NC):
            mm = pe.transpose(bank(k, 0)[0:D + 1, P * c:P * (c + 1)], xn[k][:, c, :], ident[:])
        mm.then_inc(s.turned, 1)

    def copy_xt(act, n, k):
        act.wait_ge(s.turned, n + 1)
        nc.scalar.activation(xt[k][:].rearrange("p c n -> p (c n)"), bank(k, 0)[0:D + 1, 0:NC * P], ACT.Copy).then_inc(s.xt, 1)

    def project(pe, n, k):
        pe.wait_ge(s.xt, n + 1)
        x = xt[k][:].rearrange("p c n -> p (c n)")
        for j in range(2):
            pe.matmul(bank(k, 1 + j)[0:D, 0:NC * P], wqk[:, D * j:D * (j + 1)], x, start=True, stop=True)
        for c in range(NC):
            mm = pe.matmul(bank(k, 3)[:, (D + 2) * c:(D + 2) * (c + 1)], xt[k][:, c, :], wv[:], start=True, stop=True)
        mm.then_inc(s.proj, 1)

    def copy_qk(act, n, k):
        act.wait_ge(s.proj, n + 1)
        nc.scalar.activation(qk[k][:].rearrange("p j c n -> p j (c n)"), ps[0:D, 4 * k + 1:4 * k + 3, 0:NC * P], ACT.Copy).then_inc(s.qk, 1)

    def copy_v(dve, n, k):
        src = bank(k, 3)[:, 0:(D + 2) * NC].rearrange("p (c e) -> p c e", c=NC)
        dve.wait_ge(s.proj, n + 1)
        nc.vector.tensor_copy(v[k][:, :, 0:D], src[:, :, 0:D])
        nc.vector.tensor_scalar(mask[k][:], src[:, :, D:D + 2].rearrange("p c j -> p j c"), 0.0, None, ALU.not_equal).then_inc(s.v, 1)

    def scores(pe, n, k):
        wait_apart(pe, m, (s.qk, n + 1))
        q = qk[k][:].rearrange("p j c (b t) -> p j c b t", b=2)
        for b in range(2):
            for c in range(NC):
                mm = pe.matmul(bank(k, c // 2)[D * b:D * (b + 1), 256 * (c % 2):256 * (c % 2) + T],
                               q[:, 0, c, b, :], q[:, 1, :, b, :], start=True, stop=True)
        mm.then_inc(s.scores, 1)

    def centre(dve, n, k):
        src = ps[:, 4 * k:4 * k + 2, :].rearrange("p g (c t) -> p (g c) t", t=256)[:, 0:NC, 0:T]
        dve.wait_ge(s.scores, n + 1)
        nc.vector.tensor_reduce(top[k][:], src, AX.X, ALU.max).then_inc(s.centred, 1)
        dve.wait_ge(s.centred, 2 * n + 1)
        nc.vector.tensor_tensor(sc[k][:], src, bcast(top[k][:], T), ALU.subtract).then_inc(s.centred, 1)

    def exponent(act, n, k):
        act.wait_ge(s.centred, 2 * n + 2)
        for b in range(2):
            h = slice(D * b, D * (b + 1))
            mm = nc.scalar.activation(pr[k][h, :, :, h].rearrange("p c e t -> p (c e) t"),
                                      sc[k][h].rearrange("p c (e t) -> p (c e) t", t=D), ACT.Exp, scale=D ** -0.5)
        mm.then_inc(s.probs, 1)

    def turn_probs(pe, n, k):
        pe.wait_ge(s.probs, n + 1)
        for c in range(NC):
            for e in range(NC):
                mm = pe.transpose(bank(k, c)[:, P * e:P * (e + 1)], pr[k][:, c, e, :], ident[:])
        mm.then_inc(s.turnedp, 1)

    def copy_pt(dve, n, k):
        dve.wait_ge(s.turnedp, n + 1)
        nc.vector.tensor_copy(pt[k][:].rearrange("p c e t -> p c (e t)"), ps[:, 4 * k:4 * k + 3, 0:NC * P]).then_inc(s.pt, 1)

    def heads(pe, n, k):
        pe.wait_ge(s.pt, n + 1)
        pe.wait_ge(s.v, n + 1)
        for c in range(NC):
            for e in range(NC):
                mm = pe.matmul(bank(k, 3)[:, (D + 1) * c:(D + 1) * (c + 1)], pt[k][:, c, e, :], v[k][:, e, :],
                               start=(e == 0), stop=(e == NC - 1), skip_group_check=True)
        mm.then_inc(s.heads, 1)

    def divide(dve, n, k):
        src = bank(k, 3)[:, 0:(D + 1) * NC].rearrange("p (c e) -> p c e", c=NC)
        dve.wait_ge(s.heads, n + 1)
        nc.vector.reciprocal(rs[k][:, 0, :], src[:, :, D])
        nc.vector.tensor_tensor(rs[k][:, 1, :], mask[k][:, 0, :], mask[k][:, 1, :], ALU.mult).then_inc(s.ready, 1)
        dve.wait_ge(s.ready, 3 * n + 1)
        nc.vector.tensor_tensor(rs[k][:, 0, :], rs[k][:, 0, :], rs[k][:, 1, :], ALU.mult).then_inc(s.ready, 1)
        dve.wait_ge(s.ready, 3 * n + 2)
        nc.vector.tensor_tensor(o[k][:, :, 0:D], src[:, :, 0:D], bcast(rs[k][:, 0, :], D), ALU.mult).then_inc(s.ready, 1)

    def turn_out(pe, n, k):
        pe.wait_ge(s.ready, 3 * n + 3)
        for c in range(NC):
            mm = pe.transpose(bank(k, 0)[0:D + 1, P * c:P * (c + 1)], o[k][:, c, :], ident[:])
        mm.then_inc(s.turnedo, 1)

    def copy_ot(act, n, k):
        act.wait_ge(s.turnedo, n + 1)
        nc.scalar.activation(ot[k][:].rearrange("p c n -> p (c n)"), bank(k, 0)[0:D + 1, 0:NC * P], ACT.Copy).then_inc(s.ot, 1)

    def project_out(pe, n, k):
        pe.wait_ge(s.ot, n + 1)
        for c in range(NC):
            mm = pe.matmul(bank(k, 1)[:, D * c:D * (c + 1)], ot[k][:, c, :], wo[:], start=True, stop=True)
        mm.then_inc(s.out, 1)

    def add_out(dve, n, k):
        dve.wait_ge(s.out, n + 1)
        nc.vector.tensor_tensor(pair(H, n), pair(H, n), bank(k, 1)[:, 0:ROW], ALU.add).then_inc(s.free, 1)

    return dict(sync=sync,
                tensor=rolled(m, s, nth, NPREP, [turn_x, project, scores, turn_probs, heads, turn_out, project_out]),
                scalar=rolled(m, s, nth, NPREP, [copy_xt, copy_qk, exponent, copy_ot]),
                vector=rolled(m, s, nth, NPREP, [normalise, copy_v, centre, copy_pt, divide, add_out], prep))


def common(nc, ctx):
    sb = lambda n, s: ctx.enter_context(nc.sbuf_tensor(n, s, F32))
    m = Names()
    m.H, m.XC, m.SQ = sb("H", [P, NP * ROW]), sb("XC", [P, NP * ROW]), sb("SQ", [P, NP * ROW])
    N = NP * NC
    m.msum, m.mean, m.ssq, m.var, m.rstd, m.mhalf = (sb(n, [P, N]) for n in ("msum", "mean", "ssq", "var", "rstd", "mhalf"))
    m.junk, m.junk2 = sb("junk", [1, 1]), sb("junk2", [1, 1])
    arena = sb("weights", [P, WEIGHTS])
    used = [0]

    def weight(name, shape):
        assert len(shape) == 2 and used[0] + shape[1] <= WEIGHTS, name
        used[0] += shape[1]
        return arena[0:shape[0], used[0] - shape[1]:used[0]]

    m.weight = weight
    m.n_weights = 0
    m.weights = ctx.enter_context(nc.semaphore("token_weights"))
    m.ln = Names()
    (m.ln.dve, m.ln.square, m.ln.rstd, m.ln.mhalf, m.ln.twice) = signals(nc, ctx, "ln", (
        "dve", "square", "rstd", "mhalf", "twice"))
    return m


def slices(nc, ctx, work, m, d, nth):
    wb = m.weight
    sb = lambda n, s: work.enter_context(nc.sbuf_tensor("sl_" + n, s, F32))
    s = Names()
    (s.prep, s.wsl, s.wslc, s.wab, s.wabc, s.xn, s.turned, s.xt, s.logits, s.centred, s.expd, s.weights,
     s.z, s.zn, s.turnedw, s.wt, s.turnedz, s.zt, s.st, s.stc, s.qv, s.qvc, s.s, s.sd, s.probs, s.turnedp,
     s.pt, s.ow, s.own, s.out, s.free) = signals(nc, ctx, "sl", (
        "prep", "wsl", "wslc", "wab", "wabc", "xn", "turned", "xt", "logits", "centred", "expd", "weights",
        "z", "zn", "turnedw", "wt", "turnedz", "zt", "st", "stc", "qv", "qvc", "s", "sd", "probs",
        "turnedp", "pt", "ow", "own", "out", "free"))
    ps, ident, H = m.ps, m.ident, m.H
    HD, G, HP = 8, 64, 4
    wx = wb("wx", [D, HD * (D + 1)])
    ws = wb("ws", [D, G])
    rows = wb("rows", [D + 1, 2 * HD * G])
    wfx = wb("wfx", [D + 1, HD * D])
    wq, wk, wv = wb("wq", [D, D]), wb("wk", [D, D]), wb("wv", [D, D])
    wout = wb("wout", [D, HD * D])
    bout = wb("bout", [P, D])
    wsl = wb("wsl", [D + 1, HD * G])
    wqk = wb("wqk", [P, D])
    wvo = wb("wvo", [P, HP * D])
    L2 = range(2)
    xn = [sb(f"xn{k}", [P, NC, D + 1]) for k in L2]
    xt = [sb(f"xt{k}", [D + 1, NC, P]) for k in L2]
    top = [sb(f"top{k}", [P, NC * HD]) for k in L2]
    rec = [sb(f"rec{k}", [P, 2, NC * HD]) for k in L2]
    w = [sb(f"w{k}", [P, NC, HD * G]) for k in L2]
    wt = [sb(f"wt{k}", [P, NC, HP, P]) for k in L2]
    nz = [sb(f"nz{k}", [P, 2 * HP]) for k in L2]
    zn = [sb(f"zn{k}", [P, 2, HP, D + 1]) for k in L2]
    zt = [sb(f"zt{k}", [D + 1, 2, HP, P]) for k in L2]
    st = [sb(f"st{k}", [P, HP, 2, G]) for k in L2]
    qt = [sb(f"qt{k}", [P, HP, 2, G]) for k in L2]
    vo = [sb(f"vo{k}", [P, HP, 2, D + 1]) for k in L2]
    tops = [sb(f"tops{k}", [P, 8]) for k in L2]
    ss = [sb(f"ss{k}", [P, HP, 2, G]) for k in L2]
    pr = [sb(f"pr{k}", [P, HP, 2, P]) for k in L2]
    pt = [sb(f"pt{k}", [P, HP, 2, P]) for k in L2]
    ro = [sb(f"ro{k}", [P, 8]) for k in L2]
    ow = [sb(f"ow{k}", [P, HP, 2, D]) for k in L2]
    bank = lambda k, b: ps[:, 4 * k + b, :]
    NPREP = 6 + 5

    def sync(sp):
        for dst, src in ((wx, "wx"), (ws, "ws"), (wfx, "wfx"), (wq, "wqT"), (wk, "wkT"), (wv, "wvT"), (wout, "wout")):
            m.n_weights += 1
            sp.dma_start(dst[:], d["ffn_" + src]).then_inc(m.weights, 16)
        m.n_weights += 2
        sp.dma_start(rows[:], d["ffn_rows"].broadcast_to([D + 1, 2 * HD * G])).then_inc(m.weights, 16)
        sp.dma_start(bout[:], d["ffn_bout"].broadcast_to([P, D])).then_inc(m.weights, 16)

    def weights_tensor(pe):
        pe.wait_ge(m.weights, 16 * m.n_weights)
        for h in range(HD):
            mm = pe.matmul(ps[0:D + 1, 0, G * h:G * (h + 1)], wx[:, (D + 1) * h:(D + 1) * (h + 1)], ws[:], start=True, stop=True)
        mm.then_inc(s.wsl, 1)
        for j in range(2):
            pe.matmul(ps[D * j:D * (j + 1), 1, 0:D], wq[:], wk[:], start=True, stop=True)
            for hp in range(HP):
                c = D * (2 * hp + j)
                mm = pe.matmul(ps[D * j:D * (j + 1), 2, D * hp:D * (hp + 1)], wv[:], wout[:, c:c + D], start=True, stop=True)
        mm.then_inc(s.wab, 1)
        pe.wait_ge(s.wabc, 2)
        pe.wait_ge(s.wslc, 6)

    def weights_vector():
        dve = nc.vector
        for k in L2:
            dve.memset(xn[k][:, :, D:D + 1], 1.0).then_inc(s.prep, 1)
            dve.memset(vo[k][:, :, :, D:D + 1], 1.0).then_inc(s.prep, 1)
            dve.memset(pr[k][:], 0.0).then_inc(s.prep, 1)
        dve.memset(m.junk[:], 0.0).then_inc(s.free, 2)
        dve.wait_ge(m.weights, 16 * m.n_weights)
        t = rows[:, HD * G:]
        dve.tensor_scalar(t, t, 0.1, 5.0, ALU.max, ALU.min).then_inc(s.wslc, 1)
        dve.wait_ge(s.wslc, 1)
        dve.reciprocal(t, t).then_inc(s.wslc, 1)
        dve.wait_ge(s.wsl, 1)
        dve.tensor_copy(wsl[:], ps[0:D + 1, 0, :]).then_inc(s.wslc, 1)
        dve.wait_ge(s.wslc, 3)
        dve.tensor_tensor(wsl[D:D + 1], wsl[D:D + 1], rows[D:D + 1, 0:HD * G], ALU.add).then_inc(s.wslc, 1)
        dve.wait_ge(s.wslc, 4)
        dve.tensor_tensor(wsl[:], wsl[:], t, ALU.mult).then_inc(s.wslc, 2)
        dve.wait_ge(s.wab, 1)
        dve.tensor_copy(wqk[:], ps[:, 1, 0:D]).then_inc(s.wabc, 1)
        dve.tensor_copy(wvo[:], ps[:, 2, 0:HP * D]).then_inc(s.wabc, 1)
        dve.memset(m.junk[:], 0.0).then_inc(s.prep, 5)

    def normalise(dve, n, k):
        dve.wait_ge(s.free, n + 1)
        nc.vector.tensor_tensor(xn[k][:, :, 0:D], pair(m.XC, n).rearrange("p (c d) -> p c d", d=D),
                                bcast(pair(m.rstd, n, NC), D), ALU.mult).then_inc(s.xn, 1)

    def turn_x(pe, n, k):
        pe.wait_ge(s.xn, n + 1)
        for c in range(NC):
            mm = pe.transpose(bank(k, 0)[0:D + 1, P * c:P * (c + 1)], xn[k][:, c, :], ident[:])
        mm.then_inc(s.turned, 1)

    def copy_xt(act, n, k):
        act.wait_ge(s.turned, n + 1)
        nc.scalar.activation(xt[k][:].rearrange("p c n -> p (c n)"), bank(k, 0)[0:D + 1, 0:NC * P], ACT.Copy).then_inc(s.xt, 1)

    def logits(pe, n, k):
        pe.wait_ge(s.xt, n + 1)
        for c in range(NC):
            mm = pe.matmul(bank(k, 1 + c), xt[k][:, c, :], wsl[:], start=True, stop=True)
        mm.then_inc(s.logits, 1)

    def centre(dve, n, k):
        src = ps[:, 4 * k + 1:4 * k + 4, :].rearrange("p c (h g) -> p (c h) g", g=G)
        dst = w[k][:].rearrange("p c (h g) -> p (c h) g", g=G)
        dve.wait_ge(s.logits, n + 1)
        nc.vector.tensor_reduce(top[k][:], src, AX.X, ALU.max).then_inc(s.centred, 1)
        dve.wait_ge(s.centred, 2 * n + 1)
        nc.vector.tensor_tensor(dst, src, bcast(top[k][:], G), ALU.subtract).then_inc(s.centred, 1)

    def exponent(act, n, k):
        act.wait_ge(s.centred, 2 * n + 2)
        nc.scalar.activation(w[k][:], w[k][:], ACT.Exp).then_inc(s.expd, 1)

    def weigh(dve, n, k):
        e = w[k][:].rearrange("p c (h g) -> p (c h) g", g=G)
        dve.wait_ge(s.expd, n + 1)
        nc.vector.tensor_reduce(rec[k][:, 0, :], e, AX.X, ALU.add).then_inc(s.weights, 1)
        dve.wait_ge(s.weights, 3 * n + 1)
        nc.vector.reciprocal(rec[k][:, 1, :], rec[k][:, 0, :]).then_inc(s.weights, 1)
        dve.wait_ge(s.weights, 3 * n + 2)
        nc.vector.tensor_tensor(e, e, bcast(rec[k][:, 1, :], G), ALU.mult).then_inc(s.weights, 1)

    def gather(pe, n, k):
        wait_apart(pe, m, (s.weights, 3 * n + 3))
        for b in range(2):
            r = slice(D * b, D * (b + 1))
            for hp in range(HP):
                for c in range(NC):
                    mm = pe.matmul(bank(k, b)[:, (D + 1) * hp:(D + 1) * (hp + 1)], w[k][r, c, P * hp:P * (hp + 1)], xn[k][r, c, :],
                                   start=(c == 0), stop=(c == NC - 1), skip_group_check=True)
        mm.then_inc(s.z, 1)

    def turn_weights(pe, n, k):
        for c in range(NC):
            if c == 2:
                pe.wait_ge(s.wt, 2 * n + 1)
            for hp in range(HP):
                mm = pe.transpose(bank(k, 2 + c % 2)[:, P * hp:P * (hp + 1)], w[k][:, c, P * hp:P * (hp + 1)], ident[:])
            if c:
                mm.then_inc(s.turnedw, 1)

    def copy_wt(act, n, k):
        act.wait_ge(s.turnedw, 2 * n + 1)
        nc.scalar.activation(wt[k][:, 0:2].rearrange("p c h n -> p c (h n)"), ps[:, 4 * k + 2:4 * k + 4, :], ACT.Copy).then_inc(s.wt, 1)
        act.wait_ge(s.turnedw, 2 * n + 2)
        nc.scalar.activation(wt[k][:, 2].rearrange("p h n -> p (h n)"), bank(k, 2), ACT.Copy).then_inc(s.wt, 1)

    def slice_means(dve, n, k):
        z = ps[:, 4 * k:4 * k + 2, 0:(D + 1) * HP].rearrange("p b (h e) -> p b h e", h=HP)
        nzv = nz[k][:].rearrange("p (b h) -> p b h", b=2)
        dve.wait_ge(s.z, n + 1)
        nc.vector.tensor_scalar(nzv, z[:, :, :, D], 1e-5, None, ALU.add).then_inc(s.zn, 1)
        dve.wait_ge(s.zn, 4 * n + 1)
        nc.vector.reciprocal(nz[k][:], nz[k][:]).then_inc(s.zn, 1)
        dve.wait_ge(s.zn, 4 * n + 2)
        for b in range(2):
            nc.vector.tensor_tensor(zn[k][:, b], z[:, b], bcast(nzv[:, b, :], D + 1), ALU.mult).then_inc(s.zn, 1)

    def turn_z(pe, n, k):
        pe.wait_ge(s.zn, 4 * n + 4)
        for b in range(2):
            for hp in range(HP):
                mm = pe.transpose(bank(k, b)[0:D + 1, P * hp:P * (hp + 1)], zn[k][:, b, hp, :], ident[:])
        mm.then_inc(s.turnedz, 1)

    def copy_zt(dve, n, k):
        dve.wait_ge(s.turnedz, n + 1)
        nc.vector.tensor_copy(zt[k][:].rearrange("p b h n -> p b (h n)"), ps[0:D + 1, 4 * k:4 * k + 2, :]).then_inc(s.zt, 1)

    def slice_tokens(pe, n, k):
        pe.wait_ge(s.wt, 2 * n + 2)
        pe.wait_ge(s.zt, n + 1)
        for hp in range(HP):
            for j in range(2):
                c = D * (2 * hp + j)
                mm = pe.matmul(bank(k, 3)[D * j:D * (j + 1), P * hp:P * (hp + 1)], wfx[:, c:c + D],
                               zt[k][:, :, hp, G * j:G * (j + 1)], start=True, stop=True)
        mm.then_inc(s.st, 1)

    def copy_st(dve, n, k):
        dve.wait_ge(s.st, n + 1)
        nc.vector.tensor_copy(st[k][:].rearrange("p h b g -> p (h b g)"), bank(k, 3)).then_inc(s.stc, 1)

    def slice_qv(pe, n, k):
        wait_apart(pe, m, (s.stc, n + 1))
        for j in range(2):
            r = slice(D * j, D * (j + 1))
            pe.matmul(bank(k, 2)[r], wqk[r], st[k][r].rearrange("p h b g -> p (h b g)"), start=True, stop=True)
            for hp in range(HP):
                for b in range(2):
                    c = D * (2 * hp + b)
                    mm = pe.matmul(bank(k, 0)[r, c:c + D], st[k][r, hp, b, :], wvo[r, D * hp:D * (hp + 1)], start=True, stop=True)
        mm.then_inc(s.qv, 1)

    def copy_qv(act, n, k):
        act.wait_ge(s.qv, n + 1)
        nc.scalar.activation(qt[k][:].rearrange("p h b g -> p (h b g)"), bank(k, 2), ACT.Copy)
        nc.scalar.activation(vo[k][:].rearrange("p h b e -> p (h b) e")[:, :, 0:D], bank(k, 0).rearrange("p (m e) -> p m e", e=D), ACT.Copy).then_inc(s.qvc, 1)

    def slice_scores(pe, n, k):
        wait_apart(pe, m, (s.qvc, n + 1))
        for j in range(2):
            r = slice(D * j, D * (j + 1))
            for hp in range(HP):
                for b in range(2):
                    c = D * (2 * hp + b)
                    mm = pe.matmul(bank(k, 1)[r, c:c + D], qt[k][r, hp, b, :], st[k][r, hp, b, :], start=True, stop=True)
        mm.then_inc(s.s, 1)

    def centre_slices(dve, n, k):
        src = bank(k, 1).rearrange("p (m g) -> p m g", g=G)
        dve.wait_ge(s.s, n + 1)
        nc.vector.tensor_reduce(tops[k][:], src, AX.X, ALU.max).then_inc(s.sd, 1)
        dve.wait_ge(s.sd, 2 * n + 1)
        nc.vector.tensor_tensor(ss[k][:].rearrange("p h b g -> p (h b) g"), src, bcast(tops[k][:], G), ALU.subtract).then_inc(s.sd, 1)

    def exponent_slices(act, n, k):
        act.wait_ge(s.sd, 2 * n + 2)
        for j in range(2):
            r = slice(D * j, D * (j + 1))
            a = nc.scalar.activation(pr[k][r, :, :, r].rearrange("p h b g -> p (h b) g"),
                                     ss[k][r].rearrange("p h b g -> p (h b) g"), ACT.Exp, scale=D ** -0.5)
        a.then_inc(s.probs, 1)

    def turn_probs(pe, n, k):
        pe.wait_ge(s.probs, n + 1)
        for hp in range(HP):
            for b in range(2):
                q = 2 * hp + b
                mm = pe.transpose(bank(k, 2 + q // 4)[:, P * (q % 4):P * (q % 4 + 1)], pr[k][:, hp, b, :], ident[:])
        mm.then_inc(s.turnedp, 1)

    def copy_pt(dve, n, k):
        dve.wait_ge(s.turnedp, n + 1)
        nc.vector.tensor_copy(pt[k][:].rearrange("p (a h) b n -> p a (h b n)", a=2), ps[:, 4 * k + 2:4 * k + 4, :]).then_inc(s.pt, 1)

    def slice_out(pe, n, k):
        pe.wait_ge(s.pt, n + 1)
        for hp in range(HP):
            for b in range(2):
                q = 2 * hp + b
                mm = pe.matmul(bank(k, q // 4)[:, (D + 1) * (q % 4):(D + 1) * (q % 4 + 1)], pt[k][:, hp, b, :], vo[k][:, hp, b, :], start=True, stop=True)
        mm.then_inc(s.ow, 1)

    def divide(dve, n, k):
        src = ps[:, 4 * k:4 * k + 2, 0:(D + 1) * 4].rearrange("p a (m e) -> p a m e", m=4)
        rv = ro[k][:].rearrange("p (a m) -> p a m", a=2)
        dve.wait_ge(s.ow, n + 1)
        nc.vector.reciprocal(rv, src[:, :, :, D]).then_inc(s.own, 1)
        dve.wait_ge(s.own, 3 * n + 1)
        dst = ow[k][:].rearrange("p (a h) b e -> p a (h b) e", a=2)
        for a in range(2):
            nc.vector.tensor_tensor(dst[:, a], src[:, a, :, 0:D], bcast(rv[:, a, :], D), ALU.mult).then_inc(s.own, 1)

    def spread(pe, n, k):
        pe.wait_ge(s.own, 3 * n + 3)
        for b in range(2):
            for c in range(NC):
                for hp in range(HP):
                    mm = pe.matmul(bank(k, 2)[D * b:D * (b + 1), D * c:D * (c + 1)], wt[k][:, c, hp, D * b:D * (b + 1)], ow[k][:, hp, b, :],
                                   start=(hp == 0), stop=(hp == HP - 1), skip_group_check=True)
        mm.then_inc(s.out, 1)

    def add_out(dve, n, k):
        h3 = pair(H, n).rearrange("p (c d) -> p c d", d=D)
        dve.wait_ge(s.out, n + 1)
        nc.vector.tensor_tensor(xn[k][:, :, 0:D], bank(k, 2)[:, 0:ROW].rearrange("p (c d) -> p c d", d=D),
                                bout[:].unsqueeze(1).broadcast_to([P, NC, D]), ALU.add).then_inc(s.outb, 1)
        dve.wait_ge(s.outb, n + 1)
        nc.vector.tensor_tensor(h3, h3, xn[k][:, :, 0:D], ALU.add).then_inc(s.free, 1)

    s.outb = ctx.enter_context(nc.semaphore("sl_outb"))
    r = lambda steps, before=lambda: None: rolled(m, s, nth, NPREP, steps, before)
    loop = r([turn_x, logits, gather, turn_weights, turn_z, slice_tokens, slice_qv, slice_scores, turn_probs, slice_out, spread])

    def tensor(pe):
        weights_tensor(pe)
        loop(pe)

    return dict(sync=sync, tensor=tensor,
                scalar=r([copy_xt, exponent, copy_wt, copy_qv, exponent_slices]),
                vector=r([normalise, centre, weigh, slice_means, copy_zt, copy_st, centre_slices, copy_pt, divide, add_out], weights_vector))


class Link:

    def __init__(self, eng, sem, base):
        self.eng, self.sem, self.base, self.n = eng, sem, base, 0

    def __call__(self, instruction):
        self.n += 1
        instruction.then_inc(self.sem, 1)
        self.eng.wait_ge(self.sem, self.base + self.n)


def experts(nc, ctx, work, m, d, nth):
    wb = m.weight
    sb = lambda n, s, t=F32: work.enter_context(nc.sbuf_tensor("moe_" + n, s, t))
    s = Names()
    (s.prep, s.xn, s.turned, s.xt, s.xta, s.router, s.best, s.free, s.gates, s.exps, s.wp, s.turnedw, s.wt,
     s.zero, s.hid0, s.hid1, s.gelu0, s.gelu1, s.outs, s.bias, s.done, s.free2) = signals(nc, ctx, "moe", (
        "prep", "xn", "turned", "xt", "xta", "router", "best", "free", "gates", "exps", "wp", "turnedw",
        "wt", "zero", "hid0", "hid1", "gelu0", "gelu1", "outs", "bias", "done", "free2"))
    ps, ident, H = m.ps, m.ident, m.H
    E, HID = 8, 128
    hid, gelu = (s.hid0, s.hid1), (s.gelu0, s.gelu1)
    N = NP * NC
    gb = wb("gb", [D, 2])
    wr = wb("wr", [D + 1, E])
    w1 = wb("w1", [D + 1, E * HID])
    w2 = wb("w2", [HID, E * D])
    b2 = wb("b2", [32 * NC, ROW])
    iota = wb("iota", [P, E])
    L2 = range(2)
    xn = [sb(f"xn{k}", [P, NC, D + 1]) for k in L2]
    xt = [sb(f"xt{k}", [D + 1, NC, P]) for k in L2]
    XTA = sb("XTA", [D + 1, NP * NC * P])
    best = [sb(f"best{k}", [P, NC, E]) for k in L2]
    two = [sb(f"two{k}", [P, NC, 2]) for k in L2]
    index = [sb(f"index{k}", [P, NC, E], mybir.dt.uint32) for k in L2]
    lg = [sb(f"lg{k}", [P, NC, E]) for k in L2]
    TOP = sb("TOP", [P, N * 2])
    IX = sb("IX", [P, N * 2])
    ga = sb("ga", [P, 4, N])
    WF = sb("WF", [P, N * E])
    WG = sb("WG", [P, N * E])
    wp = [sb(f"wp{k}", [P, NC, 32]) for k in L2]
    wt = [sb(f"wt{k}", [32 * NC, P]) for k in L2]
    ht = [[sb(f"ht{k}{q}", [HID, NC * P]) for q in L2] for k in L2]
    prod = [sb(f"prod{k}", [P, NC, E, D]) for k in L2]
    red = [sb(f"red{k}", [P, NC, D]) for k in L2]
    hb = lambda k: ps[:, 6 + k, :]
    NPREP = 6

    def sync(sp):
        for dst, src in ((gb, "moe_gb"), (wr, "moe_wr"), (w1, "moe_w1"), (w2, "moe_w2")):
            m.n_weights += 1
            sp.dma_start(dst[:], d[src]).then_inc(m.weights, 16)
        sp.wait_ge(s.zero, 1)
        for c in range(NC):
            m.n_weights += 1
            sp.dma_start(b2[32 * c:32 * c + E, D * c:D * (c + 1)], d["moe_b2"]).then_inc(m.weights, 16)
        m.n_weights += 1
        sp.dma_start(iota[:], d["iota8"].broadcast_to([P, E])).then_inc(m.weights, 16)

    def zero():
        nc.vector.memset(b2[:], 0.0).then_inc(s.zero, 1)

    def prep():
        for k in L2:
            nc.vector.memset(xn[k][:, :, D:D + 1], 1.0).then_inc(s.prep, 1)
            nc.vector.memset(xt[k][D:D + 1], 1.0).then_inc(s.prep, 1)
            nc.vector.memset(wp[k][:], 0.0).then_inc(s.prep, 1)
        nc.vector.memset(m.junk[:], 0.0).then_inc(s.free, 2)
        nc.vector.memset(m.junk2[:], 0.0).then_inc(s.free2, 2)

    def normalise(dve, n, k):
        dve.wait_ge(s.free, n + 1)
        nc.vector.tensor_tensor(xn[k][:, :, 0:D], pair(m.XC, n).rearrange("p (c d) -> p c d", d=D),
                                bcast(pair(m.rstd, n, NC), D), ALU.mult).then_inc(s.xn, 1)

    def turn_x(pe, n, k):
        pe.wait_ge(s.xn, n + 1)
        for c in range(NC):
            mm = pe.transpose(ps[0:D + 1, k, P * c:P * (c + 1)], xn[k][:, c, :], ident[:])
        mm.then_inc(s.turned, 1)

    def copy_xt(act, n, k):
        act.wait_ge(s.turned, n + 1)
        act.wait_ge(s.free, n + 1)
        nc.scalar.activation(xt[k][0:D].rearrange("p c n -> p (c n)"), ps[0:D, k, 0:NC * P], ACT.Identity,
                             bias=gb[:, 1:2], scale=gb[:, 0:1]).then_inc(s.xt, 1)

    def keep_xt(pool, n, k):
        pool.wait_ge(s.xt, n + 1)
        nc.gpsimd.tensor_copy(pair(XTA, n, NC * P), xt[k][:].rearrange("p c n -> p (c n)")).then_inc(s.xta, 1)

    def router(pe, n, k):
        pe.wait_ge(s.xt, n + 1)
        for c in range(NC):
            mm = pe.matmul(ps[:, 2 + k, E * c:E * (c + 1)], xt[k][:, c, :], wr[:], start=True, stop=True)
        mm.then_inc(s.router, 1)

    def pick(dve, n, k):
        dve.wait_ge(s.router, n + 1)
        nc.vector.tensor_copy(lg[k][:].rearrange("p c e -> p (c e)"), ps[:, 2 + k, 0:NC * E]).then_inc(s.best, 1)
        for c in range(NC):
            nc.vector.max(best[k][:, c, :], ps[:, 2 + k, E * c:E * (c + 1)]).then_inc(s.best, 1)
        dve.wait_ge(s.best, 8 * n + 4)
        nc.vector.tensor_copy(two[k][:], best[k][:, :, 0:2]).then_inc(s.best, 1)
        for c in range(NC):
            nc.vector.max_index(index[k][:, c, :], best[k][:, c, :], lg[k][:, c, :]).then_inc(s.best, 1)
        dve.wait_ge(s.best, 8 * n + 8)
        nc.vector.tensor_copy(pair(TOP, n, 2 * NC), two[k][:].rearrange("p c e -> p (c e)"))
        dve.wait_ge(s.xta, n + 1)
        nc.vector.tensor_copy(pair(IX, n, 2 * NC).rearrange("p (c e) -> p c e", e=2), index[k][:, :, 0:2]).then_inc(s.free, 1)

    t1, t2 = (TOP[:].rearrange("p (n e) -> p n e", e=2)[:, :, j] for j in range(2))
    i1, i2 = (IX[:].rearrange("p (n e) -> p n e", e=2)[:, :, j] for j in range(2))
    wf3, wg3 = (t[:].rearrange("p (n e) -> p n e", e=E) for t in (WF, WG))

    def gates(dve):
        dve.wait_ge(s.free, NP + 2)
        link = Link(dve, s.gates, 0)
        io = iota[:].unsqueeze(1).broadcast_to([P, N, E])
        link(nc.vector.tensor_tensor(ga[:, 0, :], t2, t1, ALU.subtract))
        dve.wait_ge(s.exps, 1)
        link(nc.vector.tensor_scalar(ga[:, 2, :], ga[:, 1, :], 1.0, None, ALU.add))
        link(nc.vector.reciprocal(ga[:, 2, :], ga[:, 2, :]))
        link(nc.vector.tensor_tensor(ga[:, 3, :], ga[:, 1, :], ga[:, 2, :], ALU.mult))
        link(nc.vector.tensor_tensor(wf3, io, bcast(i1, E), ALU.is_equal))
        link(nc.vector.tensor_tensor(wf3, wf3, bcast(ga[:, 2, :], E), ALU.mult))
        link(nc.vector.tensor_tensor(wg3, io, bcast(i2, E), ALU.is_equal))
        link(nc.vector.tensor_tensor(wg3, wg3, bcast(ga[:, 3, :], E), ALU.mult))
        link(nc.vector.tensor_tensor(WF[:], WF[:], WG[:], ALU.add))

    def exps(act):
        act.wait_ge(s.gates, 1)
        nc.scalar.activation(ga[:, 1, :], ga[:, 0, :], ACT.Exp).then_inc(s.exps, 1)

    def stage_gates(dve, n, k):
        dve.wait_ge(s.free2, n + 1)
        nc.vector.tensor_copy(wp[k][:, :, 0:E], pair(WF, n, NC * E).rearrange("p (c e) -> p c e", e=E)).then_inc(s.wp, 1)

    def turn_gates(pe, n, k):
        wait_apart(pe, m, (s.wp, n + 1), (s.free2, n + 1))
        pe.transpose(hb(k)[0:32 * NC, 0:P], wp[k][:].rearrange("p c e -> p (c e)"), ident[:]).then_inc(s.turnedw, 1)

    def copy_gates(dve, n, k):
        dve.wait_ge(s.turnedw, n + 1)
        nc.vector.tensor_copy(wt[k][:], hb(k)[0:32 * NC, 0:P]).then_inc(s.wt, 1)

    def hidden(pe, it, k, e):
        n = 2 * it + k
        if e == 0:
            pe.wait_ge(s.wt, n + 1)
        else:
            pe.wait_ge(gelu[k], 8 * it + e)
        pe.matmul(hb(k)[:, 0:NC * P], w1[:, HID * e:HID * (e + 1)], pair(XTA, n, NC * P), start=True, stop=True).then_inc(hid[k], 1)

    def activate(act, it, k, e):
        act.wait_ge(hid[k], 8 * it + e + 1)
        if e >= 2:
            act.wait_ge(s.outs, 16 * it + 2 * (e - 2) + k + 1)
        nc.scalar.activation(ht[k][e % 2][:], hb(k)[:, 0:NC * P], ACT.Gelu).then_inc(gelu[k], 1)

    def outputs(pe, it, k, e):
        pe.wait_ge(gelu[k], 8 * it + e + 1)
        for c in range(NC):
            mm = pe.matmul(ps[:, 3 * k + c, D * e:D * (e + 1)], ht[k][e % 2][:, P * c:P * (c + 1)], w2[:, D * e:D * (e + 1)], start=True, stop=True)
        mm.then_inc(s.outs, 1)

    def biases(pe, n, k):
        pe.matmul(hb(k)[:, 0:ROW], wt[k][:], b2[:], start=True, stop=True).then_inc(s.bias, 1)

    def combine(dve, n, k):
        h = pair(H, n)
        dve.wait_ge(s.bias, n + 1)
        link = Link(dve, s.done, 3 * n)
        for c in range(NC):
            ins = nc.vector.tensor_tensor(prod[k][:, c], ps[:, 3 * k + c, :].rearrange("p (e d) -> p e d", d=D), bcast(wp[k][:, c, 0:E], D), ALU.mult)
        link(ins)
        link(nc.vector.tensor_reduce(red[k][:], prod[k][:].rearrange("p c e d -> p c d e"), AX.X, ALU.add))
        link(nc.vector.tensor_tensor(h, h, red[k][:].rearrange("p c d -> p (c d)"), ALU.add))
        nc.vector.tensor_tensor(h, h, hb(k)[:, 0:ROW], ALU.add).then_inc(s.free2, 1)

    r = lambda steps, before=lambda: None: rolled(m, s, nth, NPREP, steps, before)

    def tensor(pe):
        r([turn_x, router])(pe)
        pe.wait_ge(s.xta, NP)
        pe.wait_ge(s.gates, 9)
        with pe.Fori(0, NP // 2) as it:
            for k in L2: turn_gates(pe, 2 * it + k, k)
            for k in L2: hidden(pe, it, k, 0)
            for e in range(E):
                for k in L2:
                    if e + 1 < E:
                        hidden(pe, it, k, e + 1)
                    outputs(pe, it, k, e)
            for k in L2: biases(pe, 2 * it + k, k)

    def scalar(act):
        r([copy_xt])(act)
        exps(act)
        with act.Fori(0, NP // 2) as it:
            for e in range(E):
                for k in L2: activate(act, it, k, e)

    def vector(dve):
        r([normalise, pick], prep)(dve)
        gates(dve)
        with dve.Fori(0, NP // 2) as it:
            for step in (stage_gates, copy_gates, combine):
                for k in L2: step(dve, 2 * it + k, k)

    return dict(sync=sync, tensor=tensor, scalar=scalar, vector=vector, gpsimd=r([keep_xt]), zero=zero)


def second_norm(nc, m, s):
    def vector(dve):
        dve.wait_ge(m.ln.rstd, s)
        nc.vector.tensor_tensor(m.SQ[:].rearrange("p (n d) -> p n d", d=D), m.XC[:].rearrange("p (n d) -> p n d", d=D),
                                bcast(m.rstd[:], D), ALU.mult).then_inc(m.ln.twice, 1)
        dve.wait_ge(m.ln.twice, 1)
    return dict(vector=vector)


def recurrence(nc, ctx, work, m, d, nth):
    wb = m.weight
    sb = lambda n, s: work.enter_context(nc.sbuf_tensor("rw_" + n, s, F32))
    s = Names()
    (s.prep, s.xn, s.turned, s.xf, s.mixed, s.proj, s.projc, s.projd, s.second, s.cum, s.decays, s.sq,
     s.norms, s.rkk, s.keys, s.mats, s.masked, s.tokmaj, s.out, s.on, s.sq2, s.gr, s.turnedo, s.ot, s.y,
     s.free, s.gated) = signals(nc, ctx, "rw", (
        "prep", "xn", "turned", "xf", "mixed", "proj", "projc", "projd", "second", "cum", "decays", "sq",
        "norms", "rkk", "keys", "mats", "masked", "tokmaj", "out", "on", "sq2", "gr", "turnedo", "ot", "y",
        "free", "gated"))
    wtok, inv_pe, inv_dve, chunk_pe, chunk_dve = ([ctx.enter_context(nc.semaphore(f"rw_{n}{k}")) for k in range(2)]
                                                  for n in ("wtok", "inv_pe", "inv_dve", "chunk_pe", "chunk_dve"))
    ps, ident, H = m.ps, m.ident, m.H
    L2 = range(2)
    CH = NC
    DECAY = -0.6065306597126334
    GN_EPS = D * 1e-5
    block = {n: wb(n, [P, P]) for n in ("W_r", "W_k", "A_w", "A_a", "B_w", "B_a")}
    wv = wb("wv", [P, D])
    ag = wb("ag", [P, 2 * D])
    bg = wb("bg", [P, D])
    wo = wb("wo", [D, D])
    cols = wb("cols", [P, 12])
    rowsb = wb("rows", [P, 4 * D])
    tri = wb("tri", [D, P])
    maskT = wb("maskT", [P, P])
    levT = wb("levT", [P, 5 * D])
    lev0 = wb("lev0", [P, 2 * D])
    ones = wb("ones", [P, P])
    eye = wb("eye", [P, D])
    xn = [sb(f"xn{k}", [P, CH, D + 1]) for k in L2]
    xf = [sb(f"xf{k}", [P, 1 + T]) for k in L2]
    dl = [sb(f"dl{k}", [P, T]) for k in L2]
    xm = [sb(f"xm{k}", [P, 6, T]) for k in L2]
    R = [sb(f"R{k}", [P, CH, D]) for k in L2]
    K = [sb(f"K{k}", [P, CH, D]) for k in L2]
    za = [sb(f"za{k}", [P, 2, T]) for k in L2]
    gh = [sb(f"gh{k}", [P, 2, T]) for k in L2]
    V = [sb(f"V{k}", [P, CH, D]) for k in L2]
    a = [sb(f"a{k}", [P, CH, D]) for k in L2]
    wt = [sb(f"wt{k}", [D, CH, P]) for k in L2]
    ce = [sb(f"ce{k}", [P, CH, 2, D]) for k in L2]
    ci = [sb(f"ci{k}", [P, CH, D]) for k in L2]
    kk = [sb(f"kk{k}", [P, CH, D]) for k in L2]
    nr = [sb(f"nr{k}", [P, T]) for k in L2]
    k2 = [sb(f"k2{k}", [P, CH, D]) for k in L2]
    rk = [sb(f"rk{k}", [P, CH, D]) for k in L2]
    ar = [sb(f"ar{k}", [P, CH, 2, D]) for k in L2]
    be = [sb(f"be{k}", [P, CH, D]) for k in L2]
    ka = [sb(f"ka{k}", [P, CH, D]) for k in L2]
    bk = [sb(f"bk{k}", [P, 2, CH, D]) for k in L2]
    bkt = [sb(f"bkt{k}", [P, 2, CH, D]) for k in L2]
    mb = [sb(f"mb{k}", [P, CH, P]) for k in L2]
    mk = [sb(f"mk{k}", [P, CH, P]) for k in L2]
    lv = [sb(f"lv{k}", [P, 5, CH, D]) for k in L2]
    X = [sb(f"X{k}", [P, CH, D]) for k in L2]
    XT = [sb(f"XT{k}", [P, CH, D]) for k in L2]
    U = [sb(f"U{k}", [P, CH, D]) for k in L2]
    rh = [sb(f"rh{k}", [P, D]) for k in L2]
    us = [sb(f"us{k}", [P, D]) for k in L2]
    S = [sb(f"S{k}", [P, D]) for k in L2]
    o = [sb(f"o{k}", [P, CH, D + 1]) for k in L2]
    osq = [sb(f"osq{k}", [P, CH, D]) for k in L2]
    gn = [sb(f"gn{k}", [P, 6, CH]) for k in L2]
    ot = [sb(f"ot{k}", [D, CH, P]) for k in L2]
    mh = sb("mh", [P, CH])
    bank = lambda k, b: ps[:, 4 * k + b, :]
    third = lambda ap: ap.rearrange("p (c d) -> p c d", c=CH)
    half = lambda b: slice(D * b, D * (b + 1))
    NPREP = 8

    def sync(sp):
        sp.wait_ge(s.prep, 1)
        for n, t in block.items():
            for b in range(2):
                m.n_weights += 1
                sp.dma_start(t[half(b), half(b)], d["rw_" + n]).then_inc(m.weights, 16)
        for dst, n in ((wv, "W_v"), (ag, "A_g")):
            for b in range(2):
                m.n_weights += 1
                sp.dma_start(dst[half(b)], d["rw_" + n]).then_inc(m.weights, 16)
        for dst, n in ((bg, "B_g"), (wo, "W_o"), (tri, "tri"), (maskT, "maskT"), (levT, "levT"), (lev0, "lev0"), (ones, "ones"), (eye, "eye2")):
            m.n_weights += 1
            sp.dma_start(dst[:], d["rw_" + n]).then_inc(m.weights, 16)
        m.n_weights += 2
        sp.dma_start(cols[:, 0:10], d["rw_cols"]).then_inc(m.weights, 16)
        sp.dma_start(rowsb[:], d["rw_rows"].broadcast_to([P, 4 * D])).then_inc(m.weights, 16)

    def zero():
        for i, t in enumerate(block.values()):
            ins = nc.vector.memset(t[:], 0.0)
        ins.then_inc(s.prep, 1)

    def prep():
        for k in L2:
            nc.vector.memset(xn[k][:, :, D:D + 1], 1.0)
            nc.vector.memset(o[k][:, :, D:D + 1], 1.0)
            nc.vector.memset(xf[k][:, 0:1], 0.0)
        nc.vector.memset(mh[:], -0.5).then_inc(s.prep, 5)
        nc.vector.memset(m.junk[:], 0.0).then_inc(s.free, 2)
        nc.vector.wait_ge(m.weights, 16 * m.n_weights)
        nc.vector.tensor_scalar(cols[:, 10:11], cols[:, 7:8], -1.0, 1.0, ALU.mult, ALU.add).then_inc(s.prep, 1)
        nc.vector.tensor_scalar(cols[:, 11:12], cols[:, 9:10], 0.5, None, ALU.mult).then_inc(s.prep, 1)

    def normalise(dve, n, k):
        dve.wait_ge(s.free, n + 1)
        nc.vector.tensor_tensor(xn[k][:, :, 0:D], pair(m.XC, n).rearrange("p (c d) -> p c d", d=D),
                                bcast(pair(m.rstd, n, NC), D), ALU.mult).then_inc(s.xn, 1)

    def turn_x(pe, n, k):
        if k == 0:
            pe.wait_ge(s.xn, n + 1)
            pe.transpose(bank(k, 3)[:, 0:P], ident[:], ident[:])
        wait_apart(pe, m, (s.xn, n + 1))
        for b in range(2):
            for c in range(CH):
                mm = pe.matmul(bank(k, 0)[half(b), D * c:D * (c + 1)], xn[k][half(b), c, 0:D], eye[half(b)], start=True, stop=True)
        mm.then_inc(s.turned, 1)

    def copy_xf(dve, n, k):
        dve.wait_ge(s.turned, n + 1)
        nc.vector.tensor_copy(xf[k][:, 1:], bank(k, 0)[:, 0:T]).then_inc(s.xf, 1)

    def mix(dve, n, k):
        dve.wait_ge(s.xf, n + 1)
        nc.vector.tensor_tensor(dl[k][:], xf[k][:, 0:T], xf[k][:, 1:], ALU.subtract).then_inc(s.mixed, 1)
        dve.wait_ge(s.mixed, 2 * n + 1)
        for i in range(6):
            ins = nc.vector.scalar_tensor_tensor(xm[k][:, i, :], dl[k][:], cols[:, i:i + 1], xf[k][:, 1:], ALU.mult, ALU.add)
        ins.then_inc(s.mixed, 1)

    def project(pe, n, k):
        pe.wait_ge(s.mixed, 2 * n + 2)
        for b, j, w, i in ((0, 0, "W_r", 0), (0, 1, "W_k", 2), (1, 0, "A_w", 1), (1, 1, "A_a", 4)):
            pe.matmul(bank(k, b)[:, T * j:T * (j + 1)], block[w][:], xm[k][:, i, :], start=True, stop=True)
        for b in range(2):
            for c in range(CH):
                pe.matmul(bank(k, 2)[half(b), D * c:D * (c + 1)], xm[k][half(b), 3, D * c:D * (c + 1)], wv[half(b)], start=True, stop=True)
        pe.matmul(bank(k, 2)[:, T:2 * T], ag[half(0)], xm[k][half(0), 5, :], start=True, stop=True)
        pe.matmul(bank(k, 3)[:, 0:T], ag[half(1)], xm[k][half(1), 5, :], start=True, stop=True).then_inc(s.proj, 1)

    def copy_proj_act(act, n, k):
        act.wait_ge(s.proj, n + 1)
        nc.scalar.activation(za[k][:, 0, :], bank(k, 1)[:, 0:T], ACT.Tanh)
        nc.scalar.activation(za[k][:, 1, :], bank(k, 1)[:, T:2 * T], ACT.Copy)
        nc.scalar.activation(gh[k][:, 0, :], bank(k, 2)[:, T:2 * T], ACT.Tanh, scale=0.5)
        nc.scalar.activation(gh[k][:, 1, :], bank(k, 3)[:, 0:T], ACT.Tanh, scale=0.5)
        nc.scalar.activation(V[k][:].rearrange("p c d -> p (c d)"), bank(k, 2)[:, 0:T], ACT.Copy).then_inc(s.projc, 1)

    def copy_proj_dve(dve, n, k):
        dve.wait_ge(s.proj, n + 1)
        nc.vector.tensor_copy(K[k][:], third(bank(k, 0)[:, T:2 * T]))
        nc.vector.tensor_copy(R[k][:], third(bank(k, 0)[:, 0:T])).then_inc(s.projd, 1)
        dve.wait_ge(s.projd, 3 * n + 1)
        nc.vector.tensor_scalar(kk[k][:], K[k][:], cols[:, 6:7], None, ALU.mult).then_inc(s.projd, 1)
        dve.wait_ge(s.projd, 3 * n + 2)
        nc.vector.tensor_tensor(nr[k][:], kk[k][:].rearrange("p c d -> p (c d)"), kk[k][:].rearrange("p c d -> p (c d)"), ALU.mult).then_inc(s.projd, 1)

    def second(pe, n, k):
        pe.wait_ge(s.projc, n + 1)
        pe.wait_ge(s.projd, 3 * n + 3)
        pe.matmul(bank(k, 0)[:, 0:T], block["B_a"][:], za[k][:, 1, :], start=True, stop=True)
        pe.matmul(bank(k, 2)[:, 0:T], ones[:], nr[k][:], start=True, stop=True)
        for c in range(CH):
            mm = pe.matmul(bank(k, 1)[0:D, P * c:P * (c + 1)], za[k][:, 0, D * c:D * (c + 1)], block["B_w"][:], start=True, stop=True)
        mm.then_inc(s.second, 1)

    def rates(dve, n, k):
        dve.wait_ge(s.second, n + 1)
        nc.vector.tensor_tensor(wt[k][:], bank(k, 1)[0:D, 0:CH * P].rearrange("p (c e) -> p c e", c=CH),
                                rowsb[0:D, 0:P].unsqueeze(1).broadcast_to([D, CH, P]), ALU.add).then_inc(wtok[k], 1)
        nc.vector.tensor_scalar(nr[k][:], bank(k, 2)[:, 0:T], 1e-24, None, ALU.max).then_inc(wtok[k], 1)

    def sigmoids(act, n, k):
        act.wait_ge(s.second, n + 1)
        nc.scalar.activation(a[k][:].rearrange("p c d -> p (c d)"), bank(k, 0)[:, 0:T], ACT.Tanh, bias=cols[:, 11:12], scale=0.5).then_inc(s.sq, 1)
        act.wait_ge(wtok[k], 4 * m.turn + 1)
        nc.scalar.activation(wt[k][:], wt[k][:], ACT.Tanh, scale=0.5).then_inc(s.sq, 1)

    def root(act, n, k):
        act.wait_ge(wtok[k], 4 * m.turn + 2)
        nc.scalar.activation(nr[k][:], nr[k][:], ACT.Sqrt).then_inc(s.norms, 1)

    def finish_rates(dve, n, k):
        dve.wait_ge(s.sq, 2 * n + 2)
        nc.vector.tensor_scalar(wt[k][:], wt[k][:], DECAY / 2, DECAY / 2, ALU.mult, ALU.add).then_inc(wtok[k], 1)
        nc.vector.tensor_scalar(a[k][:], a[k][:], 0.5, 0.5, ALU.mult, ALU.add)
        nc.vector.tensor_scalar(gh[k][:], gh[k][:], 0.5, 0.5, ALU.mult, ALU.add).then_inc(wtok[k], 1)

    def cumulate(pe, n, k):
        pe.wait_ge(wtok[k], 4 * m.turn + 3)
        for c in range(CH):
            mm = pe.matmul(bank(k, 3)[:, P * c:P * (c + 1)], wt[k][:, c, :], tri[:], start=True, stop=True)
        mm.then_inc(s.cum, 1)

    def decays(act, n, k):
        act.wait_ge(s.cum, n + 1)
        src = bank(k, 3)[:, 0:CH * P]
        nc.scalar.activation(ce[k][:].rearrange("p c j t -> p (c j t)"), src, ACT.Exp)
        nc.scalar.activation(ci[k][:], src.rearrange("p (c e) -> p c e", c=CH)[:, :, 0:D], ACT.Exp, scale=-1.0).then_inc(s.decays, 1)

    def keys(dve, n, k):
        link = Link(dve, s.keys, 5 * n)
        v = nc.vector
        dve.wait_ge(s.norms, n + 1)
        dve.wait_ge(wtok[k], 4 * m.turn + 4)
        link(v.reciprocal(nr[k][:], nr[k][:]))
        v.tensor_tensor(kk[k][:], kk[k][:], third(nr[k][:]), ALU.mult)
        link(v.tensor_scalar(k2[k][:], a[k][:], cols[:, 7:8], cols[:, 10:11], ALU.mult, ALU.add))
        v.tensor_tensor(a[k][:], kk[k][:], a[k][:], ALU.mult)
        link(v.tensor_tensor(k2[k][:], K[k][:], k2[k][:], ALU.mult))
        v.scalar_tensor_tensor(rk[k][:], R[k][:], cols[:, 8:9], k2[k][:], ALU.mult, ALU.mult)
        dve.wait_ge(s.decays, n + 1)
        v.tensor_tensor(ar[k][:, :, 0, :], kk[k][:], ce[k][:, :, 1, :], ALU.mult)
        v.tensor_tensor(ar[k][:, :, 1, :], R[k][:], ce[k][:, :, 0, :], ALU.mult)
        v.tensor_tensor(be[k][:], a[k][:], ci[k][:], ALU.mult)
        link(v.tensor_tensor(ka[k][:], k2[k][:], ci[k][:], ALU.mult))
        for j, t in enumerate((be, ka)):
            ins = v.tensor_tensor(bk[k][:, j], t[k][:], bcast(ce[k][:, :, 0, D - 1], D), ALU.mult)
        link(ins)

    def matrices(pe, n, k):
        wait_apart(pe, m, (s.keys, 5 * n + 5))
        for b in range(2):
            h = half(b)
            for c in range(CH):
                both = ar[k][h, c].rearrange("p j t -> p (j t)")
                pe.matmul(bank(k, 0)[h, P * c:P * (c + 1)], be[k][h, c], both, start=True, stop=True)
                pe.matmul(bank(k, 1)[h, P * c:P * (c + 1)], ka[k][h, c], both, start=True, stop=True)
                mm = pe.matmul(bank(k, 2)[h, D * c:D * (c + 1)], ar[k][h, c, 0], be[k][h, c], start=True, stop=True)
        mm.then_inc(s.mats, 1)
        for b in range(2):
            h = half(b)
            for j in range(2):
                for c in range(CH):
                    q = D * (CH * j + c)
                    mm = pe.matmul(bank(k, 3)[h, q:q + D], bk[k][h, j, c], eye[h], start=True, stop=True)
        mm.then_inc(s.tokmaj, 1)

    def copy_tokmaj(act, n, k):
        act.wait_ge(s.tokmaj, n + 1)
        nc.scalar.activation(bkt[k][:].rearrange("p j c d -> p (j c d)"), bank(k, 3)[:, 0:2 * T], ACT.Copy).then_inc(s.rkk, 1)

    def mask(dve, n, k):
        link = Link(dve, s.masked, 3 * n)
        v = nc.vector
        mt = maskT[:].unsqueeze(1).broadcast_to([P, CH, P])
        lev = lambda i: lev0[:, D * i:D * (i + 1)].unsqueeze(1).broadcast_to([P, CH, D])
        e3 = eye[:].unsqueeze(1).broadcast_to([P, CH, D])
        dve.wait_ge(s.mats, n + 1)
        v.tensor_tensor(mk[k][:], bank(k, 1)[:, 0:CH * P].rearrange("p (c e) -> p c e", c=CH), mt, ALU.mult)
        v.tensor_tensor(X[k][:], third(bank(k, 2)[:, 0:T]), lev(1), ALU.mult)
        link(v.tensor_tensor(mb[k][:], bank(k, 0)[:, 0:CH * P].rearrange("p (c e) -> p c e", c=CH), mt, ALU.mult))
        v.tensor_tensor(XT[k][:], mb[k][:, :, 0:D], lev(0), ALU.mult)
        v.tensor_tensor(X[k][:], e3, X[k][:], ALU.subtract)
        for j in range(5):
            ins = v.tensor_tensor(lv[k][:, j], mb[k][:, :, 0:D], levT[:, D * j:D * (j + 1)].unsqueeze(1).broadcast_to([P, CH, D]), ALU.mult)
        link(ins)
        v.tensor_tensor(XT[k][:], e3, XT[k][:], ALU.subtract).then_inc(s.masked, 1)

    def level_a(pe, n, k, j):
        if j == 0:
            wait_apart(pe, m, (s.masked, 3 * n + 3))
        else:
            wait_apart(pe, m, (inv_dve[k], 10 * m.turn + 2 * j))
        for b in range(2):
            h = half(b)
            for c in range(CH):
                mm = pe.matmul(bank(k, 2)[h, D * c:D * (c + 1)], lv[k][h, j, c], X[k][h, c], start=True, stop=True)
        mm.then_inc(inv_pe[k], 1)

    def level_a_copy(dve, n, k, j):
        dve.wait_ge(inv_pe[k], 10 * m.turn + 2 * j + 1)
        nc.vector.tensor_copy(U[k][:], third(bank(k, 2)[:, 0:T])).then_inc(inv_dve[k], 1)

    def level_b(pe, n, k, j):
        wait_apart(pe, m, (inv_dve[k], 10 * m.turn + 2 * j + 1))
        for b in range(2):
            h = half(b)
            for c in range(CH):
                if j < 4:
                    pe.matmul(bank(k, 0)[h, D * c:D * (c + 1)], XT[k][h, c], U[k][h, c], start=True, stop=True)
                mm = pe.matmul(bank(k, 1)[h, D * c:D * (c + 1)], U[k][h, c], XT[k][h, c], start=True, stop=True)
        mm.then_inc(inv_pe[k], 1)

    def level_b_sub(dve, n, k, j):
        dve.wait_ge(inv_pe[k], 10 * m.turn + 2 * j + 2)
        if j < 4:
            nc.vector.tensor_tensor(X[k][:], X[k][:], third(bank(k, 0)[:, 0:T]), ALU.subtract)
        nc.vector.tensor_tensor(XT[k][:], XT[k][:], third(bank(k, 1)[:, 0:T]), ALU.subtract).then_inc(inv_dve[k], 1)

    def right_side(pe, n, k, c):
        if c == 0:
            wait_apart(pe, m, (inv_dve[k], 10 * m.turn + 10), (s.rkk, n + 1))
        else:
            wait_apart(pe, m, (chunk_dve[k], at(c - 1, 2)))
        for b in range(2):
            h = half(b)
            if c:
                pe.matmul(bank(k, 0)[h, 0:D], ar[k][h, c, 0], S[k][h], start=True, stop=False, skip_group_check=True)
            mm = pe.matmul(bank(k, 0)[h, 0:D], mk[k][h, c, 0:D], V[k][h, c], start=(c == 0), stop=True, skip_group_check=True)
        mm.then_inc(chunk_pe[k], 1)

    def at(c, i):
        return 3 * CH * m.turn + 3 * c + i + 1

    def copy_right(dve, n, k, c):
        dve.wait_ge(chunk_pe[k], at(c, 0))
        nc.vector.tensor_scalar(rh[k][:], bank(k, 0)[:, 0:D], -1.0, None, ALU.mult).then_inc(chunk_dve[k], 1)

    def solve(pe, n, k, c):
        wait_apart(pe, m, (chunk_dve[k], at(c, 0)))
        for b in range(2):
            h = half(b)
            mm = pe.matmul(bank(k, 1)[h, 0:D], XT[k][h, c], rh[k][h], start=True, stop=True)
        mm.then_inc(chunk_pe[k], 1)

    def copy_u(dve, n, k, c):
        dve.wait_ge(chunk_pe[k], at(c, 1))
        nc.vector.tensor_copy(us[k][:], bank(k, 1)[:, 0:D]).then_inc(chunk_dve[k], 1)

    def advance(pe, n, k, c):
        wait_apart(pe, m, (chunk_dve[k], at(c, 1)))
        for b in range(2):
            h = half(b)
            if c + 1 < CH:
                pe.matmul(bank(k, 2)[h, 0:D], bkt[k][h, 0, c], us[k][h], start=True, stop=False, skip_group_check=True)
                pe.matmul(bank(k, 2)[h, 0:D], bkt[k][h, 1, c], V[k][h, c], start=False, stop=True, skip_group_check=True)
        for b in range(2):
            h = half(b)
            q = slice(D * c, D * (c + 1))
            if c:
                pe.matmul(bank(k, 3)[h, q], ar[k][h, c, 1], S[k][h], start=True, stop=False, skip_group_check=True)
            pe.matmul(bank(k, 3)[h, q], mb[k][h, c, D:P], us[k][h], start=(c == 0), stop=False, skip_group_check=True)
            mm = pe.matmul(bank(k, 3)[h, q], mk[k][h, c, D:P], V[k][h, c], start=False, stop=True, skip_group_check=True)
        mm.then_inc(chunk_pe[k], 1)

    def keep_state(dve, n, k, c):
        dve.wait_ge(chunk_pe[k], at(c, 2))
        if c == 0:
            nc.vector.tensor_copy(S[k][:], bank(k, 2)[:, 0:D]).then_inc(chunk_dve[k], 1)
        elif c + 1 < CH:
            nc.vector.scalar_tensor_tensor(S[k][:], S[k][:], ce[k][:, c, 0, D - 1:D], bank(k, 2)[:, 0:D], ALU.mult, ALU.add).then_inc(chunk_dve[k], 1)
        else:
            nc.vector.tensor_reduce(gn[k][:, 0, :], third(bank(k, 3)[:, 0:T]), AX.X, ALU.add).then_inc(chunk_dve[k], 1)

    def bonus(pe, n, k):
        wait_apart(pe, m, (chunk_pe[k], at(2, 2)))
        for b in range(2):
            for c in range(CH):
                pe.matmul(bank(k, 0)[half(b), c:c + 1], rk[k][half(b), c], ones[half(b), D * b:D * b + 1], start=True, stop=True)
        for b in range(2):
            for c in range(CH):
                mm = pe.matmul(bank(k, 1)[half(b), D * c:D * (c + 1)], gh[k][:, b, D * c:D * (c + 1)], bg[:], start=True, stop=True)
        mm.then_inc(s.out, 1)

    def group_norm(dve, n, k):
        v = nc.vector
        link = Link(dve, s.on, 8 * n)
        o3 = o[k][:, :, 0:D]
        dve.wait_ge(chunk_dve[k], at(2, 2))
        link(v.tensor_scalar(gn[k][:, 1, :], gn[k][:, 0, :], 1.0 / D, None, ALU.mult))
        link(v.tensor_tensor(o3, third(bank(k, 3)[:, 0:T]), bcast(gn[k][:, 1, :], D), ALU.subtract))
        dve.wait_ge(s.sq2, n + 1)
        link(v.tensor_reduce(gn[k][:, 2, :], osq[k][:], AX.X, ALU.add))
        link(v.tensor_scalar(gn[k][:, 3, :], gn[k][:, 2, :], 1.0 / D, GN_EPS, ALU.mult, ALU.add))
        dve.wait_ge(s.gr, n + 1)
        link(v.tensor_tensor(o3, o3, bcast(gn[k][:, 4, :], D), ALU.mult))
        link(v.tensor_tensor(o3, o3, rowsb[:, 2 * D:3 * D].unsqueeze(1).broadcast_to([P, CH, D]), ALU.mult))
        dve.wait_ge(s.out, n + 1)
        v.tensor_copy(gn[k][:, 5, :], bank(k, 0)[:, 0:CH])
        link(v.tensor_tensor(o3, o3, rowsb[:, 3 * D:4 * D].unsqueeze(1).broadcast_to([P, CH, D]), ALU.add))
        link(v.tensor_tensor(V[k][:], V[k][:], bcast(gn[k][:, 5, :], D), ALU.mult))
        v.tensor_tensor(o3, o3, V[k][:], ALU.add).then_inc(s.gated, 1)
        dve.wait_ge(s.gated, 2 * n + 1)
        v.tensor_tensor(o3, o3, third(bank(k, 1)[:, 0:T]), ALU.mult).then_inc(s.gated, 1)

    def square(act, n, k):
        act.wait_ge(s.on, 8 * n + 2)
        nc.scalar.activation(osq[k][:], o[k][:, :, 0:D], ACT.Square).then_inc(s.sq2, 1)

    def group_root(pool, n, k):
        pool.wait_ge(s.on, 8 * n + 4)
        nc.gpsimd.tensor_tensor(gn[k][:, 4, :], gn[k][:, 3, :], mh[:], ALU.pow).then_inc(s.gr, 1)

    def turn_out(pe, n, k):
        pe.wait_ge(s.gated, 2 * n + 2)
        for c in range(CH):
            mm = pe.transpose(bank(k, 2)[0:D + 1, P * c:P * (c + 1)], o[k][:, c, :], ident[:])
        mm.then_inc(s.turnedo, 1)

    def copy_ot(act, n, k):
        act.wait_ge(s.turnedo, n + 1)
        nc.scalar.activation(ot[k][:].rearrange("p c n -> p (c n)"), bank(k, 2)[0:D, 0:CH * P], ACT.Copy).then_inc(s.ot, 1)

    def project_out(pe, n, k):
        wait_apart(pe, m, (s.ot, n + 1))
        for c in range(CH):
            mm = pe.matmul(bank(k, 3)[:, D * c:D * (c + 1)], ot[k][:, c, :], wo[:], start=True, stop=True)
        mm.then_inc(s.y, 1)

    def add_out(dve, n, k):
        dve.wait_ge(s.y, n + 1)
        nc.vector.tensor_tensor(pair(H, n), pair(H, n), bank(k, 3)[:, 0:T], ALU.add).then_inc(s.free, 1)

    def with_index(f, j):
        return lambda eng, n, k: f(eng, n, k, j)

    inv = lambda fa, fb: [with_index(f, j) for j in range(5) for f in (fa, fb)]
    chunks = lambda *fs: [with_index(f, c) for c in range(CH) for f in fs]
    r = lambda steps, before=lambda: None, values=None: rolled(m, s, nth, NPREP, steps, before, values)

    def pe_values(it):
        return [2 * it + 1, 2 * it + 2, 5 * (2 * it) + 5, 5 * (2 * it + 1) + 5, 3 * (2 * it) + 3, 3 * (2 * it + 1) + 3] \
            + [10 * it + i for i in range(1, 11)] + [9 * it + i for i in range(1, 10)]

    return dict(sync=sync, zero=zero,
                tensor=r([turn_x, project, second, cumulate, matrices] + inv(level_a, level_b) + chunks(right_side, solve, advance)
                         + [bonus, turn_out, project_out], values=pe_values),
                scalar=r([copy_proj_act, sigmoids, root, decays, copy_tokmaj, square, copy_ot]),
                vector=r([normalise, copy_xf, mix, copy_proj_dve, rates, finish_rates, keys, mask] + inv(level_a_copy, level_b_sub)
                         + chunks(copy_right, copy_u, keep_state) + [group_norm, add_out], prep),
                gpsimd=r([group_root]))


def early_fusion(nc, x, txt, d, out):
    with ExitStack() as ctx:
        stage_done = ctx.enter_context(nc.semaphore("stage_done"))
        operator_done = ctx.enter_context(nc.semaphore("operator_done"))
        s_tokens = ctx.enter_context(nc.semaphore("tokens_loaded"))
        s_out = ctx.enter_context(nc.semaphore("out_written"))
        ps = ctx.enter_context(nc.psum_tensor("ps", [P, 8, 512], F32))
        y_img = nc.dram_tensor("image_tokens", [B, XY], F32, kind="Internal").ap()

        def operator_barrier(eng, k):
            eng.drain().then_inc(operator_done, 1)
            eng.wait_ge(operator_done, 4 * k)

        def barrier(eng, k):
            eng.drain().then_inc(stage_done, 1)
            eng.wait_ge(stage_done, 5 * (k - step))

        fno_ctx, fno, step, fno_signals = fourier_operator(nc, operator_barrier, ps, x, y_img, d, 0)
        fno_ctx.close()

        m = common(nc, ctx)
        m.ps = ps
        m.ident = ctx.enter_context(nc.sbuf_tensor("tok_ident", [P, P], F32))
        norm = [layer_norm(nc, m, 0), layer_norm(nc, m, 1), layer_norm(nc, m, 2), layer_norm(nc, m, 3),
                layer_norm(nc, m, 4, src=m.SQ)]
        twice = second_norm(nc, m, 4)
        blocks = []
        for make, nth in ((attention, 1), (slices, 2), (recurrence, 3), (experts, 5)):
            work = ExitStack()
            blocks.append(make(nc, ctx, work, m, d, nth))
            work.close()
        att, sli, rec, moe = blocks
        halves = [slice(D * b, D * (b + 1)) for b in range(2)]
        h4 = m.H[:].rearrange("p (q c d) -> p q c d", q=NP, c=NC)

        def load(sp):
            sp.dma_start(m.ident[:], d["ident"]).then_inc(s_tokens, 16)
            for b, r in enumerate(halves):
                sp.dma_start(h4[r, :, 0, :], y_img.rearrange("(q b) (x y) -> b x q y", b=2, x=S)[b]).then_inc(s_tokens, 16)
                for c in range(1, NC):
                    src = txt.rearrange("(q b) (c t) d -> b c t q d", b=2, c=NC - 1)[b, c - 1]
                    sp.dma_start(h4[r, :, c, :], src).then_inc(s_tokens, 16)
            for block in blocks:
                block["sync"](sp)
            sp.wait_ge(s_tokens, 16 * (1 + 2 * NC))

        def store(sp):
            dst = out.rearrange("(q b) (c t) d -> b c t q d", b=2, c=NC)
            for b, r in enumerate(halves):
                for c in range(NC):
                    sp.dma_start(dst[b, c], h4[r, :, c, :]).then_inc(s_out, 16)
            sp.wait_ge(s_out, 16 * 2 * NC)

        def program(name):
            def run(eng):
                def do(part):
                    if name in part and name != "sync":
                        part[name](eng)
                if name in fno:
                    fno[name](eng)
                barrier(eng, step + 1)
                if name == "sync":
                    for sem in fno_signals:
                        eng.sem_clear(sem)
                barrier(eng, step + 2)
                if name == "sync":
                    load(eng)
                if name == "vector":
                    rec["zero"]()
                    moe["zero"]()
                if name == "gpsimd":
                    nc.gpsimd.memset(m.mhalf[:], -0.5).then_inc(m.ln.mhalf, 1)
                barrier(eng, step + 3)
                for n, block in enumerate((att, sli, rec)):
                    do(norm[n])
                    do(block)
                    barrier(eng, step + 4 + n)
                do(norm[3])
                do(twice)
                barrier(eng, step + 7)
                do(norm[4])
                do(moe)
                barrier(eng, step + 8)
                if name == "sync":
                    store(eng)
            return run

        block = ctx.enter_context(nc.Block())
        block.sync(program("sync"))
        block.tensor(program("tensor"))
        block.scalar(program("scalar"))
        block.vector(program("vector"))
        block.gpsimd(program("gpsimd"))



def token_arrays(i):
    cat=np.concatenate
    r=lambda a: a.reshape(1,-1)
    a={}
    a["ident"]=np.eye(128,dtype=np.float32)
    g=lambda n: np.asarray(i["L0_attn_"+n])
    a["att_wqk"]=cat([cat([g("Wq").T,g("Wk").T],1),cat([r(g("bq")),r(g("bk"))],1)],0)
    a["att_wv"]=cat([cat([g("Wv").T,g("Wq").T[:,:1],g("Wk").T[:,:1]],1),cat([r(g("bv")),r(g("bq")[:1]),r(g("bk")[:1])],1)],0)
    a["att_wo"]=cat([g("Wo").T,r(g("bo"))],0)
    g=lambda n: np.asarray(i["L0_ffn_"+n])
    wx=cat([g("W_x"),r(g("b_x"))],0).reshape(65,8,64)
    a["ffn_wx"]=wx.transpose(2,1,0).reshape(64,8*65)
    a["ffn_ws"]=g("W_slice")
    a["ffn_rows"]=cat([np.tile(g("b_slice"),8)[None],np.repeat(g("temperature").reshape(-1),64)[None]],1)
    a["ffn_wfx"]=cat([g("W_fx"),r(g("b_fx"))],0)
    a["ffn_wqT"]=g("W_q").T; a["ffn_wkT"]=g("W_k").T; a["ffn_wvT"]=g("W_v").T
    a["ffn_wout"]=g("W_out").reshape(8,64,64).transpose(1,0,2).reshape(64,512)
    a["ffn_bout"]=r(g("b_out"))
    g=lambda n: np.asarray(i["L1_ffn_"+n])
    a["moe_gb"]=np.stack([g("gamma"),g("beta")],1)
    a["moe_wr"]=cat([g("Wr"),r(g("br"))],0)
    a["moe_w1"]=cat([g("W1").transpose(1,0,2).reshape(64,1024),g("b1").reshape(1,1024)],0)
    a["moe_w2"]=g("W2").transpose(1,0,2).reshape(128,512)
    a["moe_b2"]=g("b2")
    a["iota8"]=np.arange(8,dtype=np.float32)[None]
    g=lambda n: np.asarray(i["L1_attn_"+n])
    for n in ("W_r","W_k","A_w","A_a","B_w","B_a","W_v","A_g","B_g","W_o"): a["rw_"+n]=g(n)
    c=lambda v: v.reshape(64,-1)
    a["rw_cols"]=np.tile(cat([c(g("x_mix").T),c(g("k_k")),c(g("k_a")),c(g("r_k")),c(g("b_a"))],1),(2,1))
    a["rw_rows"]=cat([np.tile(g("b_w"),2),g("gn_w"),g("gn_b")])[None]
    t=np.arange(64)
    tri=(t[:,None]<=t[None]).astype(np.float32); strict=(t[:,None]<t[None]).astype(np.float32)
    a["rw_tri"]=cat([tri,strict],1)
    a["rw_maskT"]=np.tile(cat([strict,tri],1),(2,1))
    lv=[]
    for j in range(6):
        bs=1<<j
        mt=((t[:,None]//(2*bs)==t[None]//(2*bs))&(t[:,None]//bs%2==0)&(t[None]//bs%2==1)).astype(np.float32)
        lv.append(mt)
    a["rw_levT"]=np.tile(np.stack(lv[1:],1).reshape(64,320),(2,1))
    a["rw_lev0"]=np.tile(np.concatenate([lv[0],lv[0].T],1),(2,1))
    a["rw_ones"]=np.kron(np.eye(2),np.ones((64,64))).astype(np.float32)
    a["rw_eye2"]=np.tile(np.eye(64),(2,1)).astype(np.float32)
    return a


def operator_arrays(i):
    g = lambda n: np.asarray(i["L0_tok_" + n])
    a = fourier_constants()
    a["avg4"] = np.kron(np.ones((QB, QB)), np.eye(C)).astype(np.float32) / np.float32(QB)
    line = np.linspace(0.0, 1.0, S, dtype=np.float32)
    a["grid"] = np.stack([np.repeat(line, S), np.tile(line, S), np.ones(XY, np.float32)])
    for n in ("p_w", "p_b", "w_w", "q_w"):
        a[n] = g(n)
    for n in ("w_b", "bn_g", "bn_b"):
        a[n] = g(n).T
    fw = np.stack([g("fw1"), g("fw2")])
    a["modes"] = fw.transpose(1, 0, 6, 2, 5, 4, 3).reshape(L, P, -1)
    a["q_b4"] = np.tile(g("q_b").reshape(1, 1), (QB, 1))
    return a


def kernel(**inputs):
    import concourse.bacc as _bacc
    from concourse.bass_utils import run_bass_kernel_spmd as _run

    nc = _bacc.Bacc("TRN2", target_bir_lowering=False, num_devices=1)
    arrays, d = {}, {}
    laid = {**operator_arrays(inputs), **token_arrays(inputs),
            "x": np.asarray(inputs["x"]).reshape(B, XY), "txt": np.asarray(inputs["txt"])}
    for name, a in laid.items():
        a = np.ascontiguousarray(a)
        arrays[f"in_{name}"] = a
        d[name] = nc.dram_tensor(f"in_{name}", a.shape, F32, kind="ExternalInput").ap()
    out = nc.dram_tensor("out_0", (B, T, D), F32, kind="ExternalOutput").ap()
    early_fusion(nc, d["x"], d["txt"], d, out)
    r = _run(nc, [arrays], core_ids=[0])
    return r.results[0]["out_0"]
```

```python
from contextlib import ExitStack

import concourse.bass as bass
import numpy as np
from concourse import mybir

F32 = mybir.dt.float32
ALU = mybir.AluOpType
ACT = mybir.ActivationFunctionType
AX = mybir.AxisListType

P = 128
S = 64
XY = S * S
C = 32
L = 4
KY = 12
KX = 24
B = 32
QB = 4
NQ = B // QB
NSUB = XY // 512
BN_EPS = 1e-5


def fourier_constants():
    n = np.arange(S)
    ky = np.arange(KY)
    kx = np.concatenate([np.arange(KX // 2), np.arange(S - KX // 2, S)])
    ay = 2 * np.pi * np.outer(n, ky) / S
    ax = 2 * np.pi * np.outer(n, kx) / S
    fy = np.zeros((2, S, KY, 2, 2))
    for a in range(2):
        fy[a, :, :, a, 0] = np.cos(ay)
        fy[a, :, :, a, 1] = -np.sin(ay)
    fx = np.zeros((S, 2, 2, KX, 2))
    re = np.stack([np.cos(ax), np.sin(ax)], 1)
    im = np.stack([-np.sin(ax), np.cos(ax)], 1)
    fx[:, :, 0, :, 0] = re
    fx[:, :, 0, :, 1] = im
    fx[:, :, 1, :, 0] = -im
    fx[:, :, 1, :, 1] = re
    ix = np.zeros((2, KX, 2, 2, S, 2))
    for a in range(2):
        ix[a, :, 0, a, :, 0] = np.cos(ax).T
        ix[a, :, 1, a, :, 0] = -np.sin(ax).T
        ix[a, :, 0, a, :, 1] = np.sin(ax).T
        ix[a, :, 1, a, :, 1] = np.cos(ax).T
    wgt = np.where(ky == 0, 1.0, 2.0)[:, None] / XY
    iy = np.zeros((4, KY, 2, 4, S))
    for a in range(4):
        iy[a, :, 0, a] = wgt * np.cos(ay).T
        iy[a, :, 1, a] = -wgt * np.sin(ay).T
    f = np.float32
    return {
        "fy": fy.reshape(2 * S, KY * 4).astype(f),
        "fx": fx.reshape(2 * S, 4 * KX).astype(f),
        "ix": ix.reshape(4 * KX, 4 * S).astype(f),
        "iy": iy.reshape(8 * KY, 4 * S).astype(f),
    }


def fourier_operator(nc, barrier, ps, x, y_img, d, step0):
    ctx = ExitStack()
    sb = lambda n, s: ctx.enter_context(nc.sbuf_tensor("fno_" + n, s, F32))
    own = []

    def sem(n):
        own.append(ctx.enter_context(nc.semaphore(n)))
        return own[-1]


    V = sb("V", [P, NQ, XY])
    XS = sb("XS", [P, KY, KX // 2, 2, B])
    W = sb("W", [P, KY, KX // 2, C])
    stage = sb("stage", [P, 4608])
    fy = sb("fy", [P, 4 * KY])
    fx = sb("fx", [P, 4 * KX])
    ix = sb("ix", [4 * KX, 4 * S])
    iy = sb("iy", [8 * KY, 4 * S])
    ident = sb("ident", [P, P])
    avg4 = sb("avg4", [P, P])
    lift = sb("lift", [P, P])
    conv = sb("conv", [P, P])
    pv = sb("pv", [P, 3, L])
    stats = sb("stats", [P, NQ * NSUB, 6])
    agg = sb("agg", [P, 16])
    qcol = sb("qcol", [P, QB])
    qone = sb("qone", [P, QB])
    qb = sb("qb", [QB, 2])

    VB = [stage[:, 512 * k:512 * (k + 1)].rearrange("p (t n) -> p t n", n=P) for k in range(3)]
    Y1 = stage[:, 1536:1536 + 1536].rearrange("p (k n) -> p k n", n=P)
    T1 = stage[:, 3072:3072 + 1536].rearrange("p (k n) -> p k n", n=P)
    O = stage[:].rearrange("p (q k m) -> p q k m", q=NQ, k=KY)
    xs_flat = XS[:].rearrange("p k x s b -> p (k x s b)")
    T2 = [xs_flat[0:4 * KX, 768 * k:768 * (k + 1)].rearrange("p (k n) -> p k n", n=P) for k in range(2)]
    G = xs_flat[:, 3072:3072 + 1536].rearrange("p (x m) -> p x m", m=2 * KY)
    G2 = [xs_flat[0:8 * KY, 4608 + 2048 * k:4608 + 2048 * (k + 1)].rearrange("p (j n) -> p j n", n=P)
          for k in range(2)]
    V0 = xs_flat[:, 0:XY].rearrange("p (q n) -> p q n", q=1)
    FS = V[:, NQ - 1, 0:1152]
    lifts = V[:, NQ - 1, 1152:1152 + NQ * P]

    s_const = sem("fno_const"); s_zero = sem("fno_v0_zero"); s_qzero = sem("fno_qone_zero"); s_lay = sem("fno_layer_weights")
    s_w = sem("fno_mode_weights"); s_x = sem("fno_images"); s_rows = sem("fno_v_rows"); s_yout = sem("fno_out")
    s_xr = sem("fno_lifted"); s_fs = sem("fno_fs_ready")
    s_lift = sem("fno_lift_products"); s_liftc = sem("fno_lift_products_copied"); s_vzero = sem("fno_v_zero")
    s_v = sem("fno_v_ready")
    s_tr = sem("fno_v_turned"); s_vb = sem("fno_vb_ready")
    s_f1 = sem("fno_f1"); s_y1 = sem("fno_y1_ready")
    s_t1p = sem("fno_y1_turned"); s_t1 = sem("fno_t1_ready")
    s_f2 = sem("fno_f2"); s_xa = sem("fno_xs_by_act"); s_xd = sem("fno_xs_by_dve")
    s_mix = sem("fno_mixed"); s_oa = sem("fno_o_by_act"); s_od = sem("fno_o_by_dve")
    s_t2p = sem("fno_o_turned"); s_t2 = sem("fno_t2_ready")
    s_gp = sem("fno_gp"); s_g = sem("fno_g_ready")
    s_g2p = sem("fno_g_turned"); s_g2 = sem("fno_g2_ready")
    s_sum = sem("fno_summed"); s_vw = sem("fno_v_written"); s_st = sem("fno_stats")
    s_bn = sem("fno_bn_dve"); s_bnp = sem("fno_bn_pe"); s_bna = sem("fno_bn_act"); s_scale = sem("fno_scale")
    s_q = sem("fno_q"); s_qv = sem("fno_q_copied"); s_qc = sem("fno_q_col")

    scale, shift = agg[:, 8:9], agg[:, 9:10]

    def sync_program(sp):
        n = 0
        sp.dma_start(V0[0:B, 0, :], x).then_inc(s_x, 16)
        for dst, src in ((ident, d["ident"]), (fy, d["fy"]), (fx, d["fx"])):
            sp.dma_start(dst[:], src).then_inc(s_x, 16)
        sp.wait_ge(s_zero, 2)
        sp.dma_start(V0[B:B + 3, 0, :], d["grid"]).then_inc(s_x, 16)
        for dst, src in ((lifts, d["lifts"]), (lift, d["lift"]), (ix, d["ix"]), (iy, d["iy"]), (avg4, d["avg4"])):
            sp.dma_start(dst[:] if dst is not lifts else dst, src).then_inc(s_const, 16); n += 1

        def layer_weights(l):
            sp.dma_start(W[:].rearrange("p k x c -> p (k x c)"), d["modes"][bass.ds(l, 1)].rearrange("l p n -> (l p) n")).then_inc(s_w, 16)
        def conv_weights(l):
            sp.dma_start(conv[:], d["w_blocks"][bass.ds(l, 1)].rearrange("l c e -> (l c) e")).then_inc(s_lay, 16)
        conv_weights(0)
        sp.wait_ge(s_qzero, 1)
        for b in range(QB):
            c = slice(C * b, C * (b + 1))
            for k, name in enumerate(("w_b", "bn_g", "bn_b")):
                sp.dma_start(pv[c, k, :], d[name]).then_inc(s_const, 16)
            sp.dma_start(qone[c, b:b + 1], d["q_w"]).then_inc(s_const, 16)
            n += 4
        sp.dma_start(qb[0:QB, 0:1], d["q_b4"]).then_inc(s_const, 16); n += 1
        assert n == NDMA, n
        layer_weights(0)

        def v_rows(q0, q1):
            n = q1 - q0
            sp.dma_start(V[0:QB, q0:q1, :], x[QB * q0:QB * q1, :].rearrange("(q b) n -> b q n", b=QB)).then_inc(s_rows, 16)
            sp.dma_start(V[QB:QB + 3, q0:q1, :], d["grid"].unsqueeze(1).broadcast_to([3, n, XY])).then_inc(s_rows, 16)
            sp.dma_start(V[QB + 3:C, q0:q1, :], d["zero"].unsqueeze(1).broadcast_to([C - QB - 3, n, XY])).then_inc(s_rows, 16)
        v_rows(0, NQ - 1)
        sp.wait_ge(s_xr, NQ)
        v_rows(NQ - 1, NQ)
        barrier(sp, step0 + 1)
        for l in range(L - 1):
            barrier(sp, step0 + 2 + 3 * l)
            layer_weights(l + 1)
            barrier(sp, step0 + 3 + 3 * l)
            conv_weights(l + 1)
            barrier(sp, step0 + 4 + 3 * l)
        barrier(sp, step0 + 2 + 3 * (L - 1))
        barrier(sp, step0 + 3 + 3 * (L - 1))
        sp.wait_ge(s_qv, NQ * NSUB)
        sp.dma_start(y_img.rearrange("(q b) n -> b q n", b=QB), V[0:QB]).then_inc(s_yout, 16)
        sp.wait_ge(s_yout, 16)

    NDMA = 5 + 4 * QB + 1

    def keep_clock(pe, bank, n):
        for _ in range(n):
            pe.matmul(ps[:, bank, :], ident[:], stage[:, 0:512], start=True, stop=True)

    def pe_forward(pe, n0, nq, source, first):
        def turn(t):
            q, s = divmod(t, NSUB)
            if not first:
                pe.wait_ge(s_v, NSUB * (n0 - 1) + t + 1)
            if not first or t >= 3:
                pe.wait_ge(s_vb, NSUB * n0 + t - 2)
            for j in range(4):
                piece = slice(512 * s + P * j, 512 * s + P * (j + 1))
                mm = pe.transpose(ps[:, t % 3, P * j:P * (j + 1)], source[:, q, piece], ident[:])
            mm.then_inc(s_tr, 1)

        def along_y(t):
            k = t % 2
            pe.wait_ge(s_vb, NSUB * n0 + t + 1)
            if k == 0 and (not first or t >= 4):
                pe.wait_ge(s_y1, NSUB // 2 * n0 + t // 2 - 1)
            for j in range(4):
                c = 48 * (4 * k + j)
                mm = pe.matmul(ps[:, 3 + t // 2 % 2, c:c + 48], VB[t % 3][:, j, :], fy[:], start=True, stop=True)
            mm.then_inc(s_f1, 1)

        def turn_y1(q, g):
            if g == 0:
                pe.wait_ge(s_y1, NSUB // 2 * (n0 + q + 1))
                if not first:
                    pe.wait_ge(s_xa, (n0 + q + NQ - 1) * 8)
                    pe.wait_ge(s_xd, (n0 + q + NQ - 1) * 8)
            for j in range(4):
                mm = pe.transpose(ps[:, 5 + g, P * j:P * (j + 1)], Y1[:, 4 * g + j, :], ident[:])
            mm.then_inc(s_t1p, 1)

        def along_x(q):
            pe.wait_ge(s_t1, (n0 + q + 1) * 3)
            for j in range(KY):
                mm = pe.matmul(ps[:, 5 + j // 4, 96 * (j % 4):96 * (j % 4) + 96], T1[:, j, :], fx[:], start=True, stop=True)
            mm.then_inc(s_f2, 1)

        for t in range(NSUB * (nq + 1)):
            q, s = divmod(t - NSUB, NSUB)
            if t < NSUB * nq:
                turn(t)
            if 2 <= t < NSUB * nq + 2:
                along_y(t - 2)
            if q >= 0 and 3 <= s <= 5:
                turn_y1(q, s - 3)
            if t >= NSUB * nq + 2 and not first:
                keep_clock(pe, 0, 1)
            if q >= 0 and s == 7:
                along_x(q)
        if not first:
            keep_clock(pe, 0, 6)

    def y1_view(q_sub):
        return Y1.rearrange("p k (t m) -> p t k m", m=4)[:, 8 * q_sub:8 * (q_sub + 1)]

    def xs_parts():
        return [(b, h, c) for b in range(QB) for h in range(2) for c in range(2)]

    def xs_copy(op, q, b, h, c, bank=5):
        src = ps[C * b:C * (b + 1), bank:bank + 3, 0:384].rearrange("p g (k m) -> p g k m", k=4)[:, :, :, 48 * c + 24 * h:48 * c + 24 * h + 24]
        r = 64 * h + 32 * c
        dst = XS[r:r + 32].rearrange("p (g k) x s b -> p g k (x s) b", g=3)[:, :, :, :, QB * q + b]
        return op(dst, src)

    def act_copy(dst, src):
        return nc.scalar.activation(dst, src, ACT.Copy)

    def act_forward(act, n0, nq, first):
        def ready(t):
            q, s = divmod(t, NSUB)
            v = V[:, q, 512 * s:512 * (s + 1)]
            act.activation(v, v, ACT.Relu, bias=shift, scale=scale).then_inc(s_v, 1)
        def y1(u):
            act.wait_ge(s_f1, NSUB * n0 + 2 * u + 2)
            if u % 4 == 0 and not first:
                act.wait_ge(s_t1p, (n0 + u // 4) * 3)
            src = ps[:, 3 + u % 2, 0:384].rearrange("p (t k m) -> p t k m", t=8, k=KY)
            nc.scalar.activation(y1_view(u % 4), src, ACT.Copy).then_inc(s_y1, 1)
        def xs(q, part):
            act.wait_ge(s_f2, n0 + q + 1)
            for b, h, c in xs_parts()[:8][part]:
                xs_copy(act_copy, q, b, h, c).then_inc(s_xa, 1)
        for t in range(-4, NSUB * (nq + 1) + 3):
            if not first and t + 4 < NSUB * nq:
                ready(t + 4)
            if t >= 3 and t % 2 == 1 and (t - 3) // 2 < nq * NSUB // 2:
                y1((t - 3) // 2)
            q, s = divmod(t - 2 * NSUB, NSUB)
            if not first and q >= 0 and s < 3:
                xs(q, slice(3 * s, 3 * s + 3))

    def dve_forward(dve, n0, nq, first):
        def vb(t):
            dve.wait_ge(s_tr, NSUB * n0 + t + 1)
            if t >= 3:
                dve.wait_ge(s_f1, NSUB * n0 + t - 2)
            nc.vector.tensor_copy(VB[t % 3].rearrange("p t n -> p (t n)"), ps[:, t % 3, :]).then_inc(s_vb, 1)
        def t1(q, g):
            dve.wait_ge(s_t1p, (n0 + q) * 3 + g + 1)
            if g == 0 and q:
                dve.wait_ge(s_f2, n0 + q)
            nc.vector.tensor_copy(T1[:, 4 * g:4 * g + 4, :].rearrange("p k n -> p (k n)"), ps[:, 5 + g, :]).then_inc(s_t1, 1)
        def xs(q, part):
            dve.wait_ge(s_f2, n0 + q + 1)
            for b, h, c in xs_parts()[8:][part]:
                xs_copy(nc.vector.tensor_copy, q, b, h, c).then_inc(s_xd, 1)
        for t in range(NSUB * (nq + 1) + 3):
            if t < NSUB * nq:
                vb(t)
            q, s = divmod(t - NSUB, NSUB)
            if 0 <= q < nq and 4 <= s <= 6:
                t1(q, s - 4)
            q, s = divmod(t - 2 * NSUB, NSUB)
            if not first and q >= 0 and s < 3:
                xs(q, slice(3 * s, 3 * s + 3))

    def pe_lift(pe):
        pe.wait_ge(s_const, 16 * NDMA)
        pe.wait_ge(s_fs, 3)
        for q in range(NQ):
            if q >= 2:
                pe.wait_ge(s_xa, 8 * (q - 1))
                pe.wait_ge(s_xd, 8 * (q - 1))
            for g in range(3):
                mm = pe.matmul(ps[:, 5 * (q % 2) + g, 0:384], lifts[:, P * q:P * (q + 1)],
                               FS[:, 384 * g:384 * (g + 1)], start=True, stop=True)
            mm.then_inc(s_xr, 1)
        pe.transpose(ps[:, 3, 0:P], lift[:], ident[:]).then_inc(s_lift, 1)
        pe.wait_ge(s_lay, 16)
        pe.wait_ge(s_liftc, 1)
        pe.matmul(ps[:, 4, 0:P], Y1[:, 0, :], conv[:], start=True, stop=True).then_inc(s_lift, 1)
        keep_clock(pe, 3, 8)

    def act_lift(act):
        act.wait_ge(s_f2, 1)
        act_copy(FS[:, 0:384], ps[:, 5, 0:384]).then_inc(s_fs, 1)
        for q in range(NQ):
            act.wait_ge(s_xr, q + 1)
            for b, h, c in xs_parts()[:8]:
                xs_copy(act_copy, q, b, h, c, 5 * (q % 2)).then_inc(s_xa, 1)
        act.wait_ge(s_lift, 1)
        act_copy(Y1[:, 0, :], ps[:, 3, 0:P]).then_inc(s_liftc, 1)
        act.wait_ge(s_lift, 2)
        act_copy(conv[:], ps[:, 4, 0:P]).then_inc(s_liftc, 1)

    def dve_lift(dve):
        dve.wait_ge(s_f2, 1)
        for g in (1, 2):
            nc.vector.tensor_copy(FS[:, 384 * g:384 * (g + 1)], ps[:, 5 + g, 0:384]).then_inc(s_fs, 1)
        for q in range(NQ):
            dve.wait_ge(s_xr, q + 1)
            for b, h, c in xs_parts()[8:]:
                xs_copy(nc.vector.tensor_copy, q, b, h, c, 5 * (q % 2)).then_inc(s_xd, 1)

    def pe_mix(pe, m):
        for k in range(2, KY, 2):
            pe.wait_ge(s_const, m * 24 + 4 * (k // 2))
        pe.wait_ge(s_w, 16 * m + 16)
        pe.transpose(ps[:, 0, 0:P], ident[:], ident[:])
        keep_clock(pe, 0, 1)
        for k in range(KY):
            if k >= 2:
                pe.wait_ge(s_w, 16)
                pe.wait_ge(s_od if k % 2 else s_oa, m * 24 + 4 * (k // 2))
            for j in range(KX // 2):
                for h in range(2):
                    mm = pe.matmul(ps[0:C, 4 * (k % 2) + 2 * h + j // 6, 64 * (j % 6):64 * (j % 6) + 64],
                                   W[64 * h:64 * h + 64, k, j, :],
                                   XS[64 * h:64 * h + 64, k, j].rearrange("p s b -> p (s b)"), start=True, stop=True)
            mm.then_inc(s_mix, 1)

    def o_copy(op, k, b):
        src = ps[0:C, 4 * (k % 2):4 * (k % 2) + 4, 0:384].rearrange("p g (m q b) -> p g m q b", q=NQ, b=QB)[:, :, :, :, b]
        dst = O[C * b:C * (b + 1), :, k, :].rearrange("p q (g m) -> p g m q", g=4)
        return op(dst, src)

    def act_mix(act, m):
        for k in range(0, KY, 2):
            act.wait_ge(s_mix, m * KY + k + 1)
            for b in range(QB):
                o_copy(act_copy, k, b).then_inc(s_oa, 1)

    def dve_mix(dve, m):
        for k in range(1, KY, 2):
            dve.wait_ge(s_mix, m * KY + k + 1)
            for b in range(QB):
                o_copy(nc.vector.tensor_copy, k, b).then_inc(s_od, 1)

    def pe_inverse(pe, m):
        def turn_o(q):
            if q:
                pe.wait_ge(s_g2, (m * NQ + q) * 4)
            for g in range(2):
                for j in range(3):
                    k = 6 * g + 2 * j
                    mm = pe.transpose(ps[0:4 * KX, g, P * j:P * (j + 1)], O[:, q, k:k + 2, :].rearrange("p k m -> p (k m)"), ident[:])
                mm.then_inc(s_t2p, 1)
        def along_x(q):
            for g in range(3):
                pe.wait_ge(s_t2, (m * NQ + q) * 2 + (2 if g else 1))
                if q or g == 2:
                    pe.wait_ge(s_g, (m * NQ + q) * 3 + (1 if g == 2 else 0))
                for j in range(2):
                    mm = pe.matmul(ps[:, 2 + g % 2, 256 * j:256 * (j + 1)], T2[q % 2][:, 2 * g + j, :], ix[:], start=True, stop=True)
                mm.then_inc(s_gp, 1)
        def turn_g(q):
            pe.wait_ge(s_g, (m * NQ + q) * 3 + 3)
            for g in range(4):
                if g < 2:
                    pe.wait_ge(s_t2, (m * NQ + q) * 2 + 2)
                else:
                    pe.wait_ge(s_g2, (m * NQ + q) * 4 + g - 1)
                for j in range(4):
                    mm = pe.transpose(ps[0:8 * KY, g % 2, P * j:P * (j + 1)],
                                      G[:, 16 * g + 4 * j:16 * g + 4 * j + 4, :].rearrange("p x m -> p (x m)"), ident[:])
                mm.then_inc(s_g2p, 1)
        def sums(q, s):
            t = q * NSUB + s
            if s == 0:
                pe.wait_ge(s_g2, (m * NQ + q) * 4 + 4)
            if t >= 4:
                pe.wait_ge(s_vw, m * 64 + t - 3)
            bank = ps[:, 4 + t % 4, :]
            pe.matmul(bank, conv[:], V[:, q, 512 * s:512 * (s + 1)], start=True, stop=False, skip_group_check=True)
            for j in range(2):
                mm = pe.matmul(bank[:, 256 * j:256 * (j + 1)], G2[q % 2][:, 2 * s + j, :], iy[:], start=False, stop=True, skip_group_check=True)
            mm.then_inc(s_sum, 1)
        pe.wait_ge(s_lay, 16 * m + 16)
        pe.wait_ge(s_rows, 6 * 16)
        pe.wait_ge(s_vzero, 4)
        turn_o(0); along_x(0); turn_g(0)
        for q in range(NQ):
            for s in range(NSUB):
                sums(q, s)
                if q + 1 < NQ:
                    if s == 0: turn_o(q + 1)
                    if s == 2: along_x(q + 1)
                    if s == 4: turn_g(q + 1)
        keep_clock(pe, 2, 2)
        pe.wait_ge(s_bn, 5 * m + 1)
        pe.matmul(ps[:, 0, 0:1], avg4[:], agg[:, 0:1], start=True, stop=True).then_inc(s_bnp, 1)
        pe.wait_ge(s_bn, 5 * m + 3)
        pe.matmul(ps[:, 1, 0:1], avg4[:], agg[:, 3:4], start=True, stop=True).then_inc(s_bnp, 1)
        keep_clock(pe, 2, 3)

    def dve_inverse(dve, m):
        def t2(q):
            for g in range(2):
                dve.wait_ge(s_t2p, (m * NQ + q) * 2 + g + 1)
                if g == 0 and q >= 2:
                    dve.wait_ge(s_gp, (m * NQ + q - 1) * 3)
                nc.vector.tensor_copy(T2[q % 2][:, 3 * g:3 * g + 3, :].rearrange("p k n -> p (k n)"), ps[0:4 * KX, g, 0:384]).then_inc(s_t2, 1)
        def g2(q):
            for g in range(4):
                dve.wait_ge(s_g2p, (m * NQ + q) * 4 + g + 1)
                if g == 0 and q >= 2:
                    dve.wait_ge(s_sum, m * 64 + NSUB * (q - 1))
                nc.vector.tensor_copy(G2[q % 2][:, 4 * g:4 * g + 4, :].rearrange("p k n -> p (k n)"), ps[0:8 * KY, g % 2, :]).then_inc(s_g2, 1)
        def st(q, s):
            t = q * NSUB + s
            dve.wait_ge(s_sum, m * 64 + t + 1)
            nc.vector.bn_stats(stats[:, t, :], ps[:, 4 + t % 4, :]).then_inc(s_st, 1)
        t2(0); g2(0)
        for q in range(NQ):
            for s in range(NSUB):
                st(q, s)
                if q + 1 < NQ:
                    if s == 0: t2(q + 1)
                    if s == 4: g2(q + 1)
        dve.wait_ge(s_st, 64)
        dve.wait_ge(s_st, m * 64 + 64)
        mean, var, dev, sq = agg[:, 0:1], agg[:, 1:2], agg[:, 2:3], agg[:, 3:4]
        nc.vector.bn_aggr(agg[:, 0:2], stats[:].rearrange("p n s -> p (n s)")).then_inc(s_bn, 1)
        dve.wait_ge(s_bnp, 2 * m + 1)
        nc.vector.tensor_tensor(dev, mean, ps[:, 0, 0:1], ALU.subtract).then_inc(s_bn, 1)
        dve.wait_ge(s_bn, 5 * m + 2)
        nc.vector.scalar_tensor_tensor(sq, dev, dev, var, ALU.mult, ALU.add).then_inc(s_bn, 1)
        dve.wait_ge(s_bnp, 2 * m + 2)
        nc.vector.tensor_scalar(agg[:, 4:5], ps[:, 1, 0:1], BN_EPS, None, ALU.add).then_inc(s_bn, 1)
        dve.wait_ge(s_bna, m + 1)
        nc.vector.reciprocal(agg[:, 6:7], agg[:, 5:6]).then_inc(s_bn, 1)
        dve.wait_ge(s_bn, 5 * m + 5)
        w_b, bn_g, bn_b = (pv[:, k, bass.ds(m, 1)] for k in range(3))
        nc.vector.tensor_tensor(scale, agg[:, 6:7], bn_g, ALU.mult).then_inc(s_scl, 1)
        nc.vector.tensor_tensor(agg[:, 7:8], ps[:, 0, 0:1], w_b, ALU.add).then_inc(s_scl, 1)
        dve.wait_ge(s_scl, 3 * m + 2)
        nc.vector.tensor_tensor(agg[:, 10:11], agg[:, 7:8], scale, ALU.mult).then_inc(s_scl, 1)
        dve.wait_ge(s_scl, 3 * m + 3)
        nc.vector.tensor_tensor(shift, bn_b, agg[:, 10:11], ALU.subtract).then_inc(s_scale, 1)

    s_scl = sem("fno_scl")

    def act_inverse(act, m):
        def g(q):
            for g in range(3):
                act.wait_ge(s_gp, (m * NQ + q) * 3 + g + 1)
                if g == 0 and q:
                    act.wait_ge(s_g2p, (m * NQ + q) * 4)
                src = ps[:, 2 + g % 2, :].rearrange("p (k x r) -> p k x r", k=4, r=2)
                dst = G.rearrange("p x (k r) -> p k x r", r=2)[:, 4 * g:4 * g + 4]
                nc.scalar.activation(dst, src, ACT.Copy).then_inc(s_g, 1)
        def vw(q, s):
            t = q * NSUB + s
            act.wait_ge(s_st, m * 64 + t + 1)
            act.activation(V[:, q, 512 * s:512 * (s + 1)], ps[:, 4 + t % 4, :], ACT.Identity, bias=wb_col[:]).then_inc(s_vw, 1)
        act.wait_ge(s_const, 16 * NDMA)
        nc.scalar.copy(wb_col[:], pv[:, 0, bass.ds(m, 1)]).then_inc(s_wb, 1)
        g(0)
        act.wait_ge(s_wb, m + 1)
        for q in range(NQ):
            for s in range(NSUB):
                vw(q, s)
                if q + 1 < NQ and s == 2:
                    g(q + 1)
        act.wait_ge(s_bn, 5 * m + 4)
        nc.scalar.activation(agg[:, 5:6], agg[:, 4:5], ACT.Sqrt).then_inc(s_bna, 1)

    wb_col = sb("wb_col", [P, 1])
    s_wb = sem("fno_wb")

    def tensor_program(pe):
        pe.wait_ge(s_x, 5 * 16)
        pe_forward(pe, 0, 1, V0, True)
        pe_lift(pe)
        barrier(pe, step0 + 1)
        with pe.Fori(0, L - 1) as l:
            pe_mix(pe, l)
            barrier(pe, step0 + 2 + 3 * l)
            pe_inverse(pe, l)
            barrier(pe, step0 + 3 + 3 * l)
            pe_forward(pe, NQ * l + 1, NQ, V, False)
            barrier(pe, step0 + 4 + 3 * l)
        pe_mix(pe, L - 1)
        barrier(pe, step0 + 2 + 3 * (L - 1))
        pe_inverse(pe, L - 1)
        barrier(pe, step0 + 3 + 3 * (L - 1))
        pe.wait_ge(s_qc, 2)
        pe.matmul(ps[0:QB, 4, 0:1], qone[:], agg[:, 9:10], start=True, stop=True).then_inc(s_q, 1)
        for t in range(NQ * NSUB):
            q, s = divmod(t, NSUB)
            if t >= 4:
                pe.wait_ge(s_qv, t - 3)
            pe.matmul(ps[0:QB, t % 4, :], qcol[:], V[:, q, 512 * s:512 * (s + 1)], start=True, stop=True).then_inc(s_q, 1)

    def scalar_program(act):
        act_forward(act, 0, 1, True)
        act_lift(act)
        barrier(act, step0 + 1)
        with act.Fori(0, L - 1) as l:
            act_mix(act, l)
            barrier(act, step0 + 2 + 3 * l)
            act_inverse(act, l)
            barrier(act, step0 + 3 + 3 * l)
            act.wait_ge(s_scale, l + 1)
            act_forward(act, NQ * l + 1, NQ, False)
            barrier(act, step0 + 4 + 3 * l)
        act_mix(act, L - 1)
        barrier(act, step0 + 2 + 3 * (L - 1))
        act_inverse(act, L - 1)
        barrier(act, step0 + 3 + 3 * (L - 1))
        act.wait_ge(s_q, 1)
        act.activation(qb[:, 1:2], ps[0:QB, 4, 0:1], ACT.Identity, bias=qb[:, 0:1]).then_inc(s_qc, 1)
        act.wait_ge(s_qc, 3)
        for t in range(NQ * NSUB):
            q, s = divmod(t, NSUB)
            act.wait_ge(s_q, t + 2)
            act.activation(V[0:QB, q, 512 * s:512 * (s + 1)], ps[0:QB, t % 4, :], ACT.Identity, bias=qb[:, 1:2]).then_inc(s_qv, 1)

    def vector_program(dve):
        nc.vector.memset(V0[2 * B:P, 0, :], 0.0).then_inc(s_zero, 1)
        nc.vector.memset(qone[:], 0.0).then_inc(s_qzero, 1)
        dve_forward(dve, 0, 1, True)
        dve_lift(dve)
        barrier(dve, step0 + 1)
        with dve.Fori(0, L - 1) as l:
            dve_mix(dve, l)
            barrier(dve, step0 + 2 + 3 * l)
            dve_inverse(dve, l)
            barrier(dve, step0 + 3 + 3 * l)
            dve_forward(dve, NQ * l + 1, NQ, False)
            barrier(dve, step0 + 4 + 3 * l)
        dve_mix(dve, L - 1)
        barrier(dve, step0 + 2 + 3 * (L - 1))
        dve_inverse(dve, L - 1)
        barrier(dve, step0 + 3 + 3 * (L - 1))
        dve.wait_ge(s_const, 16 * NDMA)
        nc.vector.tensor_scalar(qcol[:], qone[:], scale, None, ALU.mult).then_inc(s_qc, 2)

    def gpsimd_program(pool):
        nc.gpsimd.memset(V0[B:2 * B, 0, :], 0.0).then_inc(s_zero, 1)
        pool.wait_ge(s_zero, 2)
        for part in (slice(0, NQ - 1), slice(NQ - 1, NQ)):
            if part.start:
                pool.wait_ge(s_xr, NQ)
            for rows in (slice(C, 2 * C), slice(2 * C, P)):
                nc.gpsimd.memset(V[rows, part].rearrange("p q n -> p (q n)"), 0.0).then_inc(s_vzero, 1)

    return ctx, dict(sync=sync_program, tensor=tensor_program, scalar=scalar_program, vector=vector_program,
                     gpsimd=gpsimd_program), step0 + 3 * L, own


D = 64
T = 192
NP = 16
TURNS = NP // 2
NC = 3
ROW = NC * D
LN_EPS = 1e-5
WEIGHTS = 8192


class Names:
    pass


def signals(nc, ctx, tag, names):
    return [ctx.enter_context(nc.semaphore(f"{tag}_{n}")) for n in names]


def wait_apart(eng, m, *waits):
    waits = [(sem, eng.snap(value)) for sem, value in waits]
    eng.wait_ge(m.weights, 16)
    for sem, value in waits:
        eng.wait_ge(sem, value)


def pair(t, n, w=ROW):
    return t[:, bass.ds(n * w, w)]


def bcast(ap, w):
    return ap.unsqueeze(2).broadcast_to(list(ap.shape) + [w])


def rolled(m, s, nth, nprep, steps, before=lambda: None, values=None):
    def program(eng):
        before()
        eng.wait_ge(m.weights, 16 * m.n_weights)
        eng.wait_ge(s.prep, nprep)
        with eng.Fori(0, NP // 2) as it:
            m.turn = it
            if values:
                for v in values(it):
                    eng.wait_ge(m.weights, v)
            for step in steps:
                for k in range(2):
                    step(eng, 2 * it + k, k)
    return program


def layer_norm(nc, m, j, eps=LN_EPS, src=None):
    s = m.ln
    src = m.H if src is None else src
    h3, xc3, sq3 = (t[:].rearrange("p (n d) -> p n d", d=D) for t in (src, m.XC, m.SQ))

    def vector(dve):
        nc.vector.tensor_reduce(m.msum[:], h3, AX.X, ALU.add).then_inc(s.dve, 1)
        dve.wait_ge(s.dve, 5 * j + 1)
        nc.vector.tensor_scalar(m.mean[:], m.msum[:], 1.0 / D, None, ALU.mult).then_inc(s.dve, 1)
        dve.wait_ge(s.dve, 5 * j + 2)
        nc.vector.tensor_tensor(xc3, h3, bcast(m.mean[:], D), ALU.subtract).then_inc(s.dve, 1)
        dve.wait_ge(s.square, j + 1)
        nc.vector.tensor_reduce(m.ssq[:], sq3, AX.X, ALU.add).then_inc(s.dve, 1)
        dve.wait_ge(s.dve, 5 * j + 4)
        nc.vector.tensor_scalar(m.var[:], m.ssq[:], 1.0 / D, eps, ALU.mult, ALU.add).then_inc(s.dve, 1)

    def scalar(act):
        act.wait_ge(s.dve, 5 * j + 3)
        nc.scalar.activation(m.SQ[:], m.XC[:], ACT.Square).then_inc(s.square, 1)

    def gpsimd(pool):
        pool.wait_ge(s.dve, 5 * j + 5)
        pool.wait_ge(s.mhalf, 1)
        for t in range(TURNS):
            if TURNS * j + t:
                pool.wait_ge(s.rstd, TURNS * j + t)
            c = slice(2 * NC * t, 2 * NC * (t + 1))
            nc.gpsimd.tensor_tensor(m.rstd[:, c], m.var[:, c], m.mhalf[:, c], ALU.pow).then_inc(s.rstd, 1)

    return dict(vector=vector, scalar=scalar, gpsimd=gpsimd)


def attention(nc, ctx, work, m, d, nth):
    wb = m.weight
    sb = lambda n, s: work.enter_context(nc.sbuf_tensor("att_" + n, s, F32))
    s = Names()
    (s.prep, s.xn, s.turned, s.xt, s.proj, s.qk, s.v, s.scores, s.centred, s.probs, s.turnedp, s.pt,
     s.heads, s.ready, s.turnedo, s.ot, s.out, s.free, s.zero) = signals(nc, ctx, "att", (
        "prep", "xn", "turned", "xt", "proj", "qk", "v", "scores", "centred", "probs", "turnedp", "pt",
        "heads", "ready", "turnedo", "ot", "out", "free", "zero"))
    ps, ident, H = m.ps, m.ident, m.H
    wqk = wb("wqk", [P, 2 * D])
    wv = wb("wv", [P, D + 2])
    wo = wb("wo", [P, D])
    L2 = range(2)
    xn = [sb(f"xn{k}", [P, NC, D + 1]) for k in L2]
    xt = [sb(f"xt{k}", [P, NC, P]) for k in L2]
    qk = [sb(f"qk{k}", [D, 2, NC, P]) for k in L2]
    v = [sb(f"v{k}", [P, NC, D + 1]) for k in L2]
    mask = [sb(f"mask{k}", [P, 2, NC]) for k in L2]
    top = [sb(f"top{k}", [P, NC]) for k in L2]
    sc = [sb(f"sc{k}", [P, NC, T]) for k in L2]
    pr = [sb(f"pr{k}", [P, NC, NC, P]) for k in L2]
    pt = [sb(f"pt{k}", [P, NC, NC, P]) for k in L2]
    rs = [sb(f"rs{k}", [P, 2, NC]) for k in L2]
    o = [sb(f"o{k}", [P, NC, D + 1]) for k in L2]
    ot = [sb(f"ot{k}", [P, NC, P]) for k in L2]
    bank = lambda k, b: ps[:, 4 * k + b, :]
    NPREP = 12

    def sync(sp):
        sp.wait_ge(s.zero, 3)
        for dst, src in ((wqk, d["att_wqk"]), (wv, d["att_wv"]), (wo, d["att_wo"])):
            m.n_weights += 1
            sp.dma_start(dst[0:D + 1], src).then_inc(m.weights, 16)

    def zero():
        for w in (wqk, wv, wo):
            nc.vector.memset(w[D:P], 0.0).then_inc(s.zero, 1)

    def prep():
        for k in L2:
            nc.vector.memset(xt[k][D:P], 0.0).then_inc(s.prep, 1)
            nc.vector.memset(ot[k][D:P], 0.0).then_inc(s.prep, 1)
            nc.vector.memset(pr[k][:], 0.0).then_inc(s.prep, 1)
            nc.vector.memset(v[k][:, :, D:D + 1], 1.0).then_inc(s.prep, 1)
            nc.vector.memset(xn[k][:, :, D:D + 1], 1.0).then_inc(s.prep, 1)
            nc.vector.memset(o[k][:, :, D:D + 1], 1.0).then_inc(s.prep, 1)
        nc.vector.memset(m.junk[:], 0.0).then_inc(s.free, 2)

    def normalise(dve, n, k):
        dve.wait_ge(s.free, n + 1)
        dve.wait_ge(m.ln.rstd, TURNS * (nth - 1) + 1 + m.turn)
        nc.vector.tensor_tensor(xn[k][:, :, 0:D], pair(m.XC, n).rearrange("p (c d) -> p c d", d=D),
                                bcast(pair(m.rstd, n, NC), D), ALU.mult).then_inc(s.xn, 1)

    def turn_x(pe, n, k):
        pe.wait_ge(s.xn, n + 1)
        for c in range(NC):
            mm = pe.transpose(bank(k, 0)[0:D + 1, P * c:P * (c + 1)], xn[k][:, c, :], ident[:])
        mm.then_inc(s.turned, 1)

    def copy_xt(act, n, k):
        act.wait_ge(s.turned, n + 1)
        nc.scalar.activation(xt[k][0:D + 1].rearrange("p c n -> p (c n)"), bank(k, 0)[0:D + 1, 0:NC * P], ACT.Copy).then_inc(s.xt, 1)

    def project(pe, n, k):
        pe.wait_ge(s.xt, n + 1)
        x = xt[k][:].rearrange("p c n -> p (c n)")
        for j in range(2):
            pe.matmul(bank(k, 1 + j)[0:D, 0:NC * P], wqk[:, D * j:D * (j + 1)], x, start=True, stop=True)
        for c in range(NC):
            mm = pe.matmul(bank(k, 3)[:, (D + 2) * c:(D + 2) * (c + 1)], xt[k][:, c, :], wv[:], start=True, stop=True)
        mm.then_inc(s.proj, 1)

    def copy_qk(act, n, k):
        act.wait_ge(s.proj, n + 1)
        nc.scalar.activation(qk[k][:].rearrange("p j c n -> p j (c n)"), ps[0:D, 4 * k + 1:4 * k + 3, 0:NC * P], ACT.Copy).then_inc(s.qk, 1)

    def copy_v(dve, n, k):
        src = bank(k, 3)[:, 0:(D + 2) * NC].rearrange("p (c e) -> p c e", c=NC)
        dve.wait_ge(s.proj, n + 1)
        nc.vector.tensor_copy(v[k][:, :, 0:D], src[:, :, 0:D])
        nc.vector.tensor_scalar(mask[k][:], src[:, :, D:D + 2].rearrange("p c j -> p j c"), 0.0, None, ALU.not_equal).then_inc(s.v, 1)

    def scores(pe, n, k):
        wait_apart(pe, m, (s.qk, n + 1))
        q = qk[k][:].rearrange("p j c (b t) -> p j c b t", b=2)
        for b in range(2):
            for c in range(NC):
                mm = pe.matmul(bank(k, c // 2)[D * b:D * (b + 1), 256 * (c % 2):256 * (c % 2) + T],
                               q[:, 0, c, b, :], q[:, 1, :, b, :], start=True, stop=True)
        mm.then_inc(s.scores, 1)

    def centre(dve, n, k):
        src = ps[:, 4 * k:4 * k + 2, :].rearrange("p g (c t) -> p (g c) t", t=256)[:, 0:NC, 0:T]
        dve.wait_ge(s.scores, n + 1)
        nc.vector.tensor_reduce(top[k][:], src, AX.X, ALU.max).then_inc(s.centred, 1)
        dve.wait_ge(s.centred, 2 * n + 1)
        nc.vector.tensor_tensor(sc[k][:], src, bcast(top[k][:], T), ALU.subtract).then_inc(s.centred, 1)

    def exponent(act, n, k):
        act.wait_ge(s.centred, 2 * n + 2)
        for b in range(2):
            h = slice(D * b, D * (b + 1))
            mm = nc.scalar.activation(pr[k][h, :, :, h].rearrange("p c e t -> p (c e) t"),
                                      sc[k][h].rearrange("p c (e t) -> p (c e) t", t=D), ACT.Exp, scale=D ** -0.5)
        mm.then_inc(s.probs, 1)

    def turn_probs(pe, n, k):
        pe.wait_ge(s.probs, n + 1)
        for c in range(NC):
            for e in range(NC):
                mm = pe.transpose(bank(k, c)[:, P * e:P * (e + 1)], pr[k][:, c, e, :], ident[:])
        mm.then_inc(s.turnedp, 1)

    def copy_pt(dve, n, k):
        dve.wait_ge(s.turnedp, n + 1)
        nc.vector.tensor_copy(pt[k][:].rearrange("p c e t -> p c (e t)"), ps[:, 4 * k:4 * k + 3, 0:NC * P]).then_inc(s.pt, 1)

    def heads(pe, n, k):
        pe.wait_ge(s.pt, n + 1)
        pe.wait_ge(s.v, n + 1)
        for c in range(NC):
            for e in range(NC):
                mm = pe.matmul(bank(k, 3)[:, (D + 1) * c:(D + 1) * (c + 1)], pt[k][:, c, e, :], v[k][:, e, :],
                               start=(e == 0), stop=(e == NC - 1), skip_group_check=True)
        mm.then_inc(s.heads, 1)

    def divide(dve, n, k):
        src = bank(k, 3)[:, 0:(D + 1) * NC].rearrange("p (c e) -> p c e", c=NC)
        dve.wait_ge(s.heads, n + 1)
        nc.vector.reciprocal(rs[k][:, 0, :], src[:, :, D])
        nc.vector.tensor_tensor(rs[k][:, 1, :], mask[k][:, 0, :], mask[k][:, 1, :], ALU.mult).then_inc(s.ready, 1)
        dve.wait_ge(s.ready, 3 * n + 1)
        nc.vector.tensor_tensor(rs[k][:, 0, :], rs[k][:, 0, :], rs[k][:, 1, :], ALU.mult).then_inc(s.ready, 1)
        dve.wait_ge(s.ready, 3 * n + 2)
        nc.vector.tensor_tensor(o[k][:, :, 0:D], src[:, :, 0:D], bcast(rs[k][:, 0, :], D), ALU.mult).then_inc(s.ready, 1)

    def turn_out(pe, n, k):
        pe.wait_ge(s.ready, 3 * n + 3)
        for c in range(NC):
            mm = pe.transpose(bank(k, 0)[0:D + 1, P * c:P * (c + 1)], o[k][:, c, :], ident[:])
        mm.then_inc(s.turnedo, 1)

    def copy_ot(act, n, k):
        act.wait_ge(s.turnedo, n + 1)
        nc.scalar.activation(ot[k][0:D + 1].rearrange("p c n -> p (c n)"), bank(k, 0)[0:D + 1, 0:NC * P], ACT.Copy).then_inc(s.ot, 1)

    def project_out(pe, n, k):
        pe.wait_ge(s.ot, n + 1)
        for c in range(NC):
            mm = pe.matmul(bank(k, 1)[:, D * c:D * (c + 1)], ot[k][:, c, :], wo[:], start=True, stop=True)
        mm.then_inc(s.out, 1)

    def add_out(dve, n, k):
        dve.wait_ge(s.out, n + 1)
        nc.vector.tensor_tensor(pair(H, n), pair(H, n), bank(k, 1)[:, 0:ROW], ALU.add).then_inc(s.free, 1)

    return dict(sync=sync, zero=zero,
                tensor=rolled(m, s, nth, NPREP, [turn_x, project, scores, turn_probs, heads, turn_out, project_out]),
                scalar=rolled(m, s, nth, NPREP, [copy_xt, copy_qk, exponent, copy_ot]),
                vector=rolled(m, s, nth, NPREP, [normalise, copy_v, centre, copy_pt, divide, add_out], prep))


def common(nc, ctx):
    sb = lambda n, s: ctx.enter_context(nc.sbuf_tensor(n, s, F32))
    m = Names()
    m.H, m.XC, m.SQ = sb("H", [P, NP * ROW]), sb("XC", [P, NP * ROW]), sb("SQ", [P, NP * ROW])
    N = NP * NC
    m.msum, m.mean, m.ssq, m.var, m.rstd, m.mhalf = (sb(n, [P, N]) for n in ("msum", "mean", "ssq", "var", "rstd", "mhalf"))
    m.junk, m.junk2, m.junk3 = (sb(n, [1, 1]) for n in ("junk", "junk2", "junk3"))
    arena = sb("weights", [P, WEIGHTS])
    used = [0]

    def weight(name, shape):
        assert len(shape) == 2 and used[0] + shape[1] <= WEIGHTS, name
        used[0] += shape[1]
        return arena[0:shape[0], used[0] - shape[1]:used[0]]

    m.weight = weight
    m.n_weights = 0
    m.weights = ctx.enter_context(nc.semaphore("token_weights"))
    m.ln = Names()
    (m.ln.dve, m.ln.square, m.ln.rstd, m.ln.mhalf, m.ln.twice) = signals(nc, ctx, "ln", (
        "dve", "square", "rstd", "mhalf", "twice"))
    return m


def slices(nc, ctx, work, m, d, nth):
    wb = m.weight
    sb = lambda n, s: work.enter_context(nc.sbuf_tensor("sl_" + n, s, F32))
    s = Names()
    (s.prep, s.wsl, s.wslc, s.wab, s.wabc, s.xn, s.turned, s.xt, s.logits, s.centred, s.expd, s.weights,
     s.z, s.zn, s.turnedw, s.wt, s.turnedz, s.zt, s.st, s.stc, s.qv, s.qvc, s.s, s.sd, s.probs, s.turnedp,
     s.pt, s.ow, s.own, s.out, s.free, s.xb, s.xbz, s.zero, s.wslz) = signals(nc, ctx, "sl", (
        "prep", "wsl", "wslc", "wab", "wabc", "xn", "turned", "xt", "logits", "centred", "expd", "weights",
        "z", "zn", "turnedw", "wt", "turnedz", "zt", "st", "stc", "qv", "qvc", "s", "sd", "probs",
        "turnedp", "pt", "ow", "own", "out", "free", "xb", "xbz", "zero", "wslz"))
    ps, ident, H = m.ps, m.ident, m.H
    HD, G, HP = 8, 64, 4
    wx = wb("wx", [D, HD * (D + 1)])
    ws = wb("ws", [D, G])
    rows = wb("rows", [D + 1, 2 * HD * G])
    wfx = wb("wfx", [P, HD * D])
    wq, wk, wv = wb("wq", [D, D]), wb("wk", [D, D]), wb("wv", [D, D])
    wout = wb("wout", [D, HD * D])
    bout = wb("bout", [P, D])
    wsl = wb("wsl", [P, HD * G])
    wqk = wb("wqk", [P, P])
    wvo = wb("wvo", [P, HP * D])
    L2 = range(2)
    xn = [sb(f"xn{k}", [P, NC, D + 1]) for k in L2]
    xt = [sb(f"xt{k}", [P, NC, P]) for k in L2]
    xb = [sb(f"xb{k}", [P, NC, 2, D + 1]) for k in L2]
    top = [sb(f"top{k}", [P, NC * HD]) for k in L2]
    rec = [sb(f"rec{k}", [P, 2, NC * HD]) for k in L2]
    w = [sb(f"w{k}", [P, NC, HD * G]) for k in L2]
    wt = [sb(f"wt{k}", [P, NC, HP, P]) for k in L2]
    nz = [sb(f"nz{k}", [P, 2 * HP]) for k in L2]
    zn = [sb(f"zn{k}", [P, 2, HP, D + 1]) for k in L2]
    zt = [sb(f"zt{k}", [P, 2, HP, P]) for k in L2]
    st = [sb(f"st{k}", [P, HP, 2, G]) for k in L2]
    qt = [sb(f"qt{k}", [P, HP, 2, G]) for k in L2]
    vo = [sb(f"vo{k}", [P, HP, 2, D + 1]) for k in L2]
    tops = [sb(f"tops{k}", [P, 8]) for k in L2]
    ss = [sb(f"ss{k}", [P, HP, 2, G]) for k in L2]
    pr = [sb(f"pr{k}", [P, HP, 2, P]) for k in L2]
    pt = [sb(f"pt{k}", [P, HP, 2, P]) for k in L2]
    ro = [sb(f"ro{k}", [P, 8]) for k in L2]
    ow = [sb(f"ow{k}", [P, HP, 2, D]) for k in L2]
    bank = lambda k, b: ps[:, 4 * k + b, :]
    NPREP = 6 + 4 + 4 + 5

    def sync(sp):
        sp.wait_ge(s.zero, 1)
        for dst, src in ((wx, "wx"), (ws, "ws"), (wfx[0:D + 1], "wfx"), (wq, "wqT"), (wk, "wkT"), (wv, "wvT"), (wout, "wout")):
            m.n_weights += 1
            sp.dma_start(dst[:], d["ffn_" + src]).then_inc(m.weights, 16)
        m.n_weights += 2
        sp.dma_start(rows[:], d["ffn_rows"].broadcast_to([D + 1, 2 * HD * G])).then_inc(m.weights, 16)
        sp.dma_start(bout[:], d["ffn_bout"].broadcast_to([P, D])).then_inc(m.weights, 16)

    def zero():
        nc.vector.memset(wfx[D:P], 0.0).then_inc(s.zero, 1)

    def weights_tensor(pe):
        pe.wait_ge(m.weights, 16 * m.n_weights)
        for h in range(HD):
            mm = pe.matmul(ps[0:D + 1, 0, G * h:G * (h + 1)], wx[:, (D + 1) * h:(D + 1) * (h + 1)], ws[:], start=True, stop=True)
        mm.then_inc(s.wsl, 1)
        for j in range(2):
            pe.matmul(ps[D * j:D * (j + 1), 1, 0:D], wq[:], wk[:], start=True, stop=True)
            for hp in range(HP):
                c = D * (2 * hp + j)
                mm = pe.matmul(ps[D * j:D * (j + 1), 2, D * hp:D * (hp + 1)], wv[:], wout[:, c:c + D], start=True, stop=True)
        mm.then_inc(s.wab, 1)
        pe.wait_ge(s.wabc, 3)
        pe.wait_ge(s.wslc, 6)

    def weights_vector():
        dve = nc.vector
        dve.memset(wsl[D:P], 0.0).then_inc(s.wslz, 1)
        for k in L2:
            dve.memset(xt[k][D:P], 0.0).then_inc(s.prep, 1)
            dve.memset(zt[k][D:P], 0.0).then_inc(s.prep, 1)
            dve.memset(xn[k][:, :, D:D + 1], 1.0).then_inc(s.prep, 1)
            dve.memset(vo[k][:, :, :, D:D + 1], 1.0).then_inc(s.prep, 1)
            dve.memset(pr[k][:], 0.0).then_inc(s.prep, 1)
        dve.memset(wqk[:], 0.0).then_inc(s.xbz, 1)
        for k in L2:
            dve.memset(xb[k][:], 0.0).then_inc(s.xbz, 1)
            dve.wait_ge(s.xbz, k + 2)
            for b in range(2):
                dve.memset(xb[k][D * b:D * (b + 1), :, b, D:D + 1], 1.0).then_inc(s.prep, 1)
        dve.memset(m.junk[:], 0.0).then_inc(s.free, 2)
        dve.wait_ge(m.weights, 16 * m.n_weights)
        t = rows[:, HD * G:]
        dve.tensor_scalar(t, t, 0.1, 5.0, ALU.max, ALU.min).then_inc(s.wslc, 1)
        dve.wait_ge(s.wslc, 1)
        dve.reciprocal(t, t).then_inc(s.wslc, 1)
        dve.wait_ge(s.wsl, 1)
        dve.wait_ge(s.wslz, 1)
        dve.tensor_copy(wsl[0:D + 1], ps[0:D + 1, 0, :]).then_inc(s.wslc, 1)
        dve.wait_ge(s.wslc, 3)
        dve.tensor_tensor(wsl[D:D + 1], wsl[D:D + 1], rows[D:D + 1, 0:HD * G], ALU.add).then_inc(s.wslc, 1)
        dve.wait_ge(s.wslc, 4)
        dve.tensor_tensor(wsl[0:D + 1], wsl[0:D + 1], t, ALU.mult).then_inc(s.wslc, 2)
        dve.wait_ge(s.wab, 1)
        for b in range(2):
            r = slice(D * b, D * (b + 1))
            dve.tensor_copy(wqk[r, r], ps[r, 1, 0:D]).then_inc(s.wabc, 1)
        dve.tensor_copy(wvo[:], ps[:, 2, 0:HP * D]).then_inc(s.wabc, 1)
        dve.memset(m.junk[:], 0.0).then_inc(s.prep, 5)

    def normalise(dve, n, k):
        dve.wait_ge(s.free, n + 1)
        dve.wait_ge(m.ln.rstd, TURNS * (nth - 1) + 1 + m.turn)
        nc.vector.tensor_tensor(xn[k][:, :, 0:D], pair(m.XC, n).rearrange("p (c d) -> p c d", d=D),
                                bcast(pair(m.rstd, n, NC), D), ALU.mult).then_inc(s.xn, 1)

    def turn_x(pe, n, k):
        pe.wait_ge(s.xn, n + 1)
        for c in range(NC):
            mm = pe.transpose(bank(k, 0)[0:D + 1, P * c:P * (c + 1)], xn[k][:, c, :], ident[:])
        mm.then_inc(s.turned, 1)

    def copy_xt(act, n, k):
        act.wait_ge(s.turned, n + 1)
        nc.scalar.activation(xt[k][0:D + 1].rearrange("p c n -> p (c n)"), bank(k, 0)[0:D + 1, 0:NC * P], ACT.Copy).then_inc(s.xt, 1)

    def copy_xb(act, n, k):
        act.wait_ge(s.xn, n + 1)
        for b in range(2):
            r = slice(D * b, D * (b + 1))
            a = nc.scalar.activation(xb[k][r, :, b, 0:D], xn[k][r, :, 0:D], ACT.Copy)
        a.then_inc(s.xb, 1)

    def logits(pe, n, k):
        pe.wait_ge(s.xt, n + 1)
        for c in range(NC):
            mm = pe.matmul(bank(k, 1 + c), xt[k][:, c, :], wsl[:], start=True, stop=True)
        mm.then_inc(s.logits, 1)

    def centre(dve, n, k):
        src = ps[:, 4 * k + 1:4 * k + 4, :].rearrange("p c (h g) -> p (c h) g", g=G)
        dst = w[k][:].rearrange("p c (h g) -> p (c h) g", g=G)
        dve.wait_ge(s.logits, n + 1)
        nc.vector.tensor_reduce(top[k][:], src, AX.X, ALU.max).then_inc(s.centred, 1)
        dve.wait_ge(s.centred, 2 * n + 1)
        nc.vector.tensor_tensor(dst, src, bcast(top[k][:], G), ALU.subtract).then_inc(s.centred, 1)

    def exponent(act, n, k):
        act.wait_ge(s.centred, 2 * n + 2)
        nc.scalar.activation(w[k][:], w[k][:], ACT.Exp).then_inc(s.expd, 1)

    def weigh(dve, n, k):
        e = w[k][:].rearrange("p c (h g) -> p (c h) g", g=G)
        dve.wait_ge(s.expd, n + 1)
        nc.vector.tensor_reduce(rec[k][:, 0, :], e, AX.X, ALU.add).then_inc(s.weights, 1)
        dve.wait_ge(s.weights, 3 * n + 1)
        nc.vector.reciprocal(rec[k][:, 1, :], rec[k][:, 0, :]).then_inc(s.weights, 1)
        dve.wait_ge(s.weights, 3 * n + 2)
        nc.vector.tensor_tensor(e, e, bcast(rec[k][:, 1, :], G), ALU.mult).then_inc(s.weights, 1)

    def gather(pe, n, k):
        pe.wait_ge(s.weights, 3 * n + 3)
        pe.wait_ge(s.xb, n + 1)
        for hp in range(HP):
            q = 2 * (D + 1) * (hp % 2)
            for c in range(NC):
                mm = pe.matmul(bank(k, hp // 2)[:, q:q + 2 * (D + 1)], w[k][:, c, P * hp:P * (hp + 1)],
                               xb[k][:, c].rearrange("p b e -> p (b e)"), start=(c == 0), stop=(c == NC - 1), skip_group_check=True)
        mm.then_inc(s.z, 1)

    def turn_weights(pe, n, k):
        for c in range(NC):
            if c == 2:
                pe.wait_ge(s.wt, 2 * n + 1)
            for hp in range(HP):
                mm = pe.transpose(bank(k, 2 + c % 2)[:, P * hp:P * (hp + 1)], w[k][:, c, P * hp:P * (hp + 1)], ident[:])
            if c:
                mm.then_inc(s.turnedw, 1)

    def copy_wt(act, n, k):
        act.wait_ge(s.turnedw, 2 * n + 1)
        nc.scalar.activation(wt[k][:, 0:2].rearrange("p c h n -> p c (h n)"), ps[:, 4 * k + 2:4 * k + 4, :], ACT.Copy).then_inc(s.wt, 1)
        act.wait_ge(s.turnedw, 2 * n + 2)
        nc.scalar.activation(wt[k][:, 2].rearrange("p h n -> p (h n)"), bank(k, 2), ACT.Copy).then_inc(s.wt, 1)

    def slice_means(dve, n, k):
        z = ps[:, 4 * k:4 * k + 2, 0:(D + 1) * HP].rearrange("p a (h b e) -> p a h b e", h=2, b=2)
        nzv = nz[k][:].rearrange("p (a h b) -> p a h b", a=2, h=2)
        dve.wait_ge(s.z, n + 1)
        nc.vector.tensor_scalar(nzv, z[:, :, :, :, D], 1e-5, None, ALU.add).then_inc(s.zn, 1)
        dve.wait_ge(s.zn, 4 * n + 1)
        nc.vector.reciprocal(nz[k][:], nz[k][:]).then_inc(s.zn, 1)
        dve.wait_ge(s.zn, 4 * n + 2)
        for a in range(2):
            nc.vector.tensor_tensor(zn[k][:, :, 2 * a:2 * a + 2, :].rearrange("p b h e -> p h b e"), z[:, a],
                                    nzv[:, a].unsqueeze(3).broadcast_to([P, 2, 2, D + 1]), ALU.mult).then_inc(s.zn, 1)

    def turn_z(pe, n, k):
        pe.wait_ge(s.zn, 4 * n + 4)
        for b in range(2):
            for hp in range(HP):
                mm = pe.transpose(bank(k, b)[0:D + 1, P * hp:P * (hp + 1)], zn[k][:, b, hp, :], ident[:])
        mm.then_inc(s.turnedz, 1)

    def copy_zt(dve, n, k):
        dve.wait_ge(s.turnedz, n + 1)
        nc.vector.tensor_copy(zt[k][0:D + 1].rearrange("p b h n -> p b (h n)"), ps[0:D + 1, 4 * k:4 * k + 2, :]).then_inc(s.zt, 1)

    def slice_tokens(pe, n, k):
        pe.wait_ge(s.wt, 2 * n + 2)
        pe.wait_ge(s.zt, n + 1)
        for hp in range(HP):
            for j in range(2):
                c = D * (2 * hp + j)
                mm = pe.matmul(bank(k, 3)[D * j:D * (j + 1), P * hp:P * (hp + 1)], wfx[:, c:c + D],
                               zt[k][:, :, hp, G * j:G * (j + 1)], start=True, stop=True)
        mm.then_inc(s.st, 1)

    def copy_st(act, n, k):
        act.wait_ge(s.st, n + 1)
        nc.scalar.activation(st[k][:].rearrange("p h b g -> p (h b g)"), bank(k, 3), ACT.Copy).then_inc(s.stc, 1)

    def slice_qv(pe, n, k):
        pe.wait_ge(s.stc, n + 1)
        pe.matmul(bank(k, 2), wqk[:], st[k][:].rearrange("p h b g -> p (h b g)"), start=True, stop=True)
        for j in range(2):
            r = slice(D * j, D * (j + 1))
            for hp in range(HP):
                for b in range(2):
                    c = D * (2 * hp + b)
                    mm = pe.matmul(bank(k, 0)[r, c:c + D], st[k][r, hp, b, :], wvo[r, D * hp:D * (hp + 1)], start=True, stop=True)
        mm.then_inc(s.qv, 1)

    def copy_qv(act, n, k):
        act.wait_ge(s.qv, n + 1)
        nc.scalar.activation(qt[k][:].rearrange("p h b g -> p (h b g)"), bank(k, 2), ACT.Copy)
        nc.scalar.activation(vo[k][:].rearrange("p h b e -> p (h b) e")[:, :, 0:D], bank(k, 0).rearrange("p (m e) -> p m e", e=D), ACT.Copy).then_inc(s.qvc, 1)

    def slice_scores(pe, n, k):
        wait_apart(pe, m, (s.qvc, n + 1))
        for j in range(2):
            r = slice(D * j, D * (j + 1))
            for hp in range(HP):
                for b in range(2):
                    c = D * (2 * hp + b)
                    mm = pe.matmul(bank(k, 1)[r, c:c + D], qt[k][r, hp, b, :], st[k][r, hp, b, :], start=True, stop=True)
        mm.then_inc(s.s, 1)

    def centre_slices(dve, n, k):
        src = bank(k, 1).rearrange("p (m g) -> p m g", g=G)
        dve.wait_ge(s.s, n + 1)
        nc.vector.tensor_reduce(tops[k][:], src, AX.X, ALU.max).then_inc(s.sd, 1)
        dve.wait_ge(s.sd, 2 * n + 1)
        nc.vector.tensor_tensor(ss[k][:].rearrange("p h b g -> p (h b) g"), src, bcast(tops[k][:], G), ALU.subtract).then_inc(s.sd, 1)

    def exponent_slices(act, n, k):
        act.wait_ge(s.sd, 2 * n + 2)
        for j in range(2):
            r = slice(D * j, D * (j + 1))
            a = nc.scalar.activation(pr[k][r, :, :, r].rearrange("p h b g -> p (h b) g"),
                                     ss[k][r].rearrange("p h b g -> p (h b) g"), ACT.Exp, scale=D ** -0.5)
        a.then_inc(s.probs, 1)

    def turn_probs(pe, n, k):
        pe.wait_ge(s.probs, n + 1)
        for hp in range(HP):
            for b in range(2):
                q = 2 * hp + b
                mm = pe.transpose(bank(k, 2 + q // 4)[:, P * (q % 4):P * (q % 4 + 1)], pr[k][:, hp, b, :], ident[:])
        mm.then_inc(s.turnedp, 1)

    def copy_pt(act, n, k):
        act.wait_ge(s.turnedp, n + 1)
        nc.scalar.activation(pt[k][:].rearrange("p (a h) b n -> p a (h b n)", a=2), ps[:, 4 * k + 2:4 * k + 4, :], ACT.Copy).then_inc(s.pt, 1)

    def slice_out(pe, n, k):
        pe.wait_ge(s.pt, n + 1)
        for hp in range(HP):
            for b in range(2):
                q = 2 * hp + b
                mm = pe.matmul(bank(k, q // 4)[:, (D + 1) * (q % 4):(D + 1) * (q % 4 + 1)], pt[k][:, hp, b, :], vo[k][:, hp, b, :], start=True, stop=True)
        mm.then_inc(s.ow, 1)

    def divide(dve, n, k):
        src = ps[:, 4 * k:4 * k + 2, 0:(D + 1) * 4].rearrange("p a (m e) -> p a m e", m=4)
        rv = ro[k][:].rearrange("p (a m) -> p a m", a=2)
        dve.wait_ge(s.ow, n + 1)
        nc.vector.reciprocal(rv, src[:, :, :, D]).then_inc(s.own, 1)
        dve.wait_ge(s.own, 3 * n + 1)
        dst = ow[k][:].rearrange("p (a h) b e -> p a (h b) e", a=2)
        for a in range(2):
            nc.vector.tensor_tensor(dst[:, a], src[:, a, :, 0:D], bcast(rv[:, a, :], D), ALU.mult).then_inc(s.own, 1)

    def spread(pe, n, k):
        pe.wait_ge(s.own, 3 * n + 3)
        for b in range(2):
            for c in range(NC):
                for hp in range(HP):
                    mm = pe.matmul(bank(k, 2)[D * b:D * (b + 1), D * c:D * (c + 1)], wt[k][:, c, hp, D * b:D * (b + 1)], ow[k][:, hp, b, :],
                                   start=(hp == 0), stop=(hp == HP - 1), skip_group_check=True)
        mm.then_inc(s.out, 1)

    def add_out(dve, n, k):
        h3 = pair(H, n).rearrange("p (c d) -> p c d", d=D)
        dve.wait_ge(s.out, n + 1)
        nc.vector.tensor_tensor(xn[k][:, :, 0:D], bank(k, 2)[:, 0:ROW].rearrange("p (c d) -> p c d", d=D),
                                bout[:].unsqueeze(1).broadcast_to([P, NC, D]), ALU.add).then_inc(s.outb, 1)
        dve.wait_ge(s.outb, n + 1)
        nc.vector.tensor_tensor(h3, h3, xn[k][:, :, 0:D], ALU.add).then_inc(s.free, 1)

    s.outb = ctx.enter_context(nc.semaphore("sl_outb"))
    r = lambda steps, before=lambda: None: rolled(m, s, nth, NPREP, steps, before)
    loop = r([turn_x, logits, gather, turn_weights, turn_z, slice_tokens, slice_qv, slice_scores, turn_probs, slice_out, spread])

    def tensor(pe):
        weights_tensor(pe)
        loop(pe)

    return dict(zero=zero, sync=sync, tensor=tensor,
                scalar=r([copy_xb, copy_xt, exponent, copy_wt, copy_st, copy_qv, exponent_slices, copy_pt]),
                vector=r([normalise, centre, weigh, slice_means, copy_zt, centre_slices, divide, add_out], weights_vector))


class Link:

    def __init__(self, eng, sem, base):
        self.eng, self.sem, self.base, self.n = eng, sem, base, 0

    def __call__(self, instruction):
        self.n += 1
        instruction.then_inc(self.sem, 1)
        self.eng.wait_ge(self.sem, self.base + self.n)


def experts(nc, ctx, work, m, d, nth):
    wb = m.weight
    sb = lambda n, s, t=F32: work.enter_context(nc.sbuf_tensor("moe_" + n, s, t))
    s = Names()
    (s.prep, s.xn, s.turned, s.xt, s.xta, s.router, s.best, s.free, s.gates, s.exps, s.wp, s.turnedw, s.wt,
     s.zero, s.hid, s.gelu, s.outs, s.bias, s.biased, s.done, s.free2, s.xtz) = signals(nc, ctx, "moe", (
        "prep", "xn", "turned", "xt", "xta", "router", "best", "free", "gates", "exps", "wp", "turnedw",
        "wt", "zero", "hid", "gelu", "outs", "bias", "biased", "done", "free2", "xtz"))
    ps, ident, H = m.ps, m.ident, m.H
    E, HID = 8, 128
    N = NP * NC
    gb = wb("gb", [D, 2])
    wr = wb("wr", [D + 1, E])
    w1 = wb("w1", [P, E * HID])
    w2 = wb("w2", [HID, E * D])
    b2 = wb("b2", [32 * NC, ROW])
    iota = wb("iota", [P, E])
    L2 = range(2)
    xn = [sb(f"xn{k}", [P, NC, D + 1]) for k in L2]
    xt = [sb(f"xt{k}", [D + 1, NC, P]) for k in L2]
    XTA = sb("XTA", [P, NP * NC * P])
    best = [sb(f"best{k}", [P, NC, E]) for k in L2]
    two = [sb(f"two{k}", [P, NC, 2]) for k in L2]
    index = [sb(f"index{k}", [P, NC, E], mybir.dt.uint32) for k in L2]
    lg = [sb(f"lg{k}", [P, NC, E]) for k in L2]
    TOP = sb("TOP", [P, N * 2])
    IX = sb("IX", [P, N * 2])
    ga = sb("ga", [P, 4, N])
    WF = sb("WF", [P, N * E])
    WG = sb("WG", [P, N * E])
    wp = [sb(f"wp{k}", [P, NC, 32]) for k in L2]
    wt = [sb(f"wt{k}", [32 * NC, P]) for k in L2]
    ht = [sb(f"ht{q}", [HID, NC * P]) for q in L2]
    prod = [sb(f"prod{k}", [P, NC, E, D]) for k in L2]
    red = [sb(f"red{k}", [P, NC, D]) for k in L2]
    hb = lambda e: ps[:, 7 - e % 2, :]
    gate_bank = ps[:, 6, :]
    NPREP = 6

    def sync(sp):
        sp.wait_ge(s.zero, 2)
        for dst, src in ((gb, "moe_gb"), (wr, "moe_wr"), (w1[0:D + 1], "moe_w1"), (w2, "moe_w2")):
            m.n_weights += 1
            sp.dma_start(dst[:], d[src]).then_inc(m.weights, 16)
        for c in range(NC):
            m.n_weights += 1
            sp.dma_start(b2[32 * c:32 * c + E, D * c:D * (c + 1)], d["moe_b2"]).then_inc(m.weights, 16)
        m.n_weights += 1
        sp.dma_start(iota[:], d["iota8"].broadcast_to([P, E])).then_inc(m.weights, 16)

    def zero():
        nc.vector.memset(b2[:], 0.0).then_inc(s.zero, 1)
        nc.vector.memset(w1[D:P], 0.0).then_inc(s.zero, 1)

    def prep():
        for k in L2:
            nc.vector.memset(xn[k][:, :, D:D + 1], 1.0).then_inc(s.prep, 1)
            nc.vector.memset(xt[k][D:D + 1], 1.0).then_inc(s.prep, 1)
            nc.vector.memset(wp[k][:], 0.0).then_inc(s.prep, 1)
        nc.vector.memset(m.junk[:], 0.0).then_inc(s.free, 2)
        nc.vector.memset(m.junk2[:], 0.0).then_inc(s.free2, 2)
        nc.vector.memset(m.junk3[:], 0.0).then_inc(s.outs, 2)

    def normalise(dve, n, k):
        dve.wait_ge(s.free, n + 1)
        dve.wait_ge(m.ln.rstd, TURNS * (nth - 1) + 1 + m.turn)
        nc.vector.tensor_tensor(xn[k][:, :, 0:D], pair(m.XC, n).rearrange("p (c d) -> p c d", d=D),
                                bcast(pair(m.rstd, n, NC), D), ALU.mult).then_inc(s.xn, 1)

    def turn_x(pe, n, k):
        pe.wait_ge(s.xn, n + 1)
        for c in range(NC):
            mm = pe.transpose(ps[0:D + 1, k, P * c:P * (c + 1)], xn[k][:, c, :], ident[:])
        mm.then_inc(s.turned, 1)

    def copy_xt(act, n, k):
        act.wait_ge(s.turned, n + 1)
        act.wait_ge(s.free, n + 1)
        nc.scalar.activation(xt[k][0:D].rearrange("p c n -> p (c n)"), ps[0:D, k, 0:NC * P], ACT.Identity,
                             bias=gb[:, 1:2], scale=gb[:, 0:1]).then_inc(s.xt, 1)

    def zero_xt():
        nc.gpsimd.wait_ge(m.ln.rstd, TURNS * nth)
        nc.gpsimd.memset(XTA[D:P], 0.0).then_inc(s.xtz, 1)

    def keep_xt(pool, n, k):
        pool.wait_ge(s.xtz, 1)
        pool.wait_ge(s.xt, n + 1)
        nc.gpsimd.tensor_copy(pair(XTA[0:D + 1], n, NC * P), xt[k][:].rearrange("p c n -> p (c n)")).then_inc(s.xta, 1)

    def router(pe, n, k):
        pe.wait_ge(s.xt, n + 1)
        for c in range(NC):
            mm = pe.matmul(ps[:, 2 + k, E * c:E * (c + 1)], xt[k][:, c, :], wr[:], start=True, stop=True)
        mm.then_inc(s.router, 1)

    def pick(dve, n, k):
        dve.wait_ge(s.router, n + 1)
        nc.vector.tensor_copy(lg[k][:].rearrange("p c e -> p (c e)"), ps[:, 2 + k, 0:NC * E]).then_inc(s.best, 1)
        for c in range(NC):
            nc.vector.max(best[k][:, c, :], ps[:, 2 + k, E * c:E * (c + 1)]).then_inc(s.best, 1)
        dve.wait_ge(s.best, 8 * n + 4)
        nc.vector.tensor_copy(two[k][:], best[k][:, :, 0:2]).then_inc(s.best, 1)
        for c in range(NC):
            nc.vector.max_index(index[k][:, c, :], best[k][:, c, :], lg[k][:, c, :]).then_inc(s.best, 1)
        dve.wait_ge(s.best, 8 * n + 8)
        nc.vector.tensor_copy(pair(TOP, n, 2 * NC), two[k][:].rearrange("p c e -> p (c e)"))
        dve.wait_ge(s.xta, n + 1)
        nc.vector.tensor_copy(pair(IX, n, 2 * NC).rearrange("p (c e) -> p c e", e=2), index[k][:, :, 0:2]).then_inc(s.free, 1)

    t1, t2 = (TOP[:].rearrange("p (n e) -> p n e", e=2)[:, :, j] for j in range(2))
    i1, i2 = (IX[:].rearrange("p (n e) -> p n e", e=2)[:, :, j] for j in range(2))
    wf3, wg3 = (t[:].rearrange("p (n e) -> p n e", e=E) for t in (WF, WG))

    def gates(dve):
        dve.wait_ge(s.free, NP + 2)
        link = Link(dve, s.gates, 0)
        io = iota[:].unsqueeze(1).broadcast_to([P, N, E])
        link(nc.vector.tensor_tensor(ga[:, 0, :], t2, t1, ALU.subtract))
        dve.wait_ge(s.exps, 1)
        link(nc.vector.tensor_scalar(ga[:, 2, :], ga[:, 1, :], 1.0, None, ALU.add))
        link(nc.vector.reciprocal(ga[:, 2, :], ga[:, 2, :]))
        link(nc.vector.tensor_tensor(ga[:, 3, :], ga[:, 1, :], ga[:, 2, :], ALU.mult))
        link(nc.vector.tensor_tensor(wf3, io, bcast(i1, E), ALU.is_equal))
        link(nc.vector.tensor_tensor(wf3, wf3, bcast(ga[:, 2, :], E), ALU.mult))
        link(nc.vector.tensor_tensor(wg3, io, bcast(i2, E), ALU.is_equal))
        link(nc.vector.tensor_tensor(wg3, wg3, bcast(ga[:, 3, :], E), ALU.mult))
        link(nc.vector.tensor_tensor(WF[:], WF[:], WG[:], ALU.add))

    def exps(act):
        act.wait_ge(s.gates, 1)
        nc.scalar.activation(ga[:, 1, :], ga[:, 0, :], ACT.Exp).then_inc(s.exps, 1)

    def stage_gates(dve, n, k):
        dve.wait_ge(s.free2, n + 1)
        nc.vector.tensor_copy(wp[k][:, :, 0:E], pair(WF, n, NC * E).rearrange("p (c e) -> p c e", e=E)).then_inc(s.wp, 1)

    def turn_gates(pe, n, k):
        wait_apart(pe, m, (s.wp, n + 1))
        pe.transpose(gate_bank[0:32 * NC, 0:P], wp[k][:].rearrange("p c e -> p (c e)"), ident[:]).then_inc(s.turnedw, 1)

    def copy_gates(dve, n, k):
        dve.wait_ge(s.turnedw, n + 1)
        nc.vector.tensor_copy(wt[k][:], gate_bank[0:32 * NC, 0:P]).then_inc(s.wt, 1)

    def biases(pe, n, k):
        pe.wait_ge(s.wt, n + 1)
        pe.matmul(gate_bank[:, 0:ROW], wt[k][:], b2[:], start=True, stop=True).then_inc(s.bias, 1)

    def add_biases(dve, n, k):
        dve.wait_ge(s.bias, n + 1)
        nc.vector.tensor_tensor(pair(H, n), pair(H, n), gate_bank[:, 0:ROW], ALU.add).then_inc(s.biased, 1)

    def hidden(pe, n, e):
        if e == 1:
            pe.wait_ge(s.biased, n + 1)
        pe.matmul(hb(e)[:, 0:NC * P], w1[:, HID * e:HID * (e + 1)], pair(XTA, n, NC * P), start=True, stop=True).then_inc(s.hid, 1)

    def activate(act, n, e):
        act.wait_ge(s.hid, 8 * n + e + 1)
        act.wait_ge(s.outs, 8 * n + e + 1)
        nc.scalar.activation(ht[e % 2][:], hb(e)[:, 0:NC * P], ACT.Gelu).then_inc(s.gelu, 1)

    def outputs(pe, n, k, e):
        if e == 0:
            pe.wait_ge(s.free2, n + 1)
        pe.wait_ge(s.gelu, 8 * n + e + 1)
        for c in range(NC):
            mm = pe.matmul(ps[:, 3 * k + c, D * e:D * (e + 1)], ht[e % 2][:, P * c:P * (c + 1)], w2[:, D * e:D * (e + 1)], start=True, stop=True)
        mm.then_inc(s.outs, 1)

    def combine(dve, n, k):
        h = pair(H, n)
        dve.wait_ge(s.outs, 8 * n + 8 + 2)
        link = Link(dve, s.done, 2 * n)
        for c in range(NC):
            ins = nc.vector.tensor_tensor(prod[k][:, c], ps[:, 3 * k + c, :].rearrange("p (e d) -> p e d", d=D), bcast(wp[k][:, c, 0:E], D), ALU.mult)
        link(ins)
        link(nc.vector.tensor_reduce(red[k][:], prod[k][:].rearrange("p c e d -> p c d e"), AX.X, ALU.add))
        dve.wait_ge(s.biased, n + 1)
        nc.vector.tensor_tensor(h, h, red[k][:].rearrange("p c d -> p (c d)"), ALU.add).then_inc(s.free2, 1)

    r = lambda steps, before=lambda: None: rolled(m, s, nth, NPREP, steps, before)

    def tensor(pe):
        r([turn_x, router])(pe)
        pe.wait_ge(s.xta, NP)
        pe.wait_ge(s.gates, 9)
        with pe.Fori(0, NP // 2) as it:
            for k in L2:
                n = 2 * it + k
                turn_gates(pe, n, k)
                hidden(pe, n, 0)
                biases(pe, n, k)
                hidden(pe, n, 1)
                for e in range(E):
                    outputs(pe, n, k, e)
                    if e + 2 < E:
                        hidden(pe, n, e + 2)

    def scalar(act):
        r([copy_xt])(act)
        exps(act)
        with act.Fori(0, NP) as n:
            for e in range(E):
                activate(act, n, e)

    def vector(dve):
        r([normalise, pick], prep)(dve)
        gates(dve)
        for k in L2:
            stage_gates(dve, k, k)
        copy_gates(dve, 0, 0)
        add_biases(dve, 0, 0)
        with dve.Fori(0, NP // 2 - 1) as it:
            for k in L2:
                n = 2 * it + k
                copy_gates(dve, n + 1, 1 - k)
                add_biases(dve, n + 1, 1 - k)
                combine(dve, n, k)
                stage_gates(dve, n + 2, k)
        copy_gates(dve, NP - 1, 1)
        add_biases(dve, NP - 1, 1)
        for k in L2:
            combine(dve, NP - 2 + k, k)

    return dict(sync=sync, tensor=tensor, scalar=scalar, vector=vector, gpsimd=r([keep_xt], zero_xt), zero=zero)


def second_norm(nc, m, s):
    def vector(dve):
        dve.wait_ge(m.ln.rstd, TURNS * s)
        nc.vector.tensor_tensor(m.SQ[:].rearrange("p (n d) -> p n d", d=D), m.XC[:].rearrange("p (n d) -> p n d", d=D),
                                bcast(m.rstd[:], D), ALU.mult).then_inc(m.ln.twice, 1)
        dve.wait_ge(m.ln.twice, 1)
    return dict(vector=vector)


def recurrence(nc, ctx, work, m, d, nth):
    wb = m.weight
    sb = lambda n, s: work.enter_context(nc.sbuf_tensor("rw_" + n, s, F32))
    s = Names()
    (s.prep, s.xn, s.turned, s.xf, s.mixed, s.proj, s.projc, s.projd, s.second, s.cum, s.decays, s.sq,
     s.norms, s.rkk, s.keys, s.mats, s.masked, s.tokmaj, s.out, s.on, s.sq2, s.gr, s.turnedo, s.ot, s.y,
     s.free, s.gated) = signals(nc, ctx, "rw", (
        "prep", "xn", "turned", "xf", "mixed", "proj", "projc", "projd", "second", "cum", "decays", "sq",
        "norms", "rkk", "keys", "mats", "masked", "tokmaj", "out", "on", "sq2", "gr", "turnedo", "ot", "y",
        "free", "gated"))
    wtok, inv_pe, inv_dve, chunk_pe, chunk_dve = ([ctx.enter_context(nc.semaphore(f"rw_{n}{k}")) for k in range(2)]
                                                  for n in ("wtok", "inv_pe", "inv_dve", "chunk_pe", "chunk_dve"))
    ps, ident, H = m.ps, m.ident, m.H
    L2 = range(2)
    CH = NC
    DECAY = -0.6065306597126334
    GN_EPS = D * 1e-5
    block = {n: wb(n, [P, P]) for n in ("W_r", "W_k", "A_w", "A_a", "B_w", "B_a")}
    wv = wb("wv", [P, D])
    ag = wb("ag", [P, 2 * D])
    bg = wb("bg", [P, D])
    wo = wb("wo", [D, D])
    cols = wb("cols", [P, 12])
    rowsb = wb("rows", [P, 4 * D])
    tri = wb("tri", [D, P])
    maskT = wb("maskT", [P, P])
    levT = wb("levT", [P, 5 * D])
    lev0 = wb("lev0", [P, 2 * D])
    ones = wb("ones", [P, P])
    eye = wb("eye", [P, D])
    xn = [sb(f"xn{k}", [P, CH, D + 1]) for k in L2]
    xf = [sb(f"xf{k}", [P, 1 + T]) for k in L2]
    dl = [sb(f"dl{k}", [P, T]) for k in L2]
    xm = [sb(f"xm{k}", [P, 6, T]) for k in L2]
    R = [sb(f"R{k}", [P, CH, D]) for k in L2]
    K = [sb(f"K{k}", [P, CH, D]) for k in L2]
    za = [sb(f"za{k}", [P, 2, T]) for k in L2]
    gh = [sb(f"gh{k}", [P, 2, T]) for k in L2]
    V = [sb(f"V{k}", [P, CH, D]) for k in L2]
    a = [sb(f"a{k}", [P, CH, D]) for k in L2]
    wt = [sb(f"wt{k}", [D, CH, P]) for k in L2]
    ce = [sb(f"ce{k}", [P, CH, 2, D]) for k in L2]
    ci = [sb(f"ci{k}", [P, CH, D]) for k in L2]
    kk = [sb(f"kk{k}", [P, CH, D]) for k in L2]
    nr = [sb(f"nr{k}", [P, T]) for k in L2]
    k2 = [sb(f"k2{k}", [P, CH, D]) for k in L2]
    rk = [sb(f"rk{k}", [P, CH, D]) for k in L2]
    ar = [sb(f"ar{k}", [P, CH, 2, D]) for k in L2]
    be = [sb(f"be{k}", [P, CH, D]) for k in L2]
    ka = [sb(f"ka{k}", [P, CH, D]) for k in L2]
    bk = [sb(f"bk{k}", [P, 2, CH, D]) for k in L2]
    bkt = [sb(f"bkt{k}", [P, 2, CH, D]) for k in L2]
    mb = [sb(f"mb{k}", [P, CH, P]) for k in L2]
    mk = [sb(f"mk{k}", [P, CH, P]) for k in L2]
    lv = [sb(f"lv{k}", [P, 5, CH, D]) for k in L2]
    X = [sb(f"X{k}", [P, CH, D]) for k in L2]
    XT = [sb(f"XT{k}", [P, CH, D]) for k in L2]
    U = [sb(f"U{k}", [P, CH, D]) for k in L2]
    rh = [sb(f"rh{k}", [P, D]) for k in L2]
    us = [sb(f"us{k}", [P, D]) for k in L2]
    S = [sb(f"S{k}", [P, D]) for k in L2]
    o = [sb(f"o{k}", [P, CH, D + 1]) for k in L2]
    osq = [sb(f"osq{k}", [P, CH, D]) for k in L2]
    gn = [sb(f"gn{k}", [P, 6, CH]) for k in L2]
    ot = [sb(f"ot{k}", [D, CH, P]) for k in L2]
    mh = sb("mh", [P, CH])
    bank = lambda k, b: ps[:, 4 * k + b, :]
    third = lambda ap: ap.rearrange("p (c d) -> p c d", c=CH)
    half = lambda b: slice(D * b, D * (b + 1))
    NPREP = 8

    def sync(sp):
        sp.wait_ge(s.prep, 1)
        for n, t in block.items():
            for b in range(2):
                m.n_weights += 1
                sp.dma_start(t[half(b), half(b)], d["rw_" + n]).then_inc(m.weights, 16)
        for dst, n in ((wv, "W_v"), (ag, "A_g")):
            for b in range(2):
                m.n_weights += 1
                sp.dma_start(dst[half(b)], d["rw_" + n]).then_inc(m.weights, 16)
        for dst, n in ((bg, "B_g"), (wo, "W_o"), (tri, "tri"), (maskT, "maskT"), (levT, "levT"), (lev0, "lev0"), (ones, "ones"), (eye, "eye2")):
            m.n_weights += 1
            sp.dma_start(dst[:], d["rw_" + n]).then_inc(m.weights, 16)
        m.n_weights += 2
        sp.dma_start(cols[:, 0:10], d["rw_cols"]).then_inc(m.weights, 16)
        sp.dma_start(rowsb[:], d["rw_rows"].broadcast_to([P, 4 * D])).then_inc(m.weights, 16)

    def zero():
        for i, t in enumerate(block.values()):
            ins = nc.vector.memset(t[:], 0.0)
        ins.then_inc(s.prep, 1)

    def prep():
        for k in L2:
            nc.vector.memset(xn[k][:, :, D:D + 1], 1.0)
            nc.vector.memset(o[k][:, :, D:D + 1], 1.0)
            nc.vector.memset(xf[k][:, 0:1], 0.0)
        nc.vector.memset(mh[:], -0.5).then_inc(s.prep, 5)
        nc.vector.memset(m.junk[:], 0.0).then_inc(s.free, 2)
        nc.vector.wait_ge(m.weights, 16 * m.n_weights)
        nc.vector.tensor_scalar(cols[:, 10:11], cols[:, 7:8], -1.0, 1.0, ALU.mult, ALU.add).then_inc(s.prep, 1)
        nc.vector.tensor_scalar(cols[:, 11:12], cols[:, 9:10], 0.5, None, ALU.mult).then_inc(s.prep, 1)

    def normalise(dve, n, k):
        dve.wait_ge(s.free, n + 1)
        dve.wait_ge(m.ln.rstd, TURNS * (nth - 1) + 1 + m.turn)
        nc.vector.tensor_tensor(xn[k][:, :, 0:D], pair(m.XC, n).rearrange("p (c d) -> p c d", d=D),
                                bcast(pair(m.rstd, n, NC), D), ALU.mult).then_inc(s.xn, 1)

    def turn_x(pe, n, k):
        if k == 0:
            pe.wait_ge(s.xn, n + 1)
            pe.transpose(bank(k, 3)[:, 0:P], ident[:], ident[:])
        wait_apart(pe, m, (s.xn, n + 1))
        for b in range(2):
            for c in range(CH):
                mm = pe.matmul(bank(k, 0)[half(b), D * c:D * (c + 1)], xn[k][half(b), c, 0:D], eye[half(b)], start=True, stop=True)
        mm.then_inc(s.turned, 1)

    def copy_xf(dve, n, k):
        dve.wait_ge(s.turned, n + 1)
        nc.vector.tensor_copy(xf[k][:, 1:], bank(k, 0)[:, 0:T]).then_inc(s.xf, 1)

    def mix(dve, n, k):
        dve.wait_ge(s.xf, n + 1)
        nc.vector.tensor_tensor(dl[k][:], xf[k][:, 0:T], xf[k][:, 1:], ALU.subtract).then_inc(s.mixed, 1)
        dve.wait_ge(s.mixed, 2 * n + 1)
        for i in range(6):
            ins = nc.vector.scalar_tensor_tensor(xm[k][:, i, :], dl[k][:], cols[:, i:i + 1], xf[k][:, 1:], ALU.mult, ALU.add)
        ins.then_inc(s.mixed, 1)

    def project(pe, n, k):
        pe.wait_ge(s.mixed, 2 * n + 2)
        for b, j, w, i in ((0, 0, "W_r", 0), (0, 1, "W_k", 2), (1, 0, "A_w", 1), (1, 1, "A_a", 4)):
            pe.matmul(bank(k, b)[:, T * j:T * (j + 1)], block[w][:], xm[k][:, i, :], start=True, stop=True)
        for b in range(2):
            for c in range(CH):
                pe.matmul(bank(k, 2)[half(b), D * c:D * (c + 1)], xm[k][half(b), 3, D * c:D * (c + 1)], wv[half(b)], start=True, stop=True)
        pe.matmul(bank(k, 2)[:, T:2 * T], ag[half(0)], xm[k][half(0), 5, :], start=True, stop=True)
        pe.matmul(bank(k, 3)[:, 0:T], ag[half(1)], xm[k][half(1), 5, :], start=True, stop=True).then_inc(s.proj, 1)

    def copy_proj_act(act, n, k):
        act.wait_ge(s.proj, n + 1)
        nc.scalar.activation(za[k][:, 0, :], bank(k, 1)[:, 0:T], ACT.Tanh)
        nc.scalar.activation(za[k][:, 1, :], bank(k, 1)[:, T:2 * T], ACT.Copy)
        nc.scalar.activation(gh[k][:, 0, :], bank(k, 2)[:, T:2 * T], ACT.Tanh, scale=0.5)
        nc.scalar.activation(gh[k][:, 1, :], bank(k, 3)[:, 0:T], ACT.Tanh, scale=0.5)
        nc.scalar.activation(V[k][:].rearrange("p c d -> p (c d)"), bank(k, 2)[:, 0:T], ACT.Copy).then_inc(s.projc, 1)

    def copy_proj_dve(dve, n, k):
        dve.wait_ge(s.proj, n + 1)
        nc.vector.tensor_copy(K[k][:], third(bank(k, 0)[:, T:2 * T]))
        nc.vector.tensor_copy(R[k][:], third(bank(k, 0)[:, 0:T])).then_inc(s.projd, 1)
        dve.wait_ge(s.projd, 3 * n + 1)
        nc.vector.tensor_scalar(kk[k][:], K[k][:], cols[:, 6:7], None, ALU.mult).then_inc(s.projd, 1)
        dve.wait_ge(s.projd, 3 * n + 2)
        nc.vector.tensor_tensor(nr[k][:], kk[k][:].rearrange("p c d -> p (c d)"), kk[k][:].rearrange("p c d -> p (c d)"), ALU.mult).then_inc(s.projd, 1)

    def second(pe, n, k):
        pe.wait_ge(s.projc, n + 1)
        pe.wait_ge(s.projd, 3 * n + 3)
        pe.matmul(bank(k, 0)[:, 0:T], block["B_a"][:], za[k][:, 1, :], start=True, stop=True)
        pe.matmul(bank(k, 2)[:, 0:T], ones[:], nr[k][:], start=True, stop=True)
        for c in range(CH):
            mm = pe.matmul(bank(k, 1)[0:D, P * c:P * (c + 1)], za[k][:, 0, D * c:D * (c + 1)], block["B_w"][:], start=True, stop=True)
        mm.then_inc(s.second, 1)

    def rates(dve, n, k):
        dve.wait_ge(s.second, n + 1)
        nc.vector.tensor_tensor(wt[k][:], bank(k, 1)[0:D, 0:CH * P].rearrange("p (c e) -> p c e", c=CH),
                                rowsb[0:D, 0:P].unsqueeze(1).broadcast_to([D, CH, P]), ALU.add).then_inc(wtok[k], 1)
        nc.vector.tensor_scalar(nr[k][:], bank(k, 2)[:, 0:T], 1e-24, None, ALU.max).then_inc(wtok[k], 1)

    def sigmoids(act, n, k):
        act.wait_ge(s.second, n + 1)
        nc.scalar.activation(a[k][:].rearrange("p c d -> p (c d)"), bank(k, 0)[:, 0:T], ACT.Tanh, bias=cols[:, 11:12], scale=0.5).then_inc(s.sq, 1)
        act.wait_ge(wtok[k], 4 * m.turn + 1)
        nc.scalar.activation(wt[k][:], wt[k][:], ACT.Tanh, scale=0.5).then_inc(s.sq, 1)

    def root(act, n, k):
        act.wait_ge(wtok[k], 4 * m.turn + 2)
        nc.scalar.activation(nr[k][:], nr[k][:], ACT.Sqrt).then_inc(s.norms, 1)

    def finish_rates(dve, n, k):
        dve.wait_ge(s.sq, 2 * n + 2)
        nc.vector.tensor_scalar(wt[k][:], wt[k][:], DECAY / 2, DECAY / 2, ALU.mult, ALU.add).then_inc(wtok[k], 1)
        nc.vector.tensor_scalar(a[k][:], a[k][:], 0.5, 0.5, ALU.mult, ALU.add)
        nc.vector.tensor_scalar(gh[k][:], gh[k][:], 0.5, 0.5, ALU.mult, ALU.add).then_inc(wtok[k], 1)

    def cumulate(pe, n, k):
        pe.wait_ge(wtok[k], 4 * m.turn + 3)
        for c in range(CH):
            mm = pe.matmul(bank(k, 3)[:, P * c:P * (c + 1)], wt[k][:, c, :], tri[:], start=True, stop=True)
        mm.then_inc(s.cum, 1)

    def decays(act, n, k):
        act.wait_ge(s.cum, n + 1)
        src = bank(k, 3)[:, 0:CH * P]
        nc.scalar.activation(ce[k][:].rearrange("p c j t -> p (c j t)"), src, ACT.Exp)
        nc.scalar.activation(ci[k][:], src.rearrange("p (c e) -> p c e", c=CH)[:, :, 0:D], ACT.Exp, scale=-1.0).then_inc(s.decays, 1)

    def keys(dve, n, k):
        link = Link(dve, s.keys, 5 * n)
        v = nc.vector
        dve.wait_ge(s.norms, n + 1)
        dve.wait_ge(wtok[k], 4 * m.turn + 4)
        link(v.reciprocal(nr[k][:], nr[k][:]))
        v.tensor_tensor(kk[k][:], kk[k][:], third(nr[k][:]), ALU.mult)
        link(v.tensor_scalar(k2[k][:], a[k][:], cols[:, 7:8], cols[:, 10:11], ALU.mult, ALU.add))
        v.tensor_tensor(a[k][:], kk[k][:], a[k][:], ALU.mult)
        link(v.tensor_tensor(k2[k][:], K[k][:], k2[k][:], ALU.mult))
        dve.wait_ge(s.decays, n + 1)
        v.tensor_tensor(ar[k][:, :, 0, :], kk[k][:], ce[k][:, :, 1, :], ALU.mult)
        v.tensor_tensor(ar[k][:, :, 1, :], R[k][:], ce[k][:, :, 0, :], ALU.mult)
        v.tensor_tensor(be[k][:], a[k][:], ci[k][:], ALU.mult)
        link(v.tensor_tensor(ka[k][:], k2[k][:], ci[k][:], ALU.mult))
        v.scalar_tensor_tensor(rk[k][:], R[k][:], cols[:, 8:9], k2[k][:], ALU.mult, ALU.mult)
        for j, t in enumerate((be, ka)):
            ins = v.tensor_tensor(bk[k][:, j], t[k][:], bcast(ce[k][:, :, 0, D - 1], D), ALU.mult)
        link(ins)

    def matrices(pe, n, k):
        wait_apart(pe, m, (s.keys, 5 * n + 4))
        for b in range(2):
            h = half(b)
            for c in range(CH):
                both = ar[k][h, c].rearrange("p j t -> p (j t)")
                pe.matmul(bank(k, 0)[h, P * c:P * (c + 1)], be[k][h, c], both, start=True, stop=True)
                pe.matmul(bank(k, 1)[h, P * c:P * (c + 1)], ka[k][h, c], both, start=True, stop=True)
                mm = pe.matmul(bank(k, 2)[h, D * c:D * (c + 1)], ar[k][h, c, 0], be[k][h, c], start=True, stop=True)
        mm.then_inc(s.mats, 1)
        wait_apart(pe, m, (s.keys, 5 * n + 5))
        for b in range(2):
            h = half(b)
            for j in range(2):
                for c in range(CH):
                    q = D * (CH * j + c)
                    mm = pe.matmul(bank(k, 3)[h, q:q + D], bk[k][h, j, c], eye[h], start=True, stop=True)
        mm.then_inc(s.tokmaj, 1)

    def copy_tokmaj(act, n, k):
        act.wait_ge(s.tokmaj, n + 1)
        nc.scalar.activation(bkt[k][:].rearrange("p j c d -> p (j c d)"), bank(k, 3)[:, 0:2 * T], ACT.Copy).then_inc(s.rkk, 1)

    def mask(dve, n, k):
        link = Link(dve, s.masked, 3 * n)
        v = nc.vector
        mt = maskT[:].unsqueeze(1).broadcast_to([P, CH, P])
        lev = lambda i: lev0[:, D * i:D * (i + 1)].unsqueeze(1).broadcast_to([P, CH, D])
        e3 = eye[:].unsqueeze(1).broadcast_to([P, CH, D])
        dve.wait_ge(s.mats, n + 1)
        v.tensor_tensor(mk[k][:], bank(k, 1)[:, 0:CH * P].rearrange("p (c e) -> p c e", c=CH), mt, ALU.mult)
        v.tensor_tensor(X[k][:], third(bank(k, 2)[:, 0:T]), lev(1), ALU.mult)
        link(v.tensor_tensor(mb[k][:], bank(k, 0)[:, 0:CH * P].rearrange("p (c e) -> p c e", c=CH), mt, ALU.mult))
        v.tensor_tensor(XT[k][:], mb[k][:, :, 0:D], lev(0), ALU.mult)
        v.tensor_tensor(X[k][:], e3, X[k][:], ALU.subtract)
        for j in range(5):
            ins = v.tensor_tensor(lv[k][:, j], mb[k][:, :, 0:D], levT[:, D * j:D * (j + 1)].unsqueeze(1).broadcast_to([P, CH, D]), ALU.mult)
        link(ins)
        v.tensor_tensor(XT[k][:], e3, XT[k][:], ALU.subtract).then_inc(s.masked, 1)

    def level_a(pe, n, k, j):
        if j == 0:
            wait_apart(pe, m, (s.masked, 3 * n + 3))
        else:
            wait_apart(pe, m, (inv_dve[k], 10 * m.turn + 2 * j))
        for b in range(2):
            h = half(b)
            for c in range(CH):
                mm = pe.matmul(bank(k, 2)[h, D * c:D * (c + 1)], lv[k][h, j, c], X[k][h, c], start=True, stop=True)
        mm.then_inc(inv_pe[k], 1)

    def level_a_copy(dve, n, k, j):
        dve.wait_ge(inv_pe[k], 10 * m.turn + 2 * j + 1)
        nc.vector.tensor_copy(U[k][:], third(bank(k, 2)[:, 0:T])).then_inc(inv_dve[k], 1)

    def level_b(pe, n, k, j):
        wait_apart(pe, m, (inv_dve[k], 10 * m.turn + 2 * j + 1))
        for b in range(2):
            h = half(b)
            for c in range(CH):
                if j < 4:
                    pe.matmul(bank(k, 0)[h, D * c:D * (c + 1)], XT[k][h, c], U[k][h, c], start=True, stop=True)
                mm = pe.matmul(bank(k, 1)[h, D * c:D * (c + 1)], U[k][h, c], XT[k][h, c], start=True, stop=True)
        mm.then_inc(inv_pe[k], 1)

    def level_b_sub(dve, n, k, j):
        dve.wait_ge(inv_pe[k], 10 * m.turn + 2 * j + 2)
        if j < 4:
            nc.vector.tensor_tensor(X[k][:], X[k][:], third(bank(k, 0)[:, 0:T]), ALU.subtract)
        nc.vector.tensor_tensor(XT[k][:], XT[k][:], third(bank(k, 1)[:, 0:T]), ALU.subtract).then_inc(inv_dve[k], 1)

    def right_side(pe, n, k, c):
        if c == 0:
            wait_apart(pe, m, (inv_dve[k], 10 * m.turn + 10), (s.rkk, n + 1))
        else:
            wait_apart(pe, m, (chunk_dve[k], at(c - 1, 2)))
        for b in range(2):
            h = half(b)
            if c:
                mm = pe.matmul(bank(k, 0)[h, 0:D], ar[k][h, c, 0], S[k][h], start=False, stop=True, skip_group_check=True)
            else:
                mm = pe.matmul(bank(k, 0)[h, 0:D], mk[k][h, c, 0:D], V[k][h, c], start=True, stop=True, skip_group_check=True)
        mm.then_inc(chunk_pe[k], 1)

    def at(c, i):
        return 3 * CH * m.turn + 3 * c + i + 1

    def copy_right(dve, n, k, c):
        dve.wait_ge(chunk_pe[k], at(c, 0))
        nc.vector.tensor_scalar(rh[k][:], bank(k, 0)[:, 0:D], -1.0, None, ALU.mult).then_inc(chunk_dve[k], 1)

    def solve(pe, n, k, c):
        wait_apart(pe, m, (chunk_dve[k], at(c, 0)))
        for b in range(2):
            h = half(b)
            mm = pe.matmul(bank(k, 1)[h, 0:D], XT[k][h, c], rh[k][h], start=True, stop=True)
        mm.then_inc(chunk_pe[k], 1)
        q = slice(D * c, D * (c + 1))
        for b in range(2):
            h = half(b)
            if c + 1 < CH:
                pe.matmul(bank(k, 2)[h, 0:D], bkt[k][h, 1, c], V[k][h, c], start=True, stop=False, skip_group_check=True)
            pe.matmul(bank(k, 3)[h, q], mk[k][h, c, D:P], V[k][h, c], start=True, stop=False, skip_group_check=True)
            if c:
                pe.matmul(bank(k, 3)[h, q], ar[k][h, c, 1], S[k][h], start=False, stop=False, skip_group_check=True)

    def copy_u(dve, n, k, c):
        dve.wait_ge(chunk_pe[k], at(c, 1))
        nc.vector.tensor_copy(us[k][:], bank(k, 1)[:, 0:D]).then_inc(chunk_dve[k], 1)

    def advance(pe, n, k, c):
        wait_apart(pe, m, (chunk_dve[k], at(c, 1)))
        if c + 1 < CH:
            for b in range(2):
                pe.matmul(bank(k, 2)[half(b), 0:D], bkt[k][half(b), 0, c], us[k][half(b)], start=False, stop=True, skip_group_check=True)
        for b in range(2):
            mm = pe.matmul(bank(k, 3)[half(b), D * c:D * (c + 1)], mb[k][half(b), c, D:P], us[k][half(b)],
                           start=False, stop=True, skip_group_check=True)
        mm.then_inc(chunk_pe[k], 1)
        if c + 1 < CH:
            for b in range(2):
                pe.matmul(bank(k, 0)[half(b), 0:D], mk[k][half(b), c + 1, 0:D], V[k][half(b), c + 1], start=True, stop=False, skip_group_check=True)

    def keep_state(dve, n, k, c):
        dve.wait_ge(chunk_pe[k], at(c, 2))
        if c == 0:
            nc.vector.tensor_copy(S[k][:], bank(k, 2)[:, 0:D]).then_inc(chunk_dve[k], 1)
        elif c + 1 < CH:
            nc.vector.scalar_tensor_tensor(S[k][:], S[k][:], ce[k][:, c, 0, D - 1:D], bank(k, 2)[:, 0:D], ALU.mult, ALU.add).then_inc(chunk_dve[k], 1)
        else:
            nc.vector.tensor_reduce(gn[k][:, 0, :], third(bank(k, 3)[:, 0:T]), AX.X, ALU.add).then_inc(chunk_dve[k], 1)

    def bonus(pe, n, k):
        wait_apart(pe, m, (chunk_pe[k], at(2, 2)))
        for b in range(2):
            for c in range(CH):
                pe.matmul(bank(k, 0)[half(b), c:c + 1], rk[k][half(b), c], ones[half(b), D * b:D * b + 1], start=True, stop=True)
        for b in range(2):
            for c in range(CH):
                mm = pe.matmul(bank(k, 1)[half(b), D * c:D * (c + 1)], gh[k][:, b, D * c:D * (c + 1)], bg[:], start=True, stop=True)
        mm.then_inc(s.out, 1)

    def group_norm(dve, n, k):
        v = nc.vector
        link = Link(dve, s.on, 8 * n)
        o3 = o[k][:, :, 0:D]
        dve.wait_ge(chunk_dve[k], at(2, 2))
        link(v.tensor_scalar(gn[k][:, 1, :], gn[k][:, 0, :], 1.0 / D, None, ALU.mult))
        link(v.tensor_tensor(o3, third(bank(k, 3)[:, 0:T]), bcast(gn[k][:, 1, :], D), ALU.subtract))
        dve.wait_ge(s.sq2, n + 1)
        link(v.tensor_reduce(gn[k][:, 2, :], osq[k][:], AX.X, ALU.add))
        link(v.tensor_scalar(gn[k][:, 3, :], gn[k][:, 2, :], 1.0 / D, GN_EPS, ALU.mult, ALU.add))
        dve.wait_ge(s.gr, n + 1)
        link(v.tensor_tensor(o3, o3, bcast(gn[k][:, 4, :], D), ALU.mult))
        link(v.tensor_tensor(o3, o3, rowsb[:, 2 * D:3 * D].unsqueeze(1).broadcast_to([P, CH, D]), ALU.mult))
        dve.wait_ge(s.out, n + 1)
        v.tensor_copy(gn[k][:, 5, :], bank(k, 0)[:, 0:CH])
        link(v.tensor_tensor(o3, o3, rowsb[:, 3 * D:4 * D].unsqueeze(1).broadcast_to([P, CH, D]), ALU.add))
        link(v.tensor_tensor(V[k][:], V[k][:], bcast(gn[k][:, 5, :], D), ALU.mult))
        v.tensor_tensor(o3, o3, V[k][:], ALU.add).then_inc(s.gated, 1)
        dve.wait_ge(s.gated, 2 * n + 1)
        v.tensor_tensor(o3, o3, third(bank(k, 1)[:, 0:T]), ALU.mult).then_inc(s.gated, 1)

    def square(act, n, k):
        act.wait_ge(s.on, 8 * n + 2)
        nc.scalar.activation(osq[k][:], o[k][:, :, 0:D], ACT.Square).then_inc(s.sq2, 1)

    def group_root(pool, n, k):
        pool.wait_ge(s.on, 8 * n + 4)
        nc.gpsimd.tensor_tensor(gn[k][:, 4, :], gn[k][:, 3, :], mh[:], ALU.pow).then_inc(s.gr, 1)

    def turn_out(pe, n, k):
        pe.wait_ge(s.gated, 2 * n + 2)
        for c in range(CH):
            mm = pe.transpose(bank(k, 2)[0:D + 1, P * c:P * (c + 1)], o[k][:, c, :], ident[:])
        mm.then_inc(s.turnedo, 1)

    def copy_ot(act, n, k):
        act.wait_ge(s.turnedo, n + 1)
        nc.scalar.activation(ot[k][:].rearrange("p c n -> p (c n)"), bank(k, 2)[0:D, 0:CH * P], ACT.Copy).then_inc(s.ot, 1)

    def project_out(pe, n, k):
        wait_apart(pe, m, (s.ot, n + 1))
        for c in range(CH):
            mm = pe.matmul(bank(k, 3)[:, D * c:D * (c + 1)], ot[k][:, c, :], wo[:], start=True, stop=True)
        mm.then_inc(s.y, 1)

    def add_out(dve, n, k):
        dve.wait_ge(s.y, n + 1)
        nc.vector.tensor_tensor(pair(H, n), pair(H, n), bank(k, 3)[:, 0:T], ALU.add).then_inc(s.free, 1)

    def with_index(f, j):
        return lambda eng, n, k: f(eng, n, k, j)

    inv = lambda fa, fb: [with_index(f, j) for j in range(5) for f in (fa, fb)]
    chunks = lambda *fs: [with_index(f, c) for c in range(CH) for f in fs]
    r = lambda steps, before=lambda: None, values=None: rolled(m, s, nth, NPREP, steps, before, values)

    def pe_values(it):
        return [2 * it + 1, 2 * it + 2, 5 * (2 * it) + 5, 5 * (2 * it + 1) + 5, 3 * (2 * it) + 3, 3 * (2 * it + 1) + 3,
                5 * (2 * it) + 4, 5 * (2 * it + 1) + 4] \
            + [10 * it + i for i in range(1, 11)] + [9 * it + i for i in range(1, 10)]

    return dict(sync=sync, zero=zero,
                tensor=r([turn_x, project, second, cumulate, matrices] + inv(level_a, level_b) + chunks(right_side, solve, advance)
                         + [bonus, turn_out, project_out], values=pe_values),
                scalar=r([copy_proj_act, sigmoids, root, decays, copy_tokmaj, square, copy_ot]),
                vector=r([normalise, copy_xf, mix, copy_proj_dve, rates, finish_rates, keys, mask] + inv(level_a_copy, level_b_sub)
                         + chunks(copy_right, copy_u, keep_state) + [group_norm, add_out], prep),
                gpsimd=r([group_root], lambda: nc.gpsimd.wait_ge(m.ln.rstd, TURNS * nth)))


def early_fusion(nc, x, txt, d, out):
    with ExitStack() as ctx:
        stage_done = ctx.enter_context(nc.semaphore("stage_done"))
        operator_done = ctx.enter_context(nc.semaphore("operator_done"))
        s_tokens = ctx.enter_context(nc.semaphore("tokens_loaded"))
        s_out = ctx.enter_context(nc.semaphore("out_written"))
        ps = ctx.enter_context(nc.psum_tensor("ps", [P, 8, 512], F32))
        y_img = nc.dram_tensor("image_tokens", [B, XY], F32, kind="Internal").ap()

        def operator_barrier(eng, k):
            eng.drain().then_inc(operator_done, 1)
            eng.wait_ge(operator_done, 4 * k)

        def barrier(eng, k):
            eng.drain().then_inc(stage_done, 1)
            eng.wait_ge(stage_done, 5 * (k - step))

        fno_ctx, fno, step, fno_signals = fourier_operator(nc, operator_barrier, ps, x, y_img, d, 0)
        fno_ctx.close()

        m = common(nc, ctx)
        m.ps = ps
        m.ident = ctx.enter_context(nc.sbuf_tensor("tok_ident", [P, P], F32))
        norm = [layer_norm(nc, m, 0), layer_norm(nc, m, 1), layer_norm(nc, m, 2), layer_norm(nc, m, 3),
                layer_norm(nc, m, 4, src=m.SQ)]
        twice = second_norm(nc, m, 4)
        blocks = []
        for make, nth in ((attention, 1), (slices, 2), (recurrence, 3), (experts, 5)):
            work = ExitStack()
            blocks.append(make(nc, ctx, work, m, d, nth))
            work.close()
        att, sli, rec, moe = blocks
        halves = [slice(D * b, D * (b + 1)) for b in range(2)]
        h4 = m.H[:].rearrange("p (q c d) -> p q c d", q=NP, c=NC)

        def load(sp):
            sp.dma_start(m.ident[:], d["ident"]).then_inc(s_tokens, 16)
            for b, r in enumerate(halves):
                sp.dma_start(h4[r, :, 0, :], y_img.rearrange("(q b) (x y) -> b x q y", b=2, x=S)[b]).then_inc(s_tokens, 16)
                for c in range(1, NC):
                    src = txt.rearrange("(q b) (c t) d -> b c t q d", b=2, c=NC - 1)[b, c - 1]
                    sp.dma_start(h4[r, :, c, :], src).then_inc(s_tokens, 16)
            sp.wait_ge(s_tokens, 16 * (1 + 2 * NC))

        def store(sp):
            dst = out.rearrange("(q b) (c t) d -> b c t q d", b=2, c=NC)
            for b, r in enumerate(halves):
                for c in range(NC):
                    sp.dma_start(dst[b, c], h4[r, :, c, :]).then_inc(s_out, 16)
            sp.wait_ge(s_out, 16 * 2 * NC)

        def program(name):
            def run(eng):
                def do(part):
                    if name in part and name != "sync":
                        part[name](eng)
                if name in fno:
                    fno[name](eng)
                barrier(eng, step + 1)
                if name == "sync":
                    for sem in fno_signals:
                        eng.sem_clear(sem)
                barrier(eng, step + 2)
                if name == "sync":
                    load(eng)
                if name == "vector":
                    att["zero"]()
                    sli["zero"]()
                    rec["zero"]()
                    moe["zero"]()
                if name == "gpsimd":
                    nc.gpsimd.memset(m.mhalf[:], -0.5).then_inc(m.ln.mhalf, 1)
                barrier(eng, step + 3)
                if name == "sync":
                    for block in blocks:
                        block["sync"](eng)
                for n, block in enumerate((att, sli, rec)):
                    do(norm[n])
                    do(block)
                    barrier(eng, step + 4 + n)
                do(norm[3])
                do(twice)
                barrier(eng, step + 7)
                do(norm[4])
                do(moe)
                barrier(eng, step + 8)
                if name == "sync":
                    store(eng)
            return run

        block = ctx.enter_context(nc.Block())
        block.sync(program("sync"))
        block.tensor(program("tensor"))
        block.scalar(program("scalar"))
        block.vector(program("vector"))
        block.gpsimd(program("gpsimd"))



def token_arrays(i):
    cat=np.concatenate
    r=lambda a: a.reshape(1,-1)
    a={}
    a["ident"]=np.eye(128,dtype=np.float32)
    g=lambda n: np.asarray(i["L0_attn_"+n])
    a["att_wqk"]=cat([cat([g("Wq").T,g("Wk").T],1),cat([r(g("bq")),r(g("bk"))],1)],0)
    a["att_wv"]=cat([cat([g("Wv").T,g("Wq").T[:,:1],g("Wk").T[:,:1]],1),cat([r(g("bv")),r(g("bq")[:1]),r(g("bk")[:1])],1)],0)
    a["att_wo"]=cat([g("Wo").T,r(g("bo"))],0)
    g=lambda n: np.asarray(i["L0_ffn_"+n])
    wx=cat([g("W_x"),r(g("b_x"))],0).reshape(65,8,64)
    a["ffn_wx"]=wx.transpose(2,1,0).reshape(64,8*65)
    a["ffn_ws"]=g("W_slice")
    a["ffn_rows"]=cat([np.tile(g("b_slice"),8)[None],np.repeat(g("temperature").reshape(-1),64)[None]],1)
    a["ffn_wfx"]=cat([g("W_fx"),r(g("b_fx"))],0)
    a["ffn_wqT"]=g("W_q").T; a["ffn_wkT"]=g("W_k").T; a["ffn_wvT"]=g("W_v").T
    a["ffn_wout"]=g("W_out").reshape(8,64,64).transpose(1,0,2).reshape(64,512)
    a["ffn_bout"]=r(g("b_out"))
    g=lambda n: np.asarray(i["L1_ffn_"+n])
    a["moe_gb"]=np.stack([g("gamma"),g("beta")],1)
    a["moe_wr"]=cat([g("Wr"),r(g("br"))],0)
    a["moe_w1"]=cat([g("W1").transpose(1,0,2).reshape(64,1024),g("b1").reshape(1,1024)],0)
    a["moe_w2"]=g("W2").transpose(1,0,2).reshape(128,512)
    a["moe_b2"]=g("b2")
    a["iota8"]=np.arange(8,dtype=np.float32)[None]
    g=lambda n: np.asarray(i["L1_attn_"+n])
    for n in ("W_r","W_k","A_w","A_a","B_w","B_a","W_v","A_g","B_g","W_o"): a["rw_"+n]=g(n)
    c=lambda v: v.reshape(64,-1)
    a["rw_cols"]=np.tile(cat([c(g("x_mix").T),c(g("k_k")),c(g("k_a")),c(g("r_k")),c(g("b_a"))],1),(2,1))
    a["rw_rows"]=cat([np.tile(g("b_w"),2),g("gn_w"),g("gn_b")])[None]
    t=np.arange(64)
    tri=(t[:,None]<=t[None]).astype(np.float32); strict=(t[:,None]<t[None]).astype(np.float32)
    a["rw_tri"]=cat([tri,strict],1)
    a["rw_maskT"]=np.tile(cat([strict,tri],1),(2,1))
    lv=[]
    for j in range(6):
        bs=1<<j
        mt=((t[:,None]//(2*bs)==t[None]//(2*bs))&(t[:,None]//bs%2==0)&(t[None]//bs%2==1)).astype(np.float32)
        lv.append(mt)
    a["rw_levT"]=np.tile(np.stack(lv[1:],1).reshape(64,320),(2,1))
    a["rw_lev0"]=np.tile(np.concatenate([lv[0],lv[0].T],1),(2,1))
    a["rw_ones"]=np.kron(np.eye(2),np.ones((64,64))).astype(np.float32)
    a["rw_eye2"]=np.tile(np.eye(64),(2,1)).astype(np.float32)
    return a


def operator_arrays(i):
    g = lambda n: np.asarray(i["L0_tok_" + n])
    a = fourier_constants()
    a["avg4"] = np.kron(np.ones((QB, QB)), np.eye(C)).astype(np.float32) / np.float32(QB)
    line = np.linspace(0.0, 1.0, S, dtype=np.float32)
    a["grid"] = np.stack([np.repeat(line, S), np.tile(line, S), np.ones(XY, np.float32)])
    a["zero"] = np.zeros((C - QB - 3, XY), np.float32)
    a["q_w"] = g("q_w")
    for n, images in (("lift", QB), ("lifts", B)):
        a[n] = np.zeros((P, images * C), np.float32)
        for b in range(images):
            c = slice(C * b, C * (b + 1))
            a[n][b, c] = g("p_w")[0]
            a[n][images:images + 2, c] = g("p_w")[1:3]
            a[n][images + 2, c] = g("p_b")
    a["w_blocks"] = np.zeros((L, P, P), np.float32)
    for b in range(QB):
        a["w_blocks"][:, C * b:C * (b + 1), C * b:C * (b + 1)] = g("w_w")
    for n in ("w_b", "bn_g", "bn_b"):
        a[n] = g(n).T
    fw = np.stack([g("fw1"), g("fw2")])
    a["modes"] = fw.transpose(1, 0, 6, 2, 5, 4, 3).reshape(L, P, -1)
    a["q_b4"] = np.tile(g("q_b").reshape(1, 1), (QB, 1))
    return a


def kernel(**inputs):
    import concourse.bacc as _bacc
    from concourse.bass_utils import run_bass_kernel_spmd as _run

    nc = _bacc.Bacc("TRN2", target_bir_lowering=False, num_devices=1)
    arrays, d = {}, {}
    laid = {**operator_arrays(inputs), **token_arrays(inputs),
            "x": np.asarray(inputs["x"]).reshape(B, XY), "txt": np.asarray(inputs["txt"])}
    for name, a in laid.items():
        a = np.ascontiguousarray(a)
        arrays[f"in_{name}"] = a
        d[name] = nc.dram_tensor(f"in_{name}", a.shape, F32, kind="ExternalInput").ap()
    out = nc.dram_tensor("out_0", (B, T, D), F32, kind="ExternalOutput").ap()
    early_fusion(nc, d["x"], d["txt"], d, out)
    r = _run(nc, [arrays], core_ids=[0])
    return r.results[0]["out_0"]
```
